# Optimizing a Trainium2 kernel written in Bass

```python
import numpy as np
import jax
import jax.numpy as jnp

def _softmax(x, axis=-1):
    return jax.nn.softmax(x, axis=axis)

def _gelu(x):
    return jax.nn.gelu(x, approximate=True)

def _silu(x):
    return jax.nn.silu(x)

def _sigmoid(x):
    return jax.nn.sigmoid(x)

def _layernorm(x, axis=-1, eps=1e-05):
    m = jnp.mean(x, axis=axis, keepdims=True)
    v = jnp.var(x, axis=axis, keepdims=True)
    return (x - m) / jnp.sqrt(v + eps)

def _scatter_add(tgt, idx, src, axis=0):
    return tgt.at[idx].add(src)

def _segment_sum(src, seg, n):
    return jax.ops.segment_sum(src, seg, n)
kernel_name = 'mk_gnn_resnorm_d2_gnn_r32_baa2d3'

def setup_inputs(seed: int=0):
    np.random.seed(seed)
    _w = jnp.asarray

    def _rec_inputs():
        import jax
        import jax.numpy as jnp
        _gk = jax.random.key(seed)
        x = -0.000202 + 1 * jax.random.normal(jax.random.fold_in(_gk, 1), (3125, 128), jnp.float32)
        src = jax.random.randint(jax.random.fold_in(_gk, 2), (100000,), 0, 3125, jnp.int32)
        dst = jax.random.randint(jax.random.fold_in(_gk, 3), (100000,), 0, 3125, jnp.int32)
        _o = jnp.argsort(dst, stable=True)
        src = src[_o]
        dst = dst[_o]
        edge_attr_16 = 0.000254156 + 0.999948 * jax.random.normal(jax.random.fold_in(_gk, 12), (100000, 16), jnp.float32)
        edge_attr_16_n2 = 0.000254156 + 0.999948 * jax.random.normal(jax.random.fold_in(_gk, 13), (100000, 16), jnp.float32)
        return (x, src, dst, edge_attr_16, edge_attr_16_n2)
    x, src, dst, edge_attr_16, edge_attr_16_n2 = _rec_inputs()

    def _L0_gnn_setup():
        import jax, jax.numpy as jnp
        import numpy as np
        N = 50000
        E = 25000
        D_IN = 128
        SH = 16
        EA = 16
        H = 8
        DQ = 64
        DK = 64
        DV = 128
        HID = 64

        def _conv_per_edge(x_src, edge_attr, edge_sh, Wang, Wlin, W1, b1, W2):
            rad = jax.nn.relu(edge_attr @ W1 + b1) @ W2
            g = edge_sh @ Wang.T
            return x_src * g @ Wlin * rad
        key = jax.random.key(seed)
        ks = jax.random.split(key, 20)
        g = lambda k, shape, fan: jax.random.normal(k, shape, jnp.float32) / np.sqrt(fan)
        return {'node_attr': jax.random.normal(ks[0], (N, D_IN), jnp.float32), 'edge_attr': jax.random.normal(ks[1], (E, EA), jnp.float32), 'edge_sh': jax.random.normal(ks[2], (E, SH), jnp.float32), 'Wq': g(ks[3], (D_IN, DQ), D_IN), 'Wang_k': g(ks[4], (D_IN, SH), SH), 'Wlin_k': g(ks[5], (D_IN, DK), D_IN), 'W1k': g(ks[6], (EA, HID), EA), 'b1k': jnp.zeros((HID,), jnp.float32), 'W2k': g(ks[7], (HID, DK), HID), 'Wang_v': g(ks[8], (D_IN, SH), SH), 'Wlin_v': g(ks[9], (D_IN, DV), D_IN), 'W1v': g(ks[10], (EA, HID), EA), 'b1v': jnp.zeros((HID,), jnp.float32), 'W2v': g(ks[11], (HID, DV), HID), 'Wdot': g(ks[12], (DQ // H, DK // H), DQ // H), 'Wout': g(ks[13], (DV, DV), DV), 'edge_index': jax.random.randint(ks[14], (2, E), 0, N, jnp.int64)}
    _L0_gnn_all = _L0_gnn_setup()
    _L0_gnn_in = {k: v for k, v in _L0_gnn_all.items() if k in ('Wq', 'Wang_k', 'Wlin_k', 'W1k', 'b1k', 'W2k', 'Wang_v', 'Wlin_v', 'W1v', 'b1v', 'W2v', 'Wdot', 'Wout')}
    del _L0_gnn_all

    def _L1_gnn_setup():
        import jax, jax.numpy as jnp
        import numpy as np
        N_NODES = 3125
        N_EDGES = 50000
        D = 128
        L = 3
        BN_EPS = 1e-05
        key = jax.random.key(seed)
        ks = jax.random.split(key, 8)
        x = jax.random.normal(ks[0], (N_NODES, D), dtype=jnp.float32)
        edge_src = jax.random.randint(ks[1], (N_EDGES,), 0, N_NODES, dtype=jnp.int32)
        edge_dst = jax.random.randint(ks[2], (N_EDGES,), 0, N_NODES, dtype=jnp.int32)
        scale = 1.0 / np.sqrt(D)
        W1 = jax.random.normal(ks[3], (L, D, D), dtype=jnp.float32) * scale
        b1 = jnp.zeros((L, D), dtype=jnp.float32)
        W2 = jax.random.normal(ks[4], (L, D, D), dtype=jnp.float32) * scale
        b2 = jnp.zeros((L, D), dtype=jnp.float32)
        gamma = jnp.ones((L, D), dtype=jnp.float32)
        beta = jnp.zeros((L, D), dtype=jnp.float32)
        return {'x': x, 'edge_src': edge_src, 'edge_dst': edge_dst, 'W1': W1, 'b1': b1, 'W2': W2, 'b2': b2, 'gamma': gamma, 'beta': beta}
    _L1_gnn_all = _L1_gnn_setup()
    _L1_gnn_in = {k: v for k, v in _L1_gnn_all.items() if k in ('W1', 'b1', 'W2', 'b2', 'gamma', 'beta')}
    del _L1_gnn_all
    return {'x': x, 'src': src, 'dst': dst, 'edge_attr_16': edge_attr_16, 'edge_attr_16_n2': edge_attr_16_n2, 'L0_gnn_Wq': _L0_gnn_in['Wq'], 'L0_gnn_Wang_k': _L0_gnn_in['Wang_k'], 'L0_gnn_Wlin_k': _L0_gnn_in['Wlin_k'], 'L0_gnn_W1k': _L0_gnn_in['W1k'], 'L0_gnn_b1k': _L0_gnn_in['b1k'], 'L0_gnn_W2k': _L0_gnn_in['W2k'], 'L0_gnn_Wang_v': _L0_gnn_in['Wang_v'], 'L0_gnn_Wlin_v': _L0_gnn_in['Wlin_v'], 'L0_gnn_W1v': _L0_gnn_in['W1v'], 'L0_gnn_b1v': _L0_gnn_in['b1v'], 'L0_gnn_W2v': _L0_gnn_in['W2v'], 'L0_gnn_Wdot': _L0_gnn_in['Wdot'], 'L0_gnn_Wout': _L0_gnn_in['Wout'], 'L1_gnn_W1': _L1_gnn_in['W1'], 'L1_gnn_b1': _L1_gnn_in['b1'], 'L1_gnn_W2': _L1_gnn_in['W2'], 'L1_gnn_b2': _L1_gnn_in['b2'], 'L1_gnn_gamma': _L1_gnn_in['gamma'], 'L1_gnn_beta': _L1_gnn_in['beta']}

def reference(x, src, dst, edge_attr_16, edge_attr_16_n2, L0_gnn_Wq, L0_gnn_Wang_k, L0_gnn_Wlin_k, L0_gnn_W1k, L0_gnn_b1k, L0_gnn_W2k, L0_gnn_Wang_v, L0_gnn_Wlin_v, L0_gnn_W1v, L0_gnn_b1v, L0_gnn_W2v, L0_gnn_Wdot, L0_gnn_Wout, L1_gnn_W1, L1_gnn_b1, L1_gnn_W2, L1_gnn_b2, L1_gnn_gamma, L1_gnn_beta):
    import jax
    import jax.numpy as jnp

    def _L0_gnn_ref(node_attr, edge_attr, edge_sh, Wq, Wang_k, Wlin_k, W1k, b1k, W2k, Wang_v, Wlin_v, W1v, b1v, W2v, Wdot, Wout, edge_index):
        import jax, jax.numpy as jnp
        import numpy as np
        N = 50000
        E = 25000
        D_IN = 128
        SH = 16
        EA = 16
        H = 8
        DQ = 64
        DK = 64
        DV = 128
        HID = 64

        def _conv_per_edge(x_src, edge_attr, edge_sh, Wang, Wlin, W1, b1, W2):
            rad = jax.nn.relu(edge_attr @ W1 + b1) @ W2
            g = edge_sh @ Wang.T
            return x_src * g @ Wlin * rad
        src, dst = (edge_index[0], edge_index[1])
        n = node_attr.shape[0]
        e = src.shape[0]
        q = (node_attr @ Wq).reshape(n, H, DQ // H)
        x_src = node_attr[src]
        k = _conv_per_edge(x_src, edge_attr, edge_sh, Wang_k, Wlin_k, W1k, b1k, W2k).reshape(e, H, DK // H)
        v = _conv_per_edge(x_src, edge_attr, edge_sh, Wang_v, Wlin_v, W1v, b1v, W2v).reshape(e, H, DV // H)
        alpha = jnp.einsum('ehq,qk,ehk->eh', q[dst], Wdot, k)
        amax = jax.ops.segment_max(alpha, dst, num_segments=n)
        ealpha = jnp.exp(alpha - amax[dst])
        denom = jax.ops.segment_sum(ealpha, dst, num_segments=n)
        attn = ealpha / denom[dst]
        out = jax.ops.segment_sum(attn[..., None] * v, dst, num_segments=n)
        return out.reshape(n, DV) @ Wout

    def _L1_gnn_ref(x, edge_src, edge_dst, W1, b1, W2, b2, gamma, beta):
        import jax, jax.numpy as jnp
        import numpy as np
        N_NODES = 3125
        N_EDGES = 50000
        D = 128
        L = 3
        BN_EPS = 1e-05
        n = x.shape[0]
        for i in range(W1.shape[0]):
            agg = jax.ops.segment_sum(x[edge_src], edge_dst, num_segments=n)
            h = x + agg
            h = jnp.maximum(h @ W1[i] + b1[i], 0.0) @ W2[i] + b2[i]
            h = jnp.maximum(h, 0.0)
            mean = jnp.mean(h, axis=0)
            var = jnp.mean(jnp.square(h - mean), axis=0)
            x = gamma[i] * (h - mean) * jax.lax.rsqrt(var + BN_EPS) + beta[i]
        return x
    edge_index = jnp.stack([src, dst])
    x = _layernorm(x + _L0_gnn_ref(x, edge_attr_16, edge_attr_16_n2, L0_gnn_Wq, L0_gnn_Wang_k, L0_gnn_Wlin_k, L0_gnn_W1k, L0_gnn_b1k, L0_gnn_W2k, L0_gnn_Wang_v, L0_gnn_Wlin_v, L0_gnn_W1v, L0_gnn_b1v, L0_gnn_W2v, L0_gnn_Wdot, L0_gnn_Wout, edge_index), axis=-1)
    x = _layernorm(x + _L1_gnn_ref(x, src, dst, L1_gnn_W1, L1_gnn_b1, L1_gnn_W2, L1_gnn_b2, L1_gnn_gamma, L1_gnn_beta), axis=-1)
    return x

_drawn_inputs = setup_inputs


def setup_inputs(seed=0):
    import zlib

    import numpy as np

    out = dict(_drawn_inputs(seed))
    spreads = {'L0_gnn_b1k': (0.0, 0.1),
     'L0_gnn_b1v': (0.0, 0.1),
     'L1_gnn_b1': (0.0, 0.1),
     'L1_gnn_b2': (0.0, 0.1),
     'L1_gnn_gamma': (1.0, 0.2),
     'L1_gnn_beta': (0.0, 0.1)}
    factors = {}
    for name, (base, spread) in spreads.items():
        noise = np.random.default_rng([zlib.crc32(name.encode()), seed]).standard_normal(out[name].shape)
        drawn = base * np.exp(spread * noise) if base else spread * noise
        out[name] = jnp.asarray(drawn.astype(out[name].dtype))
    for name, factor in factors.items():
        out[name] = (out[name] * factor).astype(out[name].dtype)
    return out
```

```python
from contextlib import ExitStack

import concourse.bass as bass
from concourse import mybir

F32 = mybir.dt.float32
I32 = mybir.dt.int32
BF16 = mybir.dt.bfloat16
ALU = mybir.AluOpType
ACT = mybir.ActivationFunctionType
AX_X = mybir.AxisListType.X


def gnn(nc, x, src, dst, edge_attr, edge_sh, Wq, Wang_k, Wlin_k, W1k, b1k, W2k, Wang_v, Wlin_v, W1v, b1v, W2v,
        Wdot, Wout, L_W1, L_b1, L_W2, L_b2, L_gamma, L_beta, out):
    N, D = x.shape
    E = src.shape[0]
    A = edge_attr.shape[1]
    HID = W1k.shape[1]
    DK = W2k.shape[1]
    HD = Wdot.shape[0]
    H = DK // HD
    DVH = D // H
    L = L_W1.shape[0]
    P = 125
    NB = N // P
    T = E // P
    G = 4
    GE = G * P
    IT = E // (2 * GE)
    CH = 10
    CE = E // CH
    CT = T // CH
    CI = IT // CH
    CHH = CH * H
    U = 16
    SQ = 8
    S = -(-(T + NB - 1) // U) * U
    SP_ = S // SQ
    SI = S // U
    BIG = -1.0e30
    W = D + H
    NG = [(g, min(4, NB - g)) for g in range(0, NB, 4)]
    assert N == NB * P and E == IT * 2 * GE and SP_ * SQ == S and SP_ <= 128 and E == CH * CE

    ctx = ExitStack()
    with ctx:
        def sb(name, shape, dt=F32):
            return ctx.enter_context(nc.sbuf_tensor(name, shape, dt))

        def sem(name):
            return ctx.enter_context(nc.semaphore(name))

        def dram(name, shape, dt=F32):
            return nc.dram_tensor(name, shape, dt, kind="Internal").ap()

        q_table = dram("q_table", (N, DK))
        v_table = dram("v_table", (E, D))
        x_tables = [dram(f"x_table{i}", (N, D)) for i in range(L)]
        walk_dram = dram("walk_dram", (2, S), I32)

        ident = sb("ident", [128, 128])
        iota_i = sb("iota_i", [128, P], I32)
        iota_row = sb("iota_row", [128, P])
        step_i = sb("step_i", [SP_, SQ], I32)
        tile_i = sb("tile_i", [1, T], I32)
        ones = sb("ones", [1, 128])
        Wq_sb = sb("Wq_sb", [D, DK])
        Wlk = sb("Wlk", [D, DK])
        Wlv = sb("Wlv", [D, D])
        W1c = sb("W1c", [2 * A, 2 * HID])
        W2kb = sb("W2kb", [2 * HID, DK])
        W2vb = sb("W2vb", [2 * HID, D])
        b1c = sb("b1c", [2 * HID, 1])
        Wang_pad = sb("Wang_pad", [D, 2, 2 * A])
        WangT = sb("WangT", [2 * A, 2, D])
        Wdot_bd = sb("Wdot_bd", [DK, DK])
        Wout_sb = sb("Wout_sb", [D, D])
        LW1 = sb("LW1", [D, L, D])
        LW2 = sb("LW2", [D, L, D])
        Lvec = sb("Lvec", [D, 4, L])
        eps = sb("eps", [128, 1])
        first_dst = sb("first_dst", [1, T], I32)
        start_row = sb("start_row", [1, T])
        step_f = sb("step_f", [SP_, SQ])
        t_f = sb("t_f", [SP_, SQ])
        b_f = sb("b_f", [SP_, SQ])
        t125 = sb("t125", [SP_, SQ])
        b125 = sb("b125", [SP_, SQ])
        b_min = sb("b_min", [SP_, SQ])
        t_i = sb("t_i", [SP_, SQ], I32)
        b_i = sb("b_i", [SP_, SQ], I32)
        walk = sb("walk", [1, 2 * S], I32)
        srcS = sb("srcS", [P, S], I32)
        eidS = sb("eidS", [P, S], I32)
        dstS = sb("dstS", [P, S])
        x_nm = sb("x_nm", [P, NB, D])
        idx_src = sb("idx_src", [P, 2, G], I32)
        idx_dst = sb("idx_dst", [P, 2, G], I32)
        es = sb("es", [P, 2, G, 2, A])
        ring = sb("ring", [P, U, D])
        xg = ring[:, 0:2 * G, :]
        qg = ring[:, 2 * G:3 * G, :].rearrange("p a (b d) -> p (a b) d", b=2)
        sT = sb("sT", [2 * A, 2, GE])
        xT = sb("xT", [D, 2, GE])
        radk = sb("radk", [P, 2, G, DK])
        radv = sb("radv", [P, 2, G, D])
        kt = sb("kt", [P, 2, G, DK])
        vo = sb("vo", [P, 2, G, D])
        alpha_em = sb("alpha_em", [P, T * H])
        oh = sb("oh", [P, 4, P])
        gs = xT[0:P, :, :].rearrange("p a b -> p (a b)")[:, 0:4 * W].rearrange("p (a b) -> p a b", a=4)
        bufA = sb("bufA", [128, CE])
        bufR = sb("bufR", [128, CE])
        bufP = sb("bufP", [128, CE + 2], BF16)
        yk, yv, hidT = (bufA[:, k * 2 * GE:(k + 1) * 2 * GE].rearrange("p (q e) -> p q e", q=2) for k in range(3))
        al = bufA[0:CHH, :]
        run = bufR[0:CHH, :]
        pen = bufP[0:CHH, 0:CE + 1]
        dst_s = sb("dst_s", [CHH, 1], I32)
        tmp = bufA[0:P, 0:NB * D]
        cur = bufA[0:P, NB * D:2 * NB * D]
        tmp2 = bufA[0:P, 2 * NB * D:3 * NB * D]
        fT = bufR[:, 0:N]
        h1T = bufR[:, N:2 * N]
        h2T = bufR[:, 2 * N:3 * N]
        relaid = bufR[0:P, 0:T * H]
        qn = bufR[0:P, 2 * N:2 * N + NB * DK]
        acc = bufP[0:P, 0:2 * NB * W].bitcast(F32).rearrange("p (b w) -> p b w", b=NB)
        ends = sb("ends", [CHH, 4])
        carry = sb("carry", [CHH, 2])
        row_end = sb("row_end", [1, 4, CHH])
        row_c = sb("row_c", [1, 2, CHH])
        row_E = sb("row_E", [1, 2, CHH])
        st25 = sb("st25", [P, 4, NB])
        rden = sb("rden", [P, NB * H])
        st1 = sb("st1", [128, 8])

        bank = [ctx.enter_context(nc.psum_tensor(f"bank{i}", [128, 512], F32)) for i in range(8)]

        srcR = bufA[0:SP_, 0:SQ * P].bitcast(I32).rearrange("s (k p) -> s k p", k=SQ)
        dstR = bufA[0:SP_, 1000:1000 + SQ * P].bitcast(I32).rearrange("s (k p) -> s k p", k=SQ)
        rowsF = bufA[0:SP_, 2000:2000 + 3 * SQ * P].rearrange("s (w k p) -> s w k p", w=3, k=SQ)
        startB = bufA[0:SP_, 5000:5000 + T]
        junk = bufA[0:SP_, 6000:6000 + T]

        s_ident0, s_ident, s_iota = sem("s_ident0"), sem("s_ident"), sem("s_iota")
        s_zero = sem("s_zero")
        s_w, s_w2 = sem("s_w"), sem("s_w2")
        s_x, s_fd = sem("s_x"), sem("s_fd")
        s_d, s_a, s_chainA = sem("s_d"), sem("s_a"), sem("s_chainA")
        s_start, s_startB, s_steps, s_rows = sem("s_start"), sem("s_startB"), sem("s_steps"), sem("s_rows")
        s_rowsF, s_tabT, s_tab, s_walkst, s_walk = (sem("s_rowsF"), sem("s_tabT"), sem("s_tab"), sem("s_walkst"),
                                                    sem("s_walk"))
        s_wangT, s_wang = sem("s_wangT"), sem("s_wang")
        s_xnT, s_xn = sem("s_xnT"), sem("s_xn")
        s_qT, s_qTc, s_qn, s_qnc, s_qst = sem("s_qT"), sem("s_qTc"), sem("s_qn"), sem("s_qnc"), sem("s_qst")
        s_idx = [sem(f"s_idx{q}") for q in range(2)]
        s_es = [sem(f"s_es{q}") for q in range(2)]
        s_gx = [sem(f"s_gx{q}") for q in range(2)]
        s_gq = [sem(f"s_gq{q}") for q in range(2)]
        s_vst = [sem(f"s_vst{q}") for q in range(2)]
        s_T, s_gk, s_gv, s_hid, s_E = sem("s_T"), sem("s_gk"), sem("s_gv"), sem("s_hid"), sem("s_E")
        s_sTc, s_xTc, s_hidc, s_radc = sem("s_sTc"), sem("s_xTc"), sem("s_hidc"), sem("s_radc")
        s_y, s_v, s_t1, s_t2, s_al, s_vfree = (sem("s_y"), sem("s_v"), sem("s_t1"), sem("s_t2"), sem("s_al"),
                                               sem("s_vfree"))
        s_pad, s_relaid = sem("s_pad"), sem("s_relaid")
        s_halo, s_dsts, s_alT, s_alc = sem("s_halo"), sem("s_dsts"), sem("s_alT"), sem("s_alc")
        s_endsd, s_endT, s_carT, s_rowE = sem("s_endsd"), sem("s_endT"), sem("s_carT"), sem("s_rowE")
        s_sub, s_exp, s_eT, s_eTc = sem("s_sub"), sem("s_exp"), sem("s_eT"), sem("s_eTc")
        s_gather = [sem(f"s_gather{u}") for u in range(U)]
        s_cp, s_oh, s_sc, s_mm, s_acc, s_ready = sem("s_cp"), sem("s_oh"), sem("s_sc"), sem("s_mm"), sem("s_acc"), sem("s_ready")
        s_nm, s_nfT, s_nfc = sem("s_nm"), sem("s_nfT"), sem("s_nfc")
        s_m1, s_m1c, s_m2, s_m2c = sem("s_m1"), sem("s_m1c"), sem("s_m2"), sem("s_m2c")
        s_var, s_sd, s_bn, s_bkT, s_bk, s_xst = (sem("s_var"), sem("s_sd"), sem("s_bn"), sem("s_bkT"), sem("s_bk"),
                                                 sem("s_xst"))
        s_out = sem("s_out")

        def done(g):
            return g + 3

        def one_ago(g):
            return g + 2

        def two_ago(g):
            return g + 1

        PASS_A = [s_T, s_hid, s_E, s_sTc, s_xTc, s_hidc, s_radc, s_y, s_al]

        block = ctx.enter_context(nc.Block())

        @block.sync
        def _(sp):
            with nc.allow_non_contiguous_dma(reason="one value for each tile"):
                sp.dma_start(first_dst[:, :], dst.rearrange("(o t p) -> o t p", o=1, p=P)[:, :, 0]).then_inc(s_fd, 16)
            sp.dma_start(x_nm[:, :, :], x.rearrange("(b p) f -> p b f", p=P)).then_inc(s_x, 16)
            sp.wait_ge(s_zero, 1)
            loads = [(Wq_sb[:, :], Wq), (Wlk[:, :], Wlin_k), (Wlv[:, :], Wlin_v),
                     (W1c[0:A, 0:HID], W1k), (W1c[0:A, HID:], W1v), (W2kb[0:HID, :], W2k), (W2vb[HID:, :], W2v),
                     (b1c[0:HID, :], b1k.rearrange("(a b) -> a b", b=1)),
                     (b1c[HID:, :], b1v.rearrange("(a b) -> a b", b=1)),
                     (Wang_pad[:, 0, A:], Wang_k), (Wang_pad[:, 1, A:], Wang_v)]
            loads += [(Wdot_bd[h * HD:(h + 1) * HD, h * HD:(h + 1) * HD], Wdot) for h in range(H)]
            for a, b in loads:
                sp.dma_start(a, b).then_inc(s_w, 16)
            sp.wait_ge(s_steps, 1)
            with nc.allow_non_contiguous_dma(reason="two numbers for each step"):
                for w, tab in enumerate((t_i, b_i)):
                    sp.dma_start(walk_dram[w].rearrange("(k q) -> q k", k=SQ), tab[:, :]).then_inc(s_walkst, 16)
                sp.wait_ge(s_walkst, 32)
                sp.dma_start(walk[:, :], walk_dram.rearrange("(o w) s -> o (w s)", o=1)).then_inc(s_walk, 16)
                sp.dma_start(Wout_sb[:, :], Wout).then_inc(s_w2, 16)
                sp.dma_start(LW1[:, :, :], L_W1.rearrange("l a b -> a l b")).then_inc(s_w2, 16)
                sp.dma_start(LW2[:, :, :], L_W2.rearrange("l a b -> a l b")).then_inc(s_w2, 16)
                for k, vec in enumerate((L_b1, L_b2, L_gamma, L_beta)):
                    sp.dma_start(Lvec[:, k, :], vec.rearrange("l a -> a l")).then_inc(s_w2, 16)
            sp.wait_ge(s_qnc, len(range(0, NB, 8)))
            sp.dma_start(q_table.rearrange("(b p) k -> p b k", p=P),
                         qn[:, :].rearrange("p (b k) -> p b k", b=NB)).then_inc(s_qst, 16)

            src_v = src.rearrange("(i p q j) -> i q p j", p=P, q=2, j=G)
            dst_v = dst.rearrange("(i p q j) -> i q p j", p=P, q=2, j=G)
            ea_v = edge_attr.rearrange("(i p q j) a -> i q p j a", p=P, q=2, j=G)
            sh_v = edge_sh.rearrange("(i p q j) a -> i q p j a", p=P, q=2, j=G)
            v_v = v_table.rearrange("(i p q j) f -> i q p (j f)", p=P, q=2, j=G)

            def one(view, i):
                return view[bass.ds(i, 1)] if not isinstance(i, int) else view[i:i + 1]

            def load(i, q):
                sp.dma_start(idx_src[:, q, :], one(src_v, i)[0, q]).then_inc(s_idx[q], 16)
                sp.dma_start(idx_dst[:, q, :], one(dst_v, i)[0, q]).then_inc(s_idx[q], 16)
                sp.dma_start(es[:, q, :, 0, :], one(ea_v, i)[0, q]).then_inc(s_es[q], 16)
                sp.dma_start(es[:, q, :, 1, :], one(sh_v, i)[0, q]).then_inc(s_es[q], 16)

            def store(i, q):
                sp.wait_ge(s_v, 2 * i + q + 1)
                sp.sem_inc(s_pad, 1)
                sp.dma_start(one(v_v, i)[0, q], vo[:, q, :, :].rearrange("p j f -> p (j f)")).then_inc(s_vst[q], 16)

            def stored(i):
                for q in range(2):
                    sp.wait_ge(s_vst[q], 16 * i + 16)
                    sp.sem_inc(s_vfree, 1)

            sp.sem_inc(s_vfree, 2)
            for q in range(2):
                load(0, q)
            with sp.Fori(0, IT - 1) as i:
                for q in range(2):
                    g = 2 * i + q
                    sp.wait_ge(s_gx[q], 16 * G * (i + 1))
                    sp.wait_ge(s_gq[q], 16 * G * (i + 1))
                    sp.sem_inc(s_pad, 1)
                    sp.wait_ge(s_T, done(g))
                    sp.sem_inc(s_pad, 1)
                    load(i + 1, q)
                for q in range(2):
                    store(i, q)
                stored(i)
            for q in range(2):
                store(IT - 1, q)
            stored(IT - 1)

            sp.wait_ge(s_halo, 1)
            sp.wait_ge(s_al, 2 * IT + 2)
            dview = bufR[0:CHH, :].bitcast(I32)
            for c in range(CH):
                sp.dma_start(dview[c * H:(c + 1) * H, :], dst[c * CE:(c + 1) * CE].partition_broadcast(H)).then_inc(s_dsts, 16)
                if c < CH - 1:
                    sp.dma_start(dst_s[c * H:(c + 1) * H, :], dst[(c + 1) * CE:(c + 1) * CE + 1].partition_broadcast(H)).then_inc(s_dsts, 16)

            for l in range(L):
                if l == 0:
                    sp.wait_ge(s_ready, 1)
                else:
                    sp.wait_ge(s_bk, l * len(NG))
                row = x_nm[:, :, :] if l == 0 else cur.rearrange("p (b f) -> p b f", b=NB)
                sp.dma_start(x_tables[l].rearrange("(b p) f -> p b f", p=P), row).then_inc(s_xst, 16)
            sp.wait_ge(s_ready, 2)
            sp.dma_start(out.rearrange("(b p) f -> p b f", p=P),
                         tmp2.rearrange("p (b f) -> p b f", b=NB)).then_inc(s_out, 16)
            sp.wait_ge(s_out, 16)

        @block.gpsimd
        def _(pool):
            pool.memset(ident[:, :], 0.0).then_inc(s_ident0, 1)
            pool.wait_ge(s_ident0, 1)
            pool.affine_select(out=ident[:, :], in_=ident[:, :], compare_op=ALU.not_equal, fill=1.0, base=0,
                               pattern=[[-1, 128]], channel_multiplier=1).then_inc(s_ident, 1)
            pool.iota(iota_i[:, :], pattern=[[1, P]], base=0, channel_multiplier=0).then_inc(s_iota, 1)
            pool.iota(step_i[:, :], pattern=[[SP_, SQ]], base=0, channel_multiplier=1).then_inc(s_iota, 1)
            pool.iota(tile_i[:, :], pattern=[[1, T]], base=0, channel_multiplier=0).then_inc(s_iota, 1)
            pool.wait_ge(s_steps, 1)
            for rows, table in ((srcR, src), (dstR, dst)):
                for k in range(SQ):
                    pool.indirect_dma_start(rows[:, k, :], None, table.rearrange("(t p) -> t p", p=P),
                                            bass.IndirectOffsetOnAxis(ap=t_i[:, k:k + 1], axis=0)).then_inc(s_rows, 16)
            pool.wait_ge(s_qst, 16)
            with pool.Fori(0, IT) as i:
                for q in range(2):
                    g = 2 * i + q
                    pool.wait_ge(s_idx[q], 32 * i + 32)
                    pool.wait_ge(s_T, two_ago(g))
                    pool.wait_ge(s_al, two_ago(g))
                    pool.sem_inc(s_pad, 1)
                    for j in range(G):
                        pool.indirect_dma_start(xg[:, q * G + j, :], None, x,
                                                bass.IndirectOffsetOnAxis(ap=idx_src[:, q, j:j + 1], axis=0)).then_inc(s_gx[q], 16)
                    for j in range(G):
                        pool.indirect_dma_start(qg[:, q * G + j, :], None, q_table,
                                                bass.IndirectOffsetOnAxis(ap=idx_dst[:, q, j:j + 1], axis=0)).then_inc(s_gq[q], 16)
            idx_slot = kt[:, :, :, :].rearrange("p a b c -> p (a b c)")[:, 0:U].bitcast(I32)
            pool.wait_ge(s_al, 2 * IT + 2)
            pool.wait_ge(s_tab, 6)
            for n in range(L + 1):
                table, where = (v_table, eidS) if n == 0 else (x_tables[n - 1], srcS)
                if n == 0:
                    for q in range(2):
                        pool.wait_ge(s_vst[q], 16 * IT)
                else:
                    pool.wait_ge(s_xst, 16 * n)
                with pool.Fori(0, SI) as i:
                    for b in range(2):
                        a = U // 2 * b
                        pool.wait_ge(s_mm, n * S + U * i + a + U // 2)
                        pool.tensor_copy(idx_slot[:, a:a + U // 2], where[:, bass.ds(i * U + a, U // 2)]).then_inc(s_cp, 1)
                        pool.wait_ge(s_cp, 2 * (n * SI + i) + b + 1)
                        pool.sem_inc(s_pad, 1)
                        for u in range(a, a + U // 2):
                            pool.indirect_dma_start(ring[:, u, :], None, table,
                                                    bass.IndirectOffsetOnAxis(ap=idx_slot[:, u:u + 1], axis=0)).then_inc(s_gather[u], 16)

        @block.scalar
        def _(act):
            for s in (s_sTc, s_xTc, s_hidc, s_radc):
                act.sem_inc(s, 2)
            act.wait_ge(s_wangT, 1)
            act.copy(WangT[:, :, :], bank[7][0:2 * A, 0:2 * D].rearrange("p (w f) -> p w f", w=2)).then_inc(s_wang, 1)
            for k, (g, m) in enumerate(NG):
                act.wait_ge(s_xnT, k + 1)
                act.copy(fT[:, g * P:(g + m) * P], bank[k % 2][:, 0:m * P]).then_inc(s_xn, 1)
            for k, (g, m) in enumerate(NG):
                act.wait_ge(s_qT, k + 1)
                act.copy(h1T[0:DK, g * P:(g + m) * P], bank[2 + k % 2][0:DK, 0:m * P]).then_inc(s_qTc, 1)
            def copies(g, q):
                act.wait_ge(s_T, done(g))
                act.wait_ge(s_hid, two_ago(g))
                act.copy(sT[:, q, :], bank[1][0:2 * A, 0:GE]).then_inc(s_sTc, 1)
                act.wait_ge(s_y, two_ago(g))
                act.copy(xT[:, q, :], bank[0][:, 0:GE]).then_inc(s_xTc, 1)

            def relu(g, q):
                act.wait_ge(s_hid, done(g))
                act.wait_ge(s_E, two_ago(g))
                act.activation(hidT[:, q, :], bank[4][:, 0:GE], ACT.Relu, bias=b1c[:, 0:1]).then_inc(s_hidc, 1)

            def rads(g, q):
                act.wait_ge(s_E, done(g))
                act.wait_ge(s_al, two_ago(g))
                act.copy(radk[:, q, :, :], bank[5][0:P, 256:512].rearrange("p (j k) -> p j k", j=G))
                act.copy(radv[:, q, :, :], bank[7][0:P, :].rearrange("p (j k) -> p j k", j=G)).then_inc(s_radc, 1)

            with act.Fori(0, IT) as i:
                g0, g1 = 2 * i, 2 * i + 1
                copies(g0, 0)
                relu(g0, 0)
                copies(g1, 1)
                rads(g0, 0)
                relu(g1, 1)
                rads(g1, 1)

            for k in range(0, 2 * CI):
                if k % 2 == 1:
                    act.wait_ge(s_alT, k + 1)
                    act.copy(al[:, (k // 2) * 8 * P:(k // 2 + 1) * 8 * P].rearrange("c (p q j) -> c q j p", q=2, j=G)[:, k % 2],
                             bank[k % 2][0:CHH, 0:GE].rearrange("c (j p) -> c j p", j=G)).then_inc(s_alc, 1)
            act.wait_ge(s_sub, 1)
            act.activation(al, al, ACT.Exp).then_inc(s_exp, 1)
            base = {"nf": 0}

            def features():
                for k, (g, m) in enumerate(NG):
                    act.wait_ge(s_nfT, base["nf"] + k + 1)
                    act.copy(fT[:, g * P:(g + m) * P], bank[k % 2][:, 0:m * P]).then_inc(s_nfc, 1)
                base["nf"] += len(NG)

            def root(n, sd, var, scale):
                act.wait_ge(s_var, n)
                act.activation(sd, var, ACT.Sqrt, bias=eps[0:sd.shape[0], 0:1], scale=scale).then_inc(s_sd, 1)

            features()
            root(1, st25[:, 2, :], st25[:, 1, :], 1.0 / D)
            for l in range(L):
                features()
                for k, (g, m) in enumerate(NG):
                    act.wait_ge(s_m1, l * len(NG) + k + 1)
                    act.activation(h1T[:, g * P:(g + m) * P], bank[2 + k % 2][:, 0:m * P], ACT.Relu,
                                   bias=Lvec[:, 0, l:l + 1]).then_inc(s_m1c, 1)
                for k, (g, m) in enumerate(NG):
                    act.wait_ge(s_m2, l * len(NG) + k + 1)
                    act.activation(h2T[:, g * P:(g + m) * P], bank[4 + k % 2][:, 0:m * P], ACT.Relu,
                                   bias=Lvec[:, 1, l:l + 1]).then_inc(s_m2c, 1)
                root(l + 2, st1[:, 3:4], st1[:, 2:3], 1.0 / N)
                for k, (g, m) in enumerate(NG):
                    act.wait_ge(s_bkT, l * len(NG) + k + 1)
                    act.copy(cur[:, g * D:(g + m) * D], bank[6 + k % 2][0:P, 0:m * D]).then_inc(s_bk, 1)
            root(L + 2, st25[:, 2, :], st25[:, 1, :], 1.0 / D)

        @block.tensor
        def _(pe):
            for s in (s_T, s_hid, s_E):
                pe.sem_inc(s, 2)
            pe.sem_inc(s_mm, U)
            pe.wait_ge(s_ident, 1)
            pe.wait_ge(s_start, 1)
            for c in range(2):
                mm = pe.matmul(bank[5 + c][0:SP_, 0:T // 2], lhsT=ones[:, 0:SP_], rhs=start_row[:, c * (T // 2):(c + 1) * (T // 2)],
                               start=True, stop=True)
            mm.then_inc(s_startB, 1)
            pe.wait_ge(s_w, 16 * (11 + H))
            for w in range(2):
                mm = pe.transpose(bank[7][0:2 * A, w * D:(w + 1) * D], Wang_pad[:, w, :], ident[:, :])
            mm.then_inc(s_wangT, 1)
            pe.wait_ge(s_x, 16)
            for k, (g, m) in enumerate(NG):
                if k >= 2:
                    pe.wait_ge(s_xn, k - 1)
                for b in range(m):
                    mm = pe.transpose(bank[k % 2][:, b * P:(b + 1) * P], x_nm[:, g + b, :], ident[0:P, 0:P])
                mm.then_inc(s_xnT, 1)
            for k, (g, m) in enumerate(NG):
                pe.wait_ge(s_xn, k + 1)
                if k >= 2:
                    pe.wait_ge(s_qTc, k - 1)
                pe.matmul(bank[2 + k % 2][0:DK, 0:m * P], lhsT=Wq_sb[:, :], rhs=fT[:, g * P:(g + m) * P],
                          start=True, stop=True).then_inc(s_qT, 1)
            pe.wait_ge(s_qTc, len(NG))
            for k, g in enumerate(range(0, NB, 8)):
                if k >= 1:
                    pe.wait_ge(s_qnc, k)
                for b in range(g, min(g + 8, NB)):
                    mm = pe.matmul(bank[4][0:P, (b - g) * DK:(b - g + 1) * DK], lhsT=h1T[0:DK, b * P:(b + 1) * P],
                                   rhs=Wdot_bd[:, :], start=True, stop=True)
                mm.then_inc(s_qn, 1)
            pe.wait_ge(s_rowsF, 1)
            pe.wait_ge(s_wang, 1)
            for w in range(3):
                for c in range(2):
                    if 2 * w + c >= 2:
                        pe.wait_ge(s_tab, 2 * w + c - 1)
                    for k in range(4):
                        mm = pe.transpose(bank[6 + c][0:P, k * SP_:(k + 1) * SP_], rowsF[:, w, 4 * c + k, :],
                                          ident[0:SP_, 0:SP_])
                    mm.then_inc(s_tabT, 1)
            pe.wait_ge(s_tab, 6)
            def turn(i, q, g):
                pe.wait_ge(s_gx[q], 16 * G * i + 16 * G)
                pe.wait_ge(s_es[q], 32 * i + 32)
                pe.wait_ge(s_xTc, one_ago(g))
                for j in range(G):
                    pe.transpose(bank[1][0:2 * A, j * P:(j + 1) * P], es[:, q, j, :, :].rearrange("p w a -> p (w a)"),
                                 ident[0:P, 0:P])
                for j in range(G):
                    mm = pe.transpose(bank[0][:, j * P:(j + 1) * P], xg[:, q * G + j, :], ident[0:P, 0:P])
                mm.then_inc(s_T, 1)

            def features(q, g):
                pe.wait_ge(s_sTc, done(g))
                pe.wait_ge(s_y, one_ago(g))
                for w in range(2):
                    pe.matmul(bank[2 + w][:, 0:GE], lhsT=WangT[:, w, :], rhs=sT[:, q, :], start=True, stop=True)
                pe.wait_ge(s_hidc, one_ago(g))
                pe.matmul(bank[4][:, 0:GE], lhsT=W1c[:, :], rhs=sT[:, q, :], start=True, stop=True).then_inc(s_hid, 1)

            def edges(q, g):
                pe.wait_ge(s_y, done(g))
                pe.wait_ge(s_hidc, done(g))
                pe.wait_ge(s_al, one_ago(g))
                pe.wait_ge(s_radc, one_ago(g))
                for j in range(G):
                    e = slice(j * P, (j + 1) * P)
                    pe.matmul(bank[5][0:P, 256 + j * DK:256 + (j + 1) * DK], lhsT=hidT[:, q, e], rhs=W2kb[:, :], start=True, stop=True)
                    pe.matmul(bank[7][0:P, j * D:(j + 1) * D], lhsT=hidT[:, q, e], rhs=W2vb[:, :], start=True, stop=True)
                    pe.matmul(bank[5][0:P, j * DK:(j + 1) * DK], lhsT=yk[:, q, e], rhs=Wlk[:, :], start=True, stop=True)
                    mm = pe.matmul(bank[6][0:P, j * D:(j + 1) * D], lhsT=yv[:, q, e], rhs=Wlv[:, :], start=True, stop=True)
                mm.then_inc(s_E, 1)

            with pe.Fori(0, IT) as i:
                g0, g1 = 2 * i, 2 * i + 1
                turn(i, 0, g0)
                features(0, g0)
                turn(i, 1, g1)
                edges(0, g0)
                features(1, g1)
                edges(1, g1)

            pe.wait_ge(s_relaid, 1)
            for k in range(2 * CI):
                if k >= 2:
                    pe.wait_ge(s_alc if k % 2 else s_eTc, k // 2)
                for j in range(G):
                    mm = pe.transpose(bank[k % 2][0:CHH, j * P:(j + 1) * P], relaid[:, (k * G + j) * CHH:(k * G + j + 1) * CHH], ident[0:P, 0:P])
                mm.then_inc(s_alT, 1)
            pe.wait_ge(s_endsd, 1)
            for w in range(4):
                mm = pe.transpose(bank[2][0:1, w * CHH:(w + 1) * CHH], ends[:, w:w + 1], ident[0:CHH, 0:CHH])
            mm.then_inc(s_endT, 1)
            pe.wait_ge(s_rowE, 1)
            for w in range(2):
                mm = pe.matmul(bank[3][0:CHH, w:w + 1], lhsT=row_c[:, w, :], rhs=ones[:, 0:1], start=True, stop=True)
            mm.then_inc(s_carT, 1)
            pe.wait_ge(s_exp, 1)
            for k in range(CT // 5):
                if k >= 2:
                    pe.wait_ge(s_eTc, CI + k - 1)
                for t in range(5):
                    c = 5 * k + t
                    mm = pe.transpose(bank[4 + k % 2][0:P, t * CHH:(t + 1) * CHH], al[:, c * P:(c + 1) * P], ident[0:CHH, 0:CHH])
                mm.then_inc(s_eT, 1)

            def aggregate(n):
                w = W if n == 0 else D
                with pe.Fori(0, SI) as i:
                    for u in range(U):
                        st = n * S + U * i + u
                        pe.wait_ge(s_oh, st + 1)
                        if n == 0:
                            pe.wait_ge(s_sc, st + 1)
                        else:
                            pe.wait_ge(s_gather[u], 16 * (n * SI + i) + 16)
                        pe.wait_ge(s_acc, st + 1)
                        rows = gs[:, u % 4, :] if n == 0 else ring[:, u, :]
                        pe.matmul(bank[u % 4][0:P, 0:w], lhsT=oh[:, u % 4, :], rhs=rows, start=True, stop=True).then_inc(s_mm, 1)

            base = {"nf": 0}

            def transposed(k0):
                pe.wait_ge(s_nm, k0)
                for k, (g, m) in enumerate(NG):
                    if k >= 2:
                        pe.wait_ge(s_nfc, base["nf"] + k - 1)
                    for b in range(m):
                        mm = pe.transpose(bank[k % 2][:, b * P:(b + 1) * P], tmp[:, (g + b) * D:(g + b + 1) * D], ident[0:P, 0:P])
                    mm.then_inc(s_nfT, 1)
                base["nf"] += len(NG)
                pe.wait_ge(s_nfc, base["nf"])

            aggregate(0)
            transposed(1)
            pe.wait_ge(s_w2, 16 * 7)
            for k, (g, m) in enumerate(NG):
                if k >= 2:
                    pe.wait_ge(s_bn, k - 1)
                for b in range(m):
                    mm = pe.matmul(bank[2 + k % 2][0:P, b * D:(b + 1) * D], lhsT=fT[:, (g + b) * P:(g + b + 1) * P], rhs=Wout_sb[:, :],
                                   start=True, stop=True)
                mm.then_inc(s_qn, 1)
            for l in range(L):
                aggregate(l + 1)
                transposed(l + 2)
                for k, (g, m) in enumerate(NG):
                    if k >= 2:
                        pe.wait_ge(s_m1c, l * len(NG) + k - 1)
                    pe.matmul(bank[2 + k % 2][:, 0:m * P], lhsT=LW1[:, l, :], rhs=fT[:, g * P:(g + m) * P], start=True, stop=True).then_inc(s_m1, 1)
                for k, (g, m) in enumerate(NG):
                    pe.wait_ge(s_m1c, l * len(NG) + k + 1)
                    if k >= 2:
                        pe.wait_ge(s_m2c, l * len(NG) + k - 1)
                    pe.matmul(bank[4 + k % 2][:, 0:m * P], lhsT=LW2[:, l, :], rhs=h1T[:, g * P:(g + m) * P], start=True, stop=True).then_inc(s_m2, 1)
                pe.wait_ge(s_bn, len(NG) + l + 1)
                for k, (g, m) in enumerate(NG):
                    if k >= 2:
                        pe.wait_ge(s_bk, l * len(NG) + k - 1)
                    for b in range(m):
                        mm = pe.transpose(bank[6 + k % 2][0:P, b * D:(b + 1) * D], fT[:, (g + b) * P:(g + b + 1) * P], ident[:, :])
                    mm.then_inc(s_bkT, 1)

        @block.vector
        def _(dve):
            chain = [0]

            def link(ins):
                chain[0] += 1
                ins.then_inc(s_d, 1)
                dve.wait_ge(s_d, chain[0])

            for s in (s_y, s_al):
                dve.sem_inc(s, 2)
            dve.sem_inc(s_acc, 4)
            dve.memset(W1c[:, :], 0.0)
            dve.memset(W2kb[:, :], 0.0)
            dve.memset(W2vb[:, :], 0.0)
            dve.memset(Wang_pad[:, :, :], 0.0)
            dve.memset(eps[:, :], 1e-5)
            dve.memset(ones[:, :], 1.0)
            dve.memset(Wdot_bd[:, :], 0.0).then_inc(s_zero, 1)
            dve.wait_ge(s_iota, 3)
            dve.tensor_copy(iota_row[:, :], iota_i[:, :])
            dve.tensor_copy(step_f[:, :], step_i[:, :])
            dve.wait_ge(s_fd, 16)
            half = float(P // 2)
            C = 12582912.0
            link(dve.tensor_scalar(start_row[:, :], first_dst[:, :], half, 1.0 / P, ALU.subtract, ALU.mult))
            link(dve.tensor_scalar(start_row[:, :], start_row[:, :], C, None, ALU.add))
            link(dve.tensor_scalar(start_row[:, :], start_row[:, :], C, None, ALU.subtract))
            dve.tensor_tensor(start_row[:, :], start_row[:, :], tile_i[:, :], ALU.add).then_inc(s_start, 1)
            dve.wait_ge(s_startB, 1)
            for c in range(2):
                link(dve.tensor_copy(startB[:, c * (T // 2):(c + 1) * (T // 2)], bank[5 + c][0:SP_, 0:T // 2]))
            for k in range(SQ):
                link(dve.tensor_scalar(junk[:, 1:T], startB[:, 1:T], step_f[:, k:k + 1], None, ALU.is_le))
                link(dve.reduce_sum(t_f[:, k:k + 1], junk[:, 1:T], axis=AX_X))
            link(dve.tensor_tensor(b_f[:, :], step_f[:, :], t_f[:, :], ALU.subtract))
            link(dve.tensor_scalar(b_min[:, :], b_f[:, :], float(NB - 1), None, ALU.min))
            dve.tensor_scalar(t125[:, :], t_f[:, :], float(P), None, ALU.mult)
            dve.tensor_scalar(b125[:, :], b_f[:, :], float(P), None, ALU.mult)
            dve.tensor_copy(t_i[:, :], t_f[:, :])
            link(dve.tensor_copy(b_i[:, :], b_min[:, :]))
            dve.sem_inc(s_steps, 1)
            for k, g in enumerate(range(0, NB, 8)):
                m = min(8, NB - g)
                dve.wait_ge(s_qn, k + 1)
                dve.tensor_copy(qn[:, g * DK:(g + m) * DK], bank[4][0:P, 0:m * DK]).then_inc(s_qnc, 1)
            dve.wait_ge(s_rows, 16 * 2 * SQ)
            link(dve.tensor_copy(rowsF[:, 0, :, :], srcR))
            for k in range(SQ):
                dve.tensor_scalar(rowsF[:, 1, k, :], iota_row[0:SP_, :], t125[:, k:k + 1], None, ALU.add)
                link(dve.tensor_scalar(rowsF[:, 2, k, :], dstR[:, k, :], b125[:, k:k + 1], None, ALU.subtract))
            dve.sem_inc(s_rowsF, 1)
            for w, tab in enumerate((srcS, eidS, dstS)):
                for c in range(2):
                    dve.wait_ge(s_tabT, 2 * w + c + 1)
                    dve.tensor_copy(tab[:, 4 * c * SP_:4 * (c + 1) * SP_], bank[6 + c][0:P, 0:4 * SP_]).then_inc(s_tab, 1)
            def gated(q, g):
                dve.wait_ge(s_xTc, done(g))
                dve.wait_ge(s_hid, done(g))
                dve.wait_ge(s_E, two_ago(g))
                dve.tensor_tensor(yk[:, q, :], xT[:, q, :], bank[2][:, 0:GE], ALU.mult)
                dve.tensor_tensor(yv[:, q, :], xT[:, q, :], bank[3][:, 0:GE], ALU.mult).then_inc(s_y, 1)

            def finish(i, q, g):
                dve.wait_ge(s_radc, done(g))
                dve.tensor_tensor(kt[:, q, :, :], radk[:, q, :, :],
                                  bank[5][0:P, 0:256].rearrange("p (j k) -> p j k", j=G), ALU.mult).then_inc(s_t1, 1)
                dve.wait_ge(s_vfree, g + 1)
                dve.tensor_tensor(vo[:, q, :, :], radv[:, q, :, :],
                                  bank[6][0:P, :].rearrange("p (j k) -> p j k", j=G), ALU.mult).then_inc(s_v, 1)
                dve.wait_ge(s_gq[q], 16 * G * i + 16 * G)
                dve.wait_ge(s_t1, g + 1)
                dve.tensor_tensor(kt[:, q, :, :], kt[:, q, :, :], qg[:, q * G:(q + 1) * G, :], ALU.mult).then_inc(s_t2, 1)
                dve.wait_ge(s_t2, g + 1)
                dve.reduce_sum(alpha_em[:, bass.ds(g * (G * H), G * H)],
                               kt[:, q, :, :].rearrange("p j (h k) -> p (j h) k", h=H), axis=AX_X).then_inc(s_al, 1)

            with dve.Fori(0, IT) as i:
                for q in range(2):
                    gated(q, 2 * i + q)
                    finish(i, q, 2 * i + q)

            dve.wait_ge(s_al, 2 * IT + 2)
            dve.tensor_copy(relaid.rearrange("p (t c h) -> p t c h", c=CH, h=H),
                            alpha_em[:, :].rearrange("p (c t h) -> p t c h", c=CH, h=H)).then_inc(s_relaid, 1)
            for k in range(0, 2 * CI, 2):
                dve.wait_ge(s_alT, k + 1)
                dve.tensor_copy(al[:, (k // 2) * 8 * P:(k // 2 + 1) * 8 * P].rearrange("c (p q j) -> c q j p", q=2, j=G)[:, 0],
                                bank[0][0:CHH, 0:GE].rearrange("c (j p) -> c j p", j=G)).then_inc(s_eTc, 1)
            dve.wait_ge(s_alT, 2 * CI)
            dve.memset(dst_s[:, :], -1).then_inc(s_halo, 1)
            dview = bufR[0:CHH, :].bitcast(I32)
            dve.wait_ge(s_dsts, 16 * (2 * CH - 1))
            link(dve.tensor_tensor(pen[:, 1:CE], dview[:, 1:CE], dview[:, 0:CE - 1], ALU.not_equal))
            link(dve.tensor_tensor(pen[:, CE:CE + 1], dst_s[:, :], dview[:, CE - 1:CE], ALU.not_equal))
            link(dve.tensor_scalar(pen[:, 1:CE + 1], pen[:, 1:CE + 1], BIG, None, ALU.mult))
            link(dve.memset(pen[:, 0:1], 0.0))
            dve.wait_ge(s_alc, CI)
            link(dve.tensor_tensor_scan(run, pen[:, 0:CE], al, BIG, ALU.add, ALU.max))
            link(dve.tensor_tensor_scan(run[:, ::-1], pen[:, CE:0:-1], run[:, ::-1], BIG, ALU.add, ALU.max))
            FIRST, LAST, INNER, LINK = range(4)
            dve.tensor_copy(ends[:, FIRST:FIRST + 1], run[:, 0:1])
            dve.tensor_copy(ends[:, LAST:LAST + 1], run[:, CE - 1:CE])
            dve.tensor_copy(ends[:, LINK:LINK + 1], pen[:, CE:CE + 1])
            dve.tensor_reduce(ends[:, INNER:INNER + 1], pen[:, 1:CE], AX_X, ALU.min).then_inc(s_endsd, 1)
            dve.wait_ge(s_endT, 1)
            link(dve.tensor_copy(row_end[:, :, :], bank[2][0:1, 0:4 * CHH].rearrange("o (w c) -> o w c", w=4)))
            link(dve.memset(row_c[:, :, :], BIG))

            def part(row, c):
                return row[:, c * H:(c + 1) * H]

            for c in range(1, CH):
                link(dve.tensor_tensor(part(row_E[:, 0, :], c), part(row_c[:, 0, :], c - 1), part(row_end[:, INNER, :], c - 1), ALU.add))
                link(dve.tensor_tensor(part(row_E[:, 0, :], c), part(row_E[:, 0, :], c), part(row_end[:, LAST, :], c - 1), ALU.max))
                link(dve.tensor_tensor(part(row_c[:, 0, :], c), part(row_E[:, 0, :], c), part(row_end[:, LINK, :], c - 1), ALU.add))
            for c in range(CH - 2, -1, -1):
                link(dve.tensor_tensor(part(row_E[:, 1, :], c), part(row_c[:, 1, :], c + 1), part(row_end[:, INNER, :], c + 1), ALU.add))
                link(dve.tensor_tensor(part(row_E[:, 1, :], c), part(row_E[:, 1, :], c), part(row_end[:, FIRST, :], c + 1), ALU.max))
                link(dve.tensor_tensor(part(row_c[:, 1, :], c), part(row_E[:, 1, :], c), part(row_end[:, LINK, :], c), ALU.add))
            dve.sem_inc(s_rowE, 1)
            dve.wait_ge(s_carT, 1)
            link(dve.tensor_copy(carry[:, :], bank[3][0:CHH, 0:2]))
            link(dve.tensor_tensor_scan(run, pen[:, 0:CE], run, carry[:, 0:1], ALU.add, ALU.max))
            link(dve.memset(pen[:, CE:CE + 1], 0.0))
            link(dve.tensor_tensor_scan(run[:, ::-1], pen[:, CE:0:-1], run[:, ::-1], carry[:, 1:2], ALU.add, ALU.max))
            dve.tensor_tensor(al, al, run, ALU.subtract).then_inc(s_sub, 1)
            for k in range(CT // 5):
                dve.wait_ge(s_eT, k + 1)
                dve.tensor_copy(alpha_em[:, :].rearrange("p (c t h) -> p t c h", c=CH, h=H)[:, 5 * k:5 * k + 5],
                                bank[4 + k % 2][0:P, 0:5 * CHH].rearrange("p (t c h) -> p t c h", t=5, c=CH)).then_inc(s_eTc, 1)
            dve.wait_ge(s_walk, 16)
            dve.wait_ge(s_eTc, CI + CT // 5)

            def aggregate(n):
                w = W if n == 0 else D
                link(dve.memset(acc[:, :, :], 0.0))

                def prepare(i, u):
                    st = n * S + U * i + u
                    dve.wait_ge(s_mm, st + U - 3)
                    dve.tensor_scalar(oh[:, u % 4, :], iota_row[0:P, :], dstS[:, bass.ds(i * U + u, 1)], None, ALU.is_equal).then_inc(s_oh, 1)
                    if n == 0:
                        t = dve.value_load(walk[0:1, bass.ds(i * U + u, 1)], min_val=0, max_val=T - 1)
                        dve.wait_ge(s_gather[u], 16 * i + 16)
                        e = alpha_em[:, bass.ds(t * H, H)]
                        dve.tensor_tensor(gs[:, u % 4, 0:D].rearrange("p (h v) -> p h v", h=H),
                                          ring[:, u, :].rearrange("p (h v) -> p h v", h=H),
                                          e.unsqueeze(2).to_broadcast([P, H, D // H]), ALU.mult)
                        dve.tensor_copy(gs[:, u % 4, D:W], e).then_inc(s_sc, 1)

                def add(i, u):
                    st = n * S + U * i + u
                    b = dve.value_load(walk[0:1, bass.ds(i * U + u + S, 1)], min_val=0, max_val=NB - 1)
                    dve.wait_ge(s_acc, st + 4)
                    dve.wait_ge(s_mm, st + U + 1)
                    o = acc[:, bass.ds(b, 1), 0:w]
                    dve.tensor_tensor(o, bank[u % 4][0:P, 0:w].unsqueeze(1), o, ALU.add).then_inc(s_acc, 1)

                with dve.Fori(0, SI) as i:
                    for u in range(U + 2):
                        if u < U:
                            prepare(i, u)
                        if u >= 2:
                            add(i, u - 2)

            def blocks(a):
                return a.rearrange("p (b f) -> p b f", b=NB)

            def spread(a):
                return a.unsqueeze(2).to_broadcast([P, NB, D])

            def layernorm(n, y, o):
                sq = bufR[0:P, 2 * N:2 * N + NB * D]
                link(dve.reduce_sum(st25[:, 0, :], blocks(y), axis=AX_X))
                link(dve.tensor_scalar(st25[:, 0, :], st25[:, 0, :], -1.0 / D, None, ALU.mult))
                link(dve.tensor_tensor(blocks(y), blocks(y), spread(st25[:, 0, :]), ALU.add))
                link(dve.tensor_tensor(sq, y, y, ALU.mult))
                dve.reduce_sum(st25[:, 1, :], blocks(sq), axis=AX_X).then_inc(s_var, 1)
                dve.wait_ge(s_sd, n)
                link(dve.reciprocal(st25[:, 3, :], st25[:, 2, :]))
                dve.tensor_tensor(o, blocks(y), spread(st25[:, 3, :]), ALU.mult).then_inc(s_ready, 1)

            aggregate(0)
            dve.wait_ge(s_acc, S + 4)
            link(dve.tensor_scalar(rden[:, :].rearrange("p (b h) -> p b h", b=NB), acc[:, :, D:W], 0.5, None, ALU.max))
            link(dve.reciprocal(rden[:, :], rden[:, :]))
            for b in range(NB):
                mul = dve.tensor_tensor(tmp[:, b * D:(b + 1) * D].rearrange("p (h v) -> p h v", h=H),
                                        acc[:, b, 0:D].rearrange("p (h v) -> p h v", h=H),
                                        rden[:, b * H:(b + 1) * H].unsqueeze(2).to_broadcast([P, H, D // H]), ALU.mult)
            mul.then_inc(s_nm, 1)
            for k, (g, m) in enumerate(NG):
                dve.wait_ge(s_qn, len(range(0, NB, 8)) + k + 1)
                dve.tensor_tensor(tmp2[:, g * D:(g + m) * D], bank[2 + k % 2][0:P, 0:m * D],
                                  x_nm[:, g:g + m, :].rearrange("p b f -> p (b f)"), ALU.add).then_inc(s_bn, 1)
            dve.wait_ge(s_bn, len(NG))
            layernorm(1, tmp2, x_nm[:, :, :])
            dve.wait_ge(s_ready, 1)
            for l in range(L):
                aggregate(l + 1)
                dve.wait_ge(s_acc, (l + 2) * S + 4)
                dve.tensor_tensor(blocks(tmp), x_nm[:, :, :] if l == 0 else blocks(cur), acc[:, :, 0:D], ALU.add).then_inc(s_nm, 1)
                dve.wait_ge(s_m2c, (l + 1) * len(NG))
                link(dve.reduce_sum(st1[:, 0:1], h2T, axis=AX_X))
                link(dve.tensor_scalar(st1[:, 1:2], st1[:, 0:1], -1.0 / N, None, ALU.mult))
                link(dve.tensor_scalar(h2T, h2T, st1[:, 1:2], None, ALU.add))
                link(dve.tensor_tensor(fT, h2T, h2T, ALU.mult))
                dve.reduce_sum(st1[:, 2:3], fT, axis=AX_X).then_inc(s_var, 1)
                dve.wait_ge(s_sd, l + 2)
                link(dve.reciprocal(st1[:, 4:5], st1[:, 3:4]))
                link(dve.tensor_tensor(st1[:, 5:6], st1[:, 4:5], Lvec[:, 2, l:l + 1], ALU.mult))
                dve.tensor_scalar(fT, h2T, st1[:, 5:6], Lvec[:, 3, l:l + 1], ALU.mult, ALU.add).then_inc(s_bn, 1)
            dve.wait_ge(s_bk, L * len(NG))
            link(dve.tensor_tensor(blocks(tmp2), x_nm[:, :, :], blocks(cur), ALU.add))
            layernorm(L + 2, tmp2, blocks(tmp2))


_INS = ['x', 'src', 'dst', 'edge_attr_16', 'edge_attr_16_n2', 'L0_gnn_Wq', 'L0_gnn_Wang_k', 'L0_gnn_Wlin_k', 'L0_gnn_W1k',
        'L0_gnn_b1k', 'L0_gnn_W2k', 'L0_gnn_Wang_v', 'L0_gnn_Wlin_v', 'L0_gnn_W1v', 'L0_gnn_b1v', 'L0_gnn_W2v', 'L0_gnn_Wdot',
        'L0_gnn_Wout', 'L1_gnn_W1', 'L1_gnn_b1', 'L1_gnn_W2', 'L1_gnn_b2', 'L1_gnn_gamma', 'L1_gnn_beta']
_OUTS = [((3125, 128), 'float32')]


def kernel(**inputs):
    import numpy as _np
    import concourse.bacc as _bacc
    from concourse import mybir as _mybir
    from concourse.bass_utils import run_bass_kernel_spmd as _run

    nc = _bacc.Bacc("TRN2", target_bir_lowering=False, num_devices=1)
    arrays, args = {}, []
    for name in _INS:
        a = _np.ascontiguousarray(inputs[name])
        arrays[f"in_{name}_dram"] = a
        args.append(nc.dram_tensor(f"in_{name}_dram", a.shape, _mybir.dt.from_np(a.dtype), kind="ExternalInput").ap())
    for i, (shape, dtype) in enumerate(_OUTS):
        dt = _mybir.dt.from_np(_np.dtype(dtype))
        args.append(nc.dram_tensor(f"out_{i}_dram", shape, dt, kind="ExternalOutput").ap())
    gnn(nc, *args)
    r = _run(nc, [arrays], core_ids=[0])
    return r.results[0]["out_0_dram"]
```

```python
from contextlib import ExitStack

import concourse.bass as bass
from concourse import mybir

F32 = mybir.dt.float32
F16 = mybir.dt.float16
I32 = mybir.dt.int32
BF16 = mybir.dt.bfloat16
ALU = mybir.AluOpType
ACT = mybir.ActivationFunctionType
AX_X = mybir.AxisListType.X


def gnn(nc, x, src, dst, edge_attr, edge_sh, Wq, Wang_k, Wlin_k, W1k, b1k, W2k, Wang_v, Wlin_v, W1v, b1v, W2v,
        Wdot, Wout, L_W1, L_b1, L_W2, L_b2, L_gamma, L_beta, out):
    N, D = x.shape
    E = src.shape[0]
    A = edge_attr.shape[1]
    HID = W1k.shape[1]
    DK = W2k.shape[1]
    HD = Wdot.shape[0]
    H = DK // HD
    DVH = D // H
    L = L_W1.shape[0]
    P = 125
    NB = N // P
    T = E // P
    G = 4
    GE = G * P
    IT = E // (2 * GE)
    CH = 10
    CE = E // CH
    CT = T // CH
    CG = (E // GE) // CH
    CHH = CH * H
    NC = E // GE
    SK = 4
    WA = 20
    NWA = -(-N // WA)
    RA = NC + NWA - 1
    SA = 2 * NC
    QA = SA // SK
    RB = NC + NB - 1
    SB = -(-RB // 16) * 16
    QB = SB // SK
    PW = NB * WA
    GW = 500 // WA
    NV = 8
    BIG = -1.0e30
    W = D + H
    NG = [(g, min(4, NB - g)) for g in range(0, NB, 4)]
    assert N == NB * P and E == IT * 2 * GE and RA <= SA and QA <= 128 and E == CH * CE and GW * WA == 4 * P

    ctx = ExitStack()
    with ctx:
        def sb(name, shape, dt=F32):
            return ctx.enter_context(nc.sbuf_tensor(name, shape, dt))

        def sem(name):
            return ctx.enter_context(nc.semaphore(name))

        def dram(name, shape, dt=F32):
            return nc.dram_tensor(name, shape, dt, kind="Internal").ap()

        q_table = dram("q_table", (N, DK))
        v_table = dram("v_table", (E, D))
        walk_dram = dram("walk_dram", (2, 2, SA), I32)
        DUMMY = 4
        adj = dram("adj", (NWA + DUMMY, P, PW), BF16)
        adj_res = dram("adj_res", (NWA + DUMMY, P, PW), BF16)

        ident = sb("ident", [128, 128])
        iota_i = sb("iota_i", [128, P], I32)
        iota_row = sb("iota_row", [128, P])
        zero_bf = sb("zero_bf", [128, 128], BF16)
        iota_p = sb("iota_p", [128, P], BF16)
        iota_pair_i = sb("iota_pair_i", [128, PW], I32)
        iota_pair = sb("iota_pair", [128, PW], F16)
        step_i = [sb("stepA_i", [QA, SK], I32), sb("stepB_i", [QB, SK], I32)]
        chunk_i = sb("chunk_i", [1, NC], I32)
        dummy_i = sb("dummy_i", [1, SA], I32)
        ones = sb("ones", [1, 128])
        Wq_sb = sb("Wq_sb", [D, DK])
        Wlk = sb("Wlk", [D, DK])
        Wlv = sb("Wlv", [D, D])
        W1c = sb("W1c", [2 * A, 2 * HID])
        W2c = sb("W2c", [2 * HID, DK + D])
        b1c = sb("b1c", [2 * HID, 1])
        Wang_pad = sb("Wang_pad", [D, 2, 2 * A])
        WangT = sb("WangT", [2 * A, 2, D])
        Wdot_bd = sb("Wdot_bd", [DK, DK])
        Wout_sb = sb("Wout_sb", [D, D])
        LW1 = sb("LW1", [D, L, D])
        LW2 = sb("LW2", [D, L, D])
        Lvec = sb("Lvec", [D, 4, L])
        eps = sb("eps", [128, 1])
        first_dst = sb("first_dst", [1, NC], I32)
        start_row = sb("start_row", [1, 2, NC])
        step_f, c_f, w_f, wn_f, w_min, c_i, w_i = ([sb(f"{name}{k}", [q, SK], dt) for k, q in enumerate((QA, QB))]
                                                   for name, dt in (("step_f", F32), ("c_f", F32), ("w_f", F32), ("wn_f", F32),
                                                                    ("w_min", F32), ("c_i", I32), ("w_i", I32)))
        walkA = sb("walkA", [1, SA], I32)
        keep_row = sb("keep_row", [1, SA])
        junk_row = sb("junk_row", [1, SA])
        goal = sb("goal", [1, SA], I32)
        walkB = sb("walkB", [1, 2, SB], I32)
        keep = sb("keep", [P, SA])
        loA = sb("loA", [P, SA + 1, G])
        pairA = sb("pairA", [P, SA + 1, G])
        dstB = sb("dstB", [P, SB, G])
        flag_f = sb("flag_f", [1, 2])
        flag_i = sb("flag_i", [1, 2], I32)
        flag_col = sb("flag_col", [100, 1])
        x_nm = sb("x_nm", [P, NB, D])
        idx_src = sb("idx_src", [P, NC * G], I32)
        idx_dst = sb("idx_dst", [P, NC * G], I32)
        idx_slot = sb("idx_slot", [P, 2, 2 * G], I32)
        es = sb("es", [P, 2, G, 2, A])
        xg = sb("xg", [P, 2 * G, D])
        qg = sb("qg", [P, 2 * G, DK])
        rad = sb("rad", [P, 2, G, DK + D])
        kt = sb("kt", [P, 2, G, DK])
        alpha_em = sb("alpha_em", [P, T * H])
        bufA = sb("bufA", [128, CE])
        bufR = sb("bufR", [128, CE])
        bufP = sb("bufP", [128, CE + 2], BF16)
        adj_sb = [alpha_em[:, 0:GW * PW // 2].bitcast(BF16).rearrange("p (w c) -> p w c", w=GW),
                  bufA[0:P, 0:GW * PW // 2].bitcast(BF16).rearrange("p (w c) -> p w c", w=GW)]
        rest = bufA[0:P, GW * PW // 2:GW * PW // 2 + 8 * D].rearrange("p (s e) -> p s e", s=2)
        parts = bufP[0:P, 0:NB * 3 * D].rearrange("p (b w f) -> p b w f", b=NB, w=3)
        yk, yv, hidT = (bufA[:, k * 2 * GE:(k + 1) * 2 * GE].rearrange("p (q e) -> p q e", q=2) for k in range(3))
        vo = bufA[0:P, 3000:3000 + 2 * G * D].rearrange("p (q j f) -> p q j f", q=2, j=G)
        al = bufA[0:CHH, :]
        run = bufR[0:CHH, :]
        pen = bufP[0:CHH, 0:CE + 1]
        dst_s = sb("dst_s", [CHH, 1], I32)
        tmp = bufA[0:P, 0:NB * D]
        tmp2 = bufA[0:P, 2 * NB * D:3 * NB * D]
        fT = bufR[:, 0:N]
        h1T = bufR[:, N:2 * N]
        h2T = bufR[:, 2 * N:3 * N]
        ohl = bufR[0:P, 0:500].bitcast(BF16).rearrange("p (s j c) -> p s j c", s=2, j=G)
        ohp = bufR[0:P, 500:2500].bitcast(BF16).rearrange("p (s j c) -> p s j c", s=2, j=G)
        cnt = bufR[0:P, 2500:3500].rearrange("p (s c) -> p s c", s=2)
        cnt_bf = bufR[0:P, 3500:4000].bitcast(BF16).rearrange("p (s c) -> p s c", s=2)
        cnt_res = bufR[0:P, 4000:4500].bitcast(BF16).rearrange("p (s c) -> p s c", s=2)
        sT = bufR[0:2 * A, 4500:5500].rearrange("p (q e) -> p q e", q=2)
        xT = bufR[:, 5500:6500].rearrange("p (q e) -> p q e", q=2)
        relaid = bufR[0:P, 0:T * H]
        gs = bufA[0:P, 0:4 * G * W].rearrange("p (s j w) -> p s j w", s=4, j=G)
        oh = bufA[0:P, 4 * G * W:4 * G * (W + P)].rearrange("p (s j w) -> p s j w", s=4, j=G)
        v_ring = bufR[0:P, 0:NV * G * D].rearrange("p (u e) -> p u e", u=NV)
        qn = bufR[0:P, 2 * N:2 * N + NB * DK]
        acc = bufP[0:P, 0:2 * NB * W].bitcast(F32).rearrange("p (b w) -> p b w", b=NB)
        ends = sb("ends", [CHH, 4])
        carry = sb("carry", [CHH, 2])
        row_end = sb("row_end", [1, 4, CHH])
        row_c = sb("row_c", [1, 2, CHH])
        row_E = sb("row_E", [1, 2, CHH])
        st25 = sb("st25", [P, 4, NB])
        rden = sb("rden", [P, NB * H])
        st1 = sb("st1", [128, 8])
        bn6 = sb("bn6", [128, len(NG), 6])
        bn2 = sb("bn2", [128, 2])

        bank = [ctx.enter_context(nc.psum_tensor(f"bank{i}", [128, 512], F32)) for i in range(8)]

        def rows(buf, n, k):
            return buf[0:n, k * SK * GE:(k + 1) * SK * GE].rearrange("s (k e) -> s k e", k=SK)

        srcR, dstR, hiA, dlA, okA = (rows(bufA, QA, k) for k in range(5))
        dstRB = rows(alpha_em, QB, 0)
        startB = alpha_em[0:QA, 2000:2000 + 2 * NC].rearrange("p (w c) -> p w c", w=2)
        junk = alpha_em[0:QA, 2400:2400 + NC]
        deg0, deg1 = (alpha_em[0:100, 3000 + k * 1000:4000 + k * 1000] for k in range(2))

        s_ident0, s_ident, s_iota = sem("s_ident0"), sem("s_ident"), sem("s_iota")
        s_zero = sem("s_zero")
        s_w, s_w2 = sem("s_w"), sem("s_w2")
        s_x, s_fd = sem("s_x"), sem("s_fd")
        s_d, s_a, s_chainA = sem("s_d"), sem("s_a"), sem("s_chainA")
        s_start, s_startB, s_steps, s_rows = sem("s_start"), sem("s_startB"), sem("s_steps"), sem("s_rows")
        s_rowsF, s_tabT, s_tab, s_walkst, s_walk = (sem("s_rowsF"), sem("s_tabT"), sem("s_tab"), sem("s_walkst"),
                                                    sem("s_walk"))
        s_wangT, s_wang = sem("s_wangT"), sem("s_wang")
        s_xnT, s_xn = sem("s_xnT"), sem("s_xn")
        s_qT, s_qTc, s_qn, s_qnc, s_qst = sem("s_qT"), sem("s_qTc"), sem("s_qn"), sem("s_qnc"), sem("s_qst")
        s_idx = [sem(f"s_idx{q}") for q in range(2)]
        s_es = [sem(f"s_es{q}") for q in range(2)]
        s_gx = [sem(f"s_gx{q}") for q in range(2)]
        s_gq = [sem(f"s_gq{q}") for q in range(2)]
        s_vst = [sem(f"s_vst{q}") for q in range(2)]
        s_T, s_gk, s_gv, s_hid, s_E = sem("s_T"), sem("s_gk"), sem("s_gv"), sem("s_hid"), sem("s_E")
        s_sTc, s_xTc, s_hidc, s_radc = sem("s_sTc"), sem("s_xTc"), sem("s_hidc"), sem("s_radc")
        s_y, s_v, s_t1, s_t2, s_al, s_vfree = (sem("s_y"), sem("s_v"), sem("s_t1"), sem("s_t2"), sem("s_al"),
                                               sem("s_vfree"))
        s_cnt0 = sem("s_cnt0")
        s_afree, s_st = sem("s_afree"), sem("s_st")
        s_pad, s_relaid = sem("s_pad"), sem("s_relaid")
        s_halo, s_dsts, s_alT, s_alc = sem("s_halo"), sem("s_dsts"), sem("s_alT"), sem("s_alc")
        s_endsd, s_endT, s_carT, s_rowE = sem("s_endsd"), sem("s_endT"), sem("s_carT"), sem("s_rowE")
        s_sub, s_exp, s_eT, s_eTc = sem("s_sub"), sem("s_exp"), sem("s_eT"), sem("s_eTc")
        s_vld = [sem(f"s_vld{u}") for u in range(NV)]
        s_cp = sem("s_cp")
        s_oh, s_sc, s_mm, s_acc, s_ready = sem("s_oh"), sem("s_sc"), sem("s_mm"), sem("s_acc"), sem("s_ready")
        s_deg0, s_deg, s_degT, s_flag, s_flagT = sem("s_deg0"), sem("s_deg"), sem("s_degT"), sem("s_flag"), sem("s_flagT")
        s_keepr, s_keepT, s_goal = sem("s_keepr"), sem("s_keepT"), sem("s_goal")
        s_ohA, s_bm, s_cnt, s_cbf, s_cres = sem("s_ohA"), sem("s_bm"), sem("s_cnt"), sem("s_cbf"), sem("s_cres")
        s_adst = [sem(f"s_adst{k}") for k in range(2)]
        s_arst = [sem(f"s_arst{k}") for k in range(2)]
        s_ald = [sem(f"s_ald{k}") for k in range(2)]
        s_main, s_ares, s_agg, s_hT = sem("s_main"), sem("s_ares"), sem("s_agg"), sem("s_hT")
        s_hi, s_r1, s_mid, s_parts, s_xfT = sem("s_hi"), sem("s_r1"), sem("s_mid"), sem("s_parts"), sem("s_xfT")
        s_nm, s_nfT, s_nfc = sem("s_nm"), sem("s_nfT"), sem("s_nfc")
        s_m1, s_m1c, s_m2, s_m2c = sem("s_m1"), sem("s_m1c"), sem("s_m2"), sem("s_m2c")
        s_var, s_sd, s_bn, s_bkT, s_bk, s_xst = (sem("s_var"), sem("s_sd"), sem("s_bn"), sem("s_bkT"), sem("s_bk"),
                                                 sem("s_xst"))
        s_out = sem("s_out")

        def done(g):
            return g + 3

        def one_ago(g):
            return g + 2

        def two_ago(g):
            return g + 1

        def pair_bank(b):
            return bank[5 + 2 * b][0:P, :].rearrange("p (j c) -> p j c", j=2)

        NA = [(d * GW, min(GW, NWA - d * GW)) for d in range(-(-NWA // GW))]
        NGRP = len(NG)
        v_c = v_table.rearrange("(c p j) f -> c p (j f)", p=P, j=G)
        assert len(NA) == NGRP
        LG = [(l, d) for l in range(L) for d in range(NGRP)]

        block = ctx.enter_context(nc.Block())

        @block.sync
        def _(sp):
            with nc.allow_non_contiguous_dma(reason="one value for each chunk"):
                sp.dma_start(first_dst[:, :], dst.rearrange("(o c e) -> o c e", o=1, e=GE)[:, :, 0]).then_inc(s_fd, 16)
            sp.wait_ge(s_deg0, 1)
            sp.dma_start(deg0.bitcast(I32), dst.rearrange("(p e) -> p e", p=100)).then_inc(s_deg, 16)
            sp.dma_start(deg1.bitcast(I32)[0:99, :], dst[256:256 + 99000].rearrange("(p e) -> p e", p=99)).then_inc(s_deg, 16)
            sp.dma_start(deg1.bitcast(I32)[99:100, 0:E - 99256], dst[99256:E].rearrange("(p e) -> p e", p=1)).then_inc(s_deg, 16)
            sp.dma_start(x_nm[:, :, :], x.rearrange("(b p) f -> p b f", p=P)).then_inc(s_x, 16)
            sp.wait_ge(s_zero, 1)
            loads = [(Wq_sb[:, :], Wq), (Wlk[:, :], Wlin_k), (Wlv[:, :], Wlin_v),
                     (W1c[0:A, 0:HID], W1k), (W1c[0:A, HID:], W1v), (W2c[0:HID, 0:DK], W2k), (W2c[HID:, DK:], W2v),
                     (b1c[0:HID, :], b1k.rearrange("(a b) -> a b", b=1)),
                     (b1c[HID:, :], b1v.rearrange("(a b) -> a b", b=1)),
                     (Wang_pad[:, 0, A:], Wang_k), (Wang_pad[:, 1, A:], Wang_v)]
            loads += [(Wdot_bd[h * HD:(h + 1) * HD, h * HD:(h + 1) * HD], Wdot) for h in range(H)]
            for a, b in loads:
                sp.dma_start(a, b).then_inc(s_w, 16)
            sp.wait_ge(s_steps, 1)
            with nc.allow_non_contiguous_dma(reason="two numbers for each step"):
                for k, q in enumerate((QA, QB)):
                    for w, tab in enumerate((c_i[k], w_i[k])):
                        sp.dma_start(walk_dram[k, w, 0:SK * q].rearrange("(k q) -> q k", k=SK), tab[:, :]).then_inc(s_walkst, 16)
                sp.wait_ge(s_walkst, 64)
                sp.dma_start(walkA[:, :], walk_dram[0, 1:2, :]).then_inc(s_walk, 16)
                sp.dma_start(walkB[:, 0, :], walk_dram[1, 0:1, 0:SB]).then_inc(s_walk, 16)
                sp.dma_start(walkB[:, 1, :], walk_dram[1, 1:2, 0:SB]).then_inc(s_walk, 16)
                sp.dma_start(Wout_sb[:, :], Wout).then_inc(s_w2, 16)
                sp.dma_start(LW1[:, :, :], L_W1.rearrange("l a b -> a l b")).then_inc(s_w2, 16)
                sp.dma_start(LW2[:, :, :], L_W2.rearrange("l a b -> a l b")).then_inc(s_w2, 16)
                for k, vec in enumerate((L_b1, L_b2, L_gamma, L_beta)):
                    sp.dma_start(Lvec[:, k, :], vec.rearrange("l a -> a l")).then_inc(s_w2, 16)
            sp.wait_ge(s_qnc, len(range(0, NB, 8)))
            sp.dma_start(q_table.rearrange("(b p) k -> p b k", p=P),
                         qn[:, :].rearrange("p (b k) -> p b k", b=NB)).then_inc(s_qst, 16)

            src_v = src.rearrange("(i q p j) -> i q p j", p=P, q=2, j=G)
            dst_v = dst.rearrange("(i q p j) -> i q p j", p=P, q=2, j=G)
            ea_v = edge_attr.rearrange("(i q p j) a -> i q p j a", p=P, q=2, j=G)
            sh_v = edge_sh.rearrange("(i q p j) a -> i q p j a", p=P, q=2, j=G)
            v_v = v_table.rearrange("(i q p j) f -> i q p (j f)", p=P, q=2, j=G)

            def one(view, i):
                return view[bass.ds(i, 1)] if not isinstance(i, int) else view[i:i + 1]

            def load_idx(i, q):
                at = bass.ds((2 * i + q) * G, G)
                sp.dma_start(idx_src[:, at], one(src_v, i)[0, q]).then_inc(s_idx[q], 16)
                sp.dma_start(idx_dst[:, at], one(dst_v, i)[0, q]).then_inc(s_idx[q], 16)

            def load_es(i, q):
                sp.dma_start(es[:, q, :, 0, :], one(ea_v, i)[0, q]).then_inc(s_es[q], 16)
                sp.dma_start(es[:, q, :, 1, :], one(sh_v, i)[0, q]).then_inc(s_es[q], 16)

            def store(i, q):
                sp.wait_ge(s_v, 2 * i + q + 1)
                sp.sem_inc(s_pad, 1)
                sp.dma_start(one(v_v, i)[0, q], vo[:, q, :, :].rearrange("p j f -> p (j f)")).then_inc(s_vst[q], 16)

            def stored(i):
                for q in range(2):
                    sp.wait_ge(s_vst[q], 16 * i + 16)
                    sp.sem_inc(s_vfree, 1)

            sp.sem_inc(s_vfree, 2)
            for q in range(2):
                load_idx(0, q)
                load_es(0, q)
            with sp.Fori(0, IT - 1) as i:
                for q in range(2):
                    sp.wait_ge(s_idx[q], 32 * i + 32)
                    sp.sem_inc(s_pad, 1)
                    load_idx(i + 1, q)
                    sp.wait_ge(s_T, done(2 * i + q))
                    sp.sem_inc(s_pad, 1)
                    load_es(i + 1, q)
                    store(i, q)
                stored(i)
            for q in range(2):
                store(IT - 1, q)
            stored(IT - 1)

            sp.wait_ge(s_halo, 1)
            sp.wait_ge(s_al, 2 * IT + 2)
            dview = bufR[0:CHH, :].bitcast(I32)
            for c in range(CH):
                sp.dma_start(dview[c * H:(c + 1) * H, :], dst[c * CE:(c + 1) * CE].partition_broadcast(H)).then_inc(s_dsts, 16)
                if c < CH - 1:
                    sp.dma_start(dst_s[c * H:(c + 1) * H, :], dst[(c + 1) * CE:(c + 1) * CE + 1].partition_broadcast(H)).then_inc(s_dsts, 16)

            sp.wait_ge(s_flag, 1)
            over = sp.value_load(flag_i[0:1, 0:1], min_val=0, max_val=1)
            sp.wait_ge(s_sub, 1)
            with sp.Fori(0, SB // NV) as i:
                for u in range(0, NV, 2):
                    c = sp.value_load(walkB[0:1, 0, bass.ds(NV * i + u, 1)], min_val=0, max_val=NC - 1)
                    sp.wait_ge(s_sc, NV * i + u + 1)
                    sp.sem_inc(s_pad, 1)
                    sp.dma_start(v_ring[:, u, :], v_c[bass.ds(c, 1)][0]).then_inc(s_vld[u], 16)

            def residue(n):
                w0, nw = NA[n % NGRP]
                with sp.If(over):
                    sp.wait_ge(s_main, n + 1)
                    sp.dma_start(adj_sb[n % 2][:, 0:nw, :], adj_res[w0:w0 + nw].rearrange("w p c -> p w c")).then_inc(s_ares, 16)
                sp.sem_inc(s_pad, 1)

            for n, (l, d) in enumerate(LG):
                w0, nw = NA[d]
                if n >= 2:
                    sp.wait_ge(s_agg, n - 1)
                elif n == 0:
                    sp.wait_ge(s_acc, SB + 4)
                else:
                    sp.wait_ge(s_ready, 1)
                sp.dma_start(adj_sb[n % 2][:, 0:nw, :], adj[w0:w0 + nw].rearrange("w p c -> p w c")).then_inc(s_ald[n % 2], 16)
                if n >= 1:
                    residue(n - 1)
            residue(len(LG) - 1)
            sp.wait_ge(s_ready, 2)
            sp.dma_start(out.rearrange("(b p) f -> p b f", p=P),
                         tmp2.rearrange("p (b f) -> p b f", b=NB)).then_inc(s_out, 16)
            sp.wait_ge(s_out, 16)

        @block.gpsimd
        def _(pool):
            pool.memset(ident[:, :], 0.0).then_inc(s_ident0, 1)
            pool.wait_ge(s_ident0, 1)
            pool.affine_select(out=ident[:, :], in_=ident[:, :], compare_op=ALU.not_equal, fill=1.0, base=0,
                               pattern=[[-1, 128]], channel_multiplier=1).then_inc(s_ident, 1)
            pool.iota(iota_i[:, :], pattern=[[1, P]], base=0, channel_multiplier=0).then_inc(s_iota, 1)
            pool.iota(iota_pair_i[:, :], pattern=[[1, PW]], base=0, channel_multiplier=0).then_inc(s_iota, 1)
            for k, q in enumerate((QA, QB)):
                pool.iota(step_i[k][:, :], pattern=[[q, SK]], base=0, channel_multiplier=1).then_inc(s_iota, 1)
            pool.iota(chunk_i[:, :], pattern=[[1, NC]], base=0, channel_multiplier=0).then_inc(s_iota, 1)
            pool.iota(dummy_i[:, :], pattern=[[0, SA // DUMMY], [1, DUMMY]], base=NWA, channel_multiplier=0).then_inc(s_iota, 1)
            pool.wait_ge(s_steps, 1)
            for rws, table, ci in ((srcR, src, c_i[0]), (dstR, dst, c_i[0]), (dstRB, dst, c_i[1])):
                for k in range(SK):
                    pool.indirect_dma_start(rws[:, k, :].bitcast(I32), None, table.rearrange("(c e) -> c e", e=GE),
                                            bass.IndirectOffsetOnAxis(ap=ci[:, k:k + 1], axis=0)).then_inc(s_rows, 16)
            pool.wait_ge(s_qst, 16)
            def gather_x(i, q, g):
                pool.wait_ge(s_idx[q], 32 * i + 32)
                pool.wait_ge(s_T, two_ago(g))
                pool.tensor_copy(idx_slot[:, q, 0:G], idx_src[:, bass.ds(g * G, G)]).then_inc(s_cp, 1)
                pool.wait_ge(s_cp, 2 * g + 1 if isinstance(g, int) and g == 0 else 2 * g)
                pool.sem_inc(s_pad, 1)
                for j in range(G):
                    pool.indirect_dma_start(xg[:, q * G + j, :], None, x,
                                            bass.IndirectOffsetOnAxis(ap=idx_slot[:, q, j:j + 1], axis=0)).then_inc(s_gx[q], 16)

            def gather_q(i, q, g, last=False):
                pool.wait_ge(s_al, two_ago(g))
                pool.tensor_copy(idx_slot[:, q, G:2 * G], idx_dst[:, bass.ds(g * G, G)]).then_inc(s_cp, 1)
                pool.wait_ge(s_cp, 2 * g + (2 if last else 3))
                pool.sem_inc(s_pad, 1)
                for j in range(G):
                    pool.indirect_dma_start(qg[:, q * G + j, :], None, q_table,
                                            bass.IndirectOffsetOnAxis(ap=idx_slot[:, q, G + j:G + j + 1], axis=0)).then_inc(s_gq[q], 16)

            gather_x(0, 0, 0)
            with pool.Fori(0, IT - 1) as i:
                for q in range(2):
                    gather_x(i + q, 1 - q, 2 * i + q + 1)
                    gather_q(i, q, 2 * i + q)
            gather_x(IT - 1, 1, NC - 1)
            gather_q(IT - 1, 0, NC - 2)
            gather_q(IT - 1, 1, NC - 1, True)
            pool.sem_inc(s_sc, NV)
            pool.wait_ge(s_eTc, CG // 2 + CG)
            with pool.Fori(0, SB // NV) as i:
                cs = [pool.value_load(walkB[0:1, 0, bass.ds(NV * i + u, 1)], min_val=0, max_val=NC - 1) for u in range(NV)]
                for u in range(NV):
                    pool.wait_ge(s_mm, NV * i + u + 1)
                    pool.wait_ge(s_vld[u], 16 * i + 16)
                    e = alpha_em[:, bass.ds(cs[u] * (G * H), G * H)].rearrange("p (j h) -> p j h", j=G)
                    pool.tensor_copy(gs[:, u % 4, :, D:W], e)
                    pool.tensor_tensor(gs[:, u % 4, :, 0:D].rearrange("p j (h v) -> p j h v", h=H),
                                       v_ring[:, u, :].rearrange("p (j h v) -> p j h v", j=G, h=H),
                                       e.unsqueeze(3).to_broadcast([P, G, H, D // H]), ALU.mult).then_inc(s_sc, 1)

        @block.scalar
        def _(act):
            for s in (s_sTc, s_xTc, s_hidc, s_radc):
                act.sem_inc(s, 2)
            act.wait_ge(s_wangT, 1)
            act.copy(WangT[:, :, :], bank[7][0:2 * A, 0:2 * D].rearrange("p (w f) -> p w f", w=2)).then_inc(s_wang, 1)
            for k, (g, m) in enumerate(NG):
                act.wait_ge(s_xnT, k + 1)
                act.copy(fT[:, g * P:(g + m) * P], bank[k % 2][:, 0:m * P]).then_inc(s_xn, 1)
            for k, (g, m) in enumerate(NG):
                act.wait_ge(s_qT, k + 1)
                act.copy(h1T[0:DK, g * P:(g + m) * P], bank[2 + k % 2][0:DK, 0:m * P]).then_inc(s_qTc, 1)
            def copies(g, q):
                act.wait_ge(s_T, done(g))
                act.wait_ge(s_hid, two_ago(g))
                act.copy(sT[:, q, :], bank[1][0:2 * A, 0:GE]).then_inc(s_sTc, 1)
                act.wait_ge(s_y, two_ago(g))
                act.copy(xT[:, q, :], bank[0][:, 0:GE]).then_inc(s_xTc, 1)

            def relu(g, q):
                act.wait_ge(s_hid, done(g))
                act.wait_ge(s_E, two_ago(g))
                act.activation(hidT[:, q, :], bank[1][:, 0:GE], ACT.Relu, bias=b1c[:, 0:1]).then_inc(s_hidc, 1)

            def rads(g, q):
                act.wait_ge(s_E, done(g))
                act.wait_ge(s_al, two_ago(g))
                for b in range(2):
                    r = act.copy(rad[:, q, 2 * b:2 * b + 2, :], pair_bank(b)[:, :, 0:DK + D])
                r.then_inc(s_radc, 1)

            over = {}

            def put(n, k):
                w = act.value_load(goal[0:1, bass.ds(n, 1)], min_val=0, max_val=NWA + DUMMY - 1)
                act.wait_ge(s_cbf, n + 2)
                act.sem_inc(s_pad, 1)
                act.dma_start(adj[bass.ds(w, 1)][0], cnt_bf[:, k, :]).then_inc(s_adst[k], 16)
                with act.If(over["reg"]):
                    act.wait_ge(s_cres, n + 1)
                    act.sem_inc(s_pad, 1)
                    act.dma_start(adj_res[bass.ds(w, 1)][0], cnt_res[:, k, :]).then_inc(s_arst[k], 16)
                act.sem_inc(s_pad, 1)

            act.wait_ge(s_goal, 1)
            act.wait_ge(s_flag, 1)
            over["reg"] = act.value_load(flag_i[0:1, 0:1], min_val=0, max_val=1)
            act.sem_inc(s_cbf, 1)
            act.wait_ge(s_cnt0, 1)
            for k in range(2):
                act.dma_start(adj[NWA + 2 + k], cnt_bf[:, k, :]).then_inc(s_adst[k], 16)
                act.dma_start(adj_res[NWA + 2 + k], cnt_res[:, k, :]).then_inc(s_arst[k], 16)

            def slot(i, q, first, last):
                g = 2 * i + q
                relu(g, q)
                if not first:
                    narrow_put(2 * g - 1, 1, g - 1)
                if not last:
                    copies(g + 1, 1 - q)
                narrow_put(2 * g, 0, g)
                rads(g, q)

            def narrow_put(n, k, m):
                act.wait_ge(s_cnt, n + 2)
                act.wait_ge(s_adst[k], 16 * m + 16)
                act.copy(cnt_bf[:, k, :], cnt[:, k, :]).then_inc(s_cbf, 1)
                put(n, k)

            copies(0, 0)
            slot(0, 0, True, False)
            slot(0, 1, False, False)
            with act.Fori(1, IT - 1) as i:
                for q in range(2):
                    slot(i, q, False, False)
            slot(IT - 1, 0, False, False)
            slot(IT - 1, 1, False, True)
            narrow_put(SA - 1, 1, NC - 1)
            for k in range(2):
                act.wait_ge(s_adst[k], 16 * NC + 16)
                act.wait_ge(s_arst[k], 16)
            with act.If(over["reg"]):
                for k in range(2):
                    act.wait_ge(s_arst[k], 16 * NC + 16)
                act.sem_inc(s_pad, 1)
            act.sem_inc(s_afree, 1)

            for k in range(0, CG):
                if k % 2 == 1:
                    act.wait_ge(s_alT, k + 1)
                    act.copy(al[:, k * GE:(k + 1) * GE].rearrange("c (p j) -> c j p", j=G),
                             bank[k % 2][0:CHH, 0:GE].rearrange("c (j p) -> c j p", j=G)).then_inc(s_alc, 1)
            act.wait_ge(s_sub, 1)
            act.activation(al, al, ACT.Exp).then_inc(s_exp, 1)
            with act.Fori(0, SB // NV) as i:
                for u in range(1, NV, 2):
                    c = act.value_load(walkB[0:1, 0, bass.ds(NV * i + u, 1)], min_val=0, max_val=NC - 1)
                    act.wait_ge(s_sc, NV * i + u + 1)
                    act.sem_inc(s_pad, 1)
                    act.dma_start(v_ring[:, u, :], v_c[bass.ds(c, 1)][0]).then_inc(s_vld[u], 16)
            base = {"nf": 0}

            def features():
                for k, (g, m) in enumerate(NG):
                    act.wait_ge(s_nfT, base["nf"] + k + 1)
                    act.copy(fT[:, g * P:(g + m) * P], bank[k % 2][:, 0:m * P]).then_inc(s_nfc, 1)
                base["nf"] += len(NG)

            def root(n, sd, var, scale):
                act.wait_ge(s_var, n)
                act.activation(sd, var, ACT.Sqrt, bias=eps[0:sd.shape[0], 0:1], scale=scale).then_inc(s_sd, 1)

            features()
            root(1, st25[:, 2, :], st25[:, 1, :], 1.0 / D)
            for k, (g, m) in enumerate(NG):
                act.wait_ge(s_nfT, NGRP + k + 1)
                act.copy(fT[:, g * P:(g + m) * P], bank[k % 2][:, 0:m * P]).then_inc(s_nfc, 1)

            def split(n, g, m, of):
                act.copy(parts[:, g:g + m, 0, :], of).then_inc(s_hi, 1)
                act.wait_ge(s_r1, n + 1)
                act.copy(parts[:, g:g + m, 1, :], rest[:, n % 2, 0:m * D].rearrange("p (b f) -> p b f", b=m)).then_inc(s_mid, 1)

            for k, (g, m) in enumerate(NG):
                act.wait_ge(s_ready, 1)
                split(k, g, m, x_nm[:, g:g + m, :])
            for l in range(L):
                for k, (g, m) in enumerate(NG):
                    act.wait_ge(s_m1, l * NGRP + k + 1)
                    act.activation(h1T[:, g * P:(g + m) * P], bank[2 + k % 2][:, 0:m * P], ACT.Relu,
                                   bias=Lvec[:, 0, l:l + 1]).then_inc(s_m1c, 1)
                    act.wait_ge(s_m2, l * NGRP + k + 1)
                    act.activation(h2T[:, g * P:(g + m) * P], bank[4 + k % 2][:, 0:m * P], ACT.Relu,
                                   bias=Lvec[:, 1, l:l + 1]).then_inc(s_m2c, 1)
                root(l + 2, st1[:, 3:4], bn2[:, 1:2], 1.0)
                if l < L - 1:
                    for k, (g, m) in enumerate(NG):
                        act.wait_ge(s_bkT, l * NGRP + k + 1)
                        split((l + 1) * NGRP + k, g, m, bank[6 + k % 2][0:P, 0:m * D].rearrange("p (b f) -> p b f", b=m))
            root(L + 2, st25[:, 2, :], st25[:, 1, :], 1.0 / D)

        @block.tensor
        def _(pe):
            for s in (s_T, s_hid, s_E):
                pe.sem_inc(s, 2)
            pe.sem_inc(s_mm, 4)
            pe.sem_inc(s_bm, 2)
            pe.wait_ge(s_ident, 1)
            pe.wait_ge(s_start, 1)
            pe.matmul(bank[5][0:QA, 0:2 * NC], lhsT=ones[:, 0:QA], rhs=start_row[:, :, :].rearrange("o w c -> o (w c)"),
                      start=True, stop=True).then_inc(s_startB, 1)
            pe.wait_ge(s_degT, 1)
            pe.transpose(bank[6][0:1, 0:100], flag_col[:, :], ident[0:100, 0:100]).then_inc(s_flagT, 1)
            pe.wait_ge(s_w, 16 * (11 + H))
            for w in range(2):
                mm = pe.transpose(bank[7][0:2 * A, w * D:(w + 1) * D], Wang_pad[:, w, :], ident[:, :])
            mm.then_inc(s_wangT, 1)
            pe.wait_ge(s_x, 16)
            for k, (g, m) in enumerate(NG):
                if k >= 2:
                    pe.wait_ge(s_xn, k - 1)
                for b in range(m):
                    mm = pe.transpose(bank[k % 2][:, b * P:(b + 1) * P], x_nm[:, g + b, :], ident[0:P, 0:P])
                mm.then_inc(s_xnT, 1)
            for k, (g, m) in enumerate(NG):
                pe.wait_ge(s_xn, k + 1)
                if k >= 2:
                    pe.wait_ge(s_qTc, k - 1)
                pe.matmul(bank[2 + k % 2][0:DK, 0:m * P], lhsT=Wq_sb[:, :], rhs=fT[:, g * P:(g + m) * P],
                          start=True, stop=True).then_inc(s_qT, 1)
            pe.wait_ge(s_qTc, len(NG))
            for k, g in enumerate(range(0, NB, 8)):
                if k >= 1:
                    pe.wait_ge(s_qnc, k)
                for b in range(g, min(g + 8, NB)):
                    mm = pe.matmul(bank[4][0:P, (b - g) * DK:(b - g + 1) * DK], lhsT=h1T[0:DK, b * P:(b + 1) * P],
                                   rhs=Wdot_bd[:, :], start=True, stop=True)
                mm.then_inc(s_qn, 1)
            pe.wait_ge(s_wang, 1)
            n = 0
            for tab, q in ((dlA, QA), (srcR, QA), (dstRB, QB)):
                pe.wait_ge(s_rowsF, 1 if q == QA else 2)
                for k in range(SK):
                    if n >= 2:
                        pe.wait_ge(s_tab, n - 1)
                    for j in range(G):
                        mm = pe.transpose(bank[6 + n % 2][0:P, j * q:(j + 1) * q], tab[:, k, j:GE:G], ident[0:q, 0:q])
                    mm.then_inc(s_tabT, 1)
                    n += 1
            pe.wait_ge(s_tab, 3 * SK)
            pe.wait_ge(s_keepr, 1)
            pe.matmul(bank[6][0:P, 0:SA], lhsT=ones[:, 0:P], rhs=keep_row[:, :], start=True, stop=True).then_inc(s_keepT, 1)
            pe.wait_ge(s_goal, 1)
            def turn(i, q, g):
                pe.wait_ge(s_gx[q], 16 * G * i + 16 * G)
                pe.wait_ge(s_es[q], 32 * i + 32)
                pe.wait_ge(s_xTc, one_ago(g))
                pe.wait_ge(s_hidc, one_ago(g))
                for j in range(G):
                    pe.transpose(bank[1][0:2 * A, j * P:(j + 1) * P], es[:, q, j, :, :].rearrange("p w a -> p (w a)"),
                                 ident[0:P, 0:P])
                for j in range(G):
                    mm = pe.transpose(bank[0][:, j * P:(j + 1) * P], xg[:, q * G + j, :], ident[0:P, 0:P])
                mm.then_inc(s_T, 1)

            def features(q, g):
                pe.wait_ge(s_sTc, done(g))
                pe.wait_ge(s_y, one_ago(g))
                for w in range(2):
                    pe.matmul(bank[2 + w][:, 0:GE], lhsT=WangT[:, w, :], rhs=sT[:, q, :], start=True, stop=True)
                pe.wait_ge(s_hidc, one_ago(g))
                pe.matmul(bank[1][:, 0:GE], lhsT=W1c[:, :], rhs=sT[:, q, :], start=True, stop=True).then_inc(s_hid, 1)

            def edges(q, g):
                pe.wait_ge(s_y, done(g))
                pe.wait_ge(s_hidc, done(g))
                pe.wait_ge(s_al, one_ago(g))
                pe.wait_ge(s_radc, one_ago(g))
                for j in range(G):
                    e = slice(j * P, (j + 1) * P)
                    pe.matmul(pair_bank(j // 2)[:, j % 2, 0:DK + D], lhsT=hidT[:, q, e], rhs=W2c[:, :], start=True, stop=True)
                    pe.matmul(pair_bank(j // 2)[:, j % 2, DK + D:], lhsT=yk[:, q, e], rhs=Wlk[:, :], start=True, stop=True)
                    mm = pe.matmul(bank[6][0:P, j * D:(j + 1) * D], lhsT=yv[:, q, e], rhs=Wlv[:, :], start=True, stop=True)
                mm.then_inc(s_E, 1)

            def count(n, k):
                pe.wait_ge(s_ohA, n + 1)
                pe.wait_ge(s_cnt, n + 1)
                for j in range(G):
                    mm = pe.matmul(bank[4][0:P, 0:PW], lhsT=ohl[:, k, j, :], rhs=ohp[:, k, j, :], start=(j == 0), stop=(j == G - 1))
                mm.then_inc(s_bm, 1)

            def slot(i, q, last):
                g = 2 * i + q
                features(q, g)
                count(2 * g, 0)
                if not last:
                    turn(i + q, 1 - q, g + 1)
                edges(q, g)
                count(2 * g + 1, 1)

            turn(0, 0, 0)
            with pe.Fori(0, IT - 1) as i:
                for q in range(2):
                    slot(i, q, False)
            slot(IT - 1, 0, False)
            slot(IT - 1, 1, True)

            pe.wait_ge(s_relaid, 1)
            for k in range(CG):
                if k >= 2:
                    pe.wait_ge(s_alc if k % 2 else s_eTc, k // 2)
                for j in range(G):
                    mm = pe.transpose(bank[k % 2][0:CHH, j * P:(j + 1) * P], relaid[:, (k * G + j) * CHH:(k * G + j + 1) * CHH], ident[0:P, 0:P])
                mm.then_inc(s_alT, 1)
            pe.wait_ge(s_endsd, 1)
            for w in range(4):
                mm = pe.transpose(bank[2][0:1, w * CHH:(w + 1) * CHH], ends[:, w:w + 1], ident[0:CHH, 0:CHH])
            mm.then_inc(s_endT, 1)
            pe.wait_ge(s_rowE, 1)
            for w in range(2):
                mm = pe.matmul(bank[3][0:CHH, w:w + 1], lhsT=row_c[:, w, :], rhs=ones[:, 0:1], start=True, stop=True)
            mm.then_inc(s_carT, 1)
            pe.wait_ge(s_exp, 1)
            for k in range(CG):
                if k >= 2:
                    pe.wait_ge(s_eTc, CG // 2 + k - 1)
                for j in range(G):
                    mm = pe.transpose(bank[4 + k % 2][0:P, j * CHH:(j + 1) * CHH], al[:, k * GE + j:(k + 1) * GE:G], ident[0:CHH, 0:CHH])
                mm.then_inc(s_eT, 1)
            with pe.Fori(0, SB // 4) as i:
                for u in range(4):
                    st = 4 * i + u
                    pe.wait_ge(s_oh, st + 1)
                    pe.wait_ge(s_sc, st + NV + 1)
                    pe.wait_ge(s_acc, st + 1)
                    for j in range(G):
                        mm = pe.matmul(bank[u][0:P, 0:W], lhsT=oh[:, u, j, :], rhs=gs[:, u, j, :], start=(j == 0), stop=(j == G - 1))
                    mm.then_inc(s_mm, 1)

            base = {"nf": 0}

            def transposed(k0):
                pe.wait_ge(s_nm, k0)
                for k, (g, m) in enumerate(NG):
                    if k >= 2:
                        pe.wait_ge(s_nfc, base["nf"] + k - 1)
                    for b in range(m):
                        mm = pe.transpose(bank[k % 2][:, b * P:(b + 1) * P], tmp[:, (g + b) * D:(g + b + 1) * D], ident[0:P, 0:P])
                    mm.then_inc(s_nfT, 1)
                base["nf"] += len(NG)
                pe.wait_ge(s_nfc, base["nf"])

            transposed(1)
            pe.wait_ge(s_w2, 16 * 7)
            for k, (g, m) in enumerate(NG):
                if k >= 2:
                    pe.wait_ge(s_bn, k - 1)
                for b in range(m):
                    mm = pe.matmul(bank[2 + k % 2][0:P, b * D:(b + 1) * D], lhsT=fT[:, (g + b) * P:(g + b + 1) * P], rhs=Wout_sb[:, :],
                                   start=True, stop=True)
                mm.then_inc(s_qn, 1)
            pe.wait_ge(s_ready, 1)
            for k, (g, m) in enumerate(NG):
                if k >= 2:
                    pe.wait_ge(s_nfc, NGRP + k - 1)
                for b in range(m):
                    mm = pe.transpose(bank[k % 2][:, b * P:(b + 1) * P], x_nm[:, g + b, :], ident[0:P, 0:P])
                mm.then_inc(s_nfT, 1)
            pe.wait_ge(s_nfc, 2 * NGRP)
            pe.wait_ge(s_flag, 1)
            over = pe.value_load(flag_i[0:1, 0:1], min_val=0, max_val=1)

            def products(n, first):
                d = n % NGRP
                o = bank[n % 2][:, 0:NA[d][1] * WA]
                cols = adj_sb[n % 2][:, 0:NA[d][1], :].rearrange("p w (b n) -> p b w n", b=NB)
                for b in range(NB):
                    for w in range(3):
                        mm = pe.matmul(o, lhsT=parts[:, b, w, :], rhs=cols[:, b], start=first and b == 0 and w == 0,
                                       stop=False)
                return mm

            def close(n):
                d = n % NGRP
                return pe.matmul(bank[n % 2][:, 0:NA[d][1] * WA], lhsT=zero_bf[0:P, :],
                                 rhs=adj_sb[n % 2][:, 0:NA[d][1], 0:WA], start=False, stop=True)

            def mlp1(l, k):
                g, m = NG[k]
                pe.wait_ge(s_hT, l * NGRP + k + 1)
                if k >= 2:
                    pe.wait_ge(s_m1c, l * NGRP + k - 1)
                pe.matmul(bank[2 + k % 2][:, 0:m * P], lhsT=LW1[:, l, :], rhs=fT[:, g * P:(g + m) * P], start=True, stop=True).then_inc(s_m1, 1)

            def mlp2(l, k):
                g, m = NG[k]
                pe.wait_ge(s_m1c, l * NGRP + k + 1)
                if k >= 2:
                    pe.wait_ge(s_m2c, l * NGRP + k - 1)
                pe.matmul(bank[4 + k % 2][:, 0:m * P], lhsT=LW2[:, l, :], rhs=h1T[:, g * P:(g + m) * P], start=True, stop=True).then_inc(s_m2, 1)

            for l in range(L):
                pe.wait_ge(s_parts, (l + 1) * NGRP)
                for d in range(NGRP):
                    n = l * NGRP + d
                    pe.wait_ge(s_ald[n % 2], 16 * (n // 2) + 16)
                    if n >= 2:
                        pe.wait_ge(s_hT, n - 1)
                    products(n, True).then_inc(s_main, 1)
                    with pe.If(over):
                        pe.wait_ge(s_ares, 16 * n + 16)
                        products(n, False)
                    close(n).then_inc(s_agg, 1)
                    if d >= 1:
                        mlp1(l, d - 1)
                    if d >= 2:
                        mlp2(l, d - 2)
                mlp1(l, NGRP - 1)
                mlp2(l, NGRP - 2)
                mlp2(l, NGRP - 1)
                for k, (g, m) in enumerate(NG):
                    pe.wait_ge(s_bn, NGRP + l * NGRP + k + 1)
                    if l * NGRP + k >= 2:
                        pe.wait_ge(s_bk, l * NGRP + k - 1)
                    for b in range(m):
                        mm = pe.transpose(bank[6 + k % 2][0:P, b * D:(b + 1) * D], fT[:, (g + b) * P:(g + b + 1) * P], ident[:, :])
                    mm.then_inc(s_bkT, 1)

        @block.vector
        def _(dve):
            chain = [0]

            def link(ins):
                chain[0] += 1
                ins.then_inc(s_d, 1)
                dve.wait_ge(s_d, chain[0])

            for s in (s_y, s_al):
                dve.sem_inc(s, 2)
            dve.sem_inc(s_acc, 4)
            dve.sem_inc(s_cnt, 1)
            dve.memset(zero_bf[:, :], 0.0)
            dve.memset(loA[:, SA:SA + 1, :], 0.0)
            dve.memset(pairA[:, SA:SA + 1, :], 0.0)
            dve.memset(keep_row[:, :], 0.0)
            dve.memset(deg1, 0.0).then_inc(s_deg0, 1)
            dve.memset(W1c[:, :], 0.0)
            dve.memset(W2c[:, :], 0.0)
            dve.memset(Wang_pad[:, :, :], 0.0)
            dve.memset(eps[:, :], 1e-5)
            dve.memset(ones[:, :], 1.0)
            dve.memset(Wdot_bd[:, :], 0.0).then_inc(s_zero, 1)
            dve.wait_ge(s_iota, 6)
            dve.tensor_copy(iota_row[:, :], iota_i[:, :])
            dve.tensor_copy(iota_p[:, :], iota_i[:, :])
            dve.tensor_copy(iota_pair[:, :], iota_pair_i[:, :])
            dve.wait_ge(s_fd, 16)
            C = 12582912.0

            def window(o, of, size, k):
                link(dve.tensor_scalar(o, of, (size - 1) / 2.0, 1.0 / size, ALU.subtract, ALU.mult))
                link(dve.tensor_scalar(o, o, C, None, ALU.add))
                link(dve.tensor_scalar(o, o, C, None, ALU.subtract))

            for k, size in enumerate((WA, P)):
                window(start_row[:, k, :], first_dst[:, :], size, k)
                link(dve.tensor_tensor(start_row[:, k, :], start_row[:, k, :], chunk_i[:, :], ALU.add))
            dve.sem_inc(s_start, 1)
            dve.wait_ge(s_startB, 1)
            link(dve.tensor_copy(startB, bank[5][0:QA, 0:2 * NC].rearrange("p (w c) -> p w c", w=2)))
            for w, (q, size, last) in enumerate(((QA, WA, NWA + SA), (QB, P, NB - 1))):
                link(dve.tensor_copy(step_f[w][:, :], step_i[w][:, :]))
                for k in range(SK):
                    link(dve.tensor_scalar(junk[0:q, 1:NC], startB[0:q, w, 1:NC], step_f[w][:, k:k + 1], None, ALU.is_le))
                    link(dve.reduce_sum(c_f[w][:, k:k + 1], junk[0:q, 1:NC], axis=AX_X))
                link(dve.tensor_tensor(w_f[w][:, :], step_f[w][:, :], c_f[w][:, :], ALU.subtract))
                link(dve.tensor_scalar(w_min[w][:, :], w_f[w][:, :], float(last), None, ALU.min))
                link(dve.tensor_scalar(wn_f[w][:, :], w_f[w][:, :], float(size), None, ALU.mult))
                link(dve.tensor_copy(c_i[w][:, :], c_f[w][:, :]))
                link(dve.tensor_copy(w_i[w][:, :], w_min[w][:, :]))
            dve.sem_inc(s_steps, 1)
            dve.wait_ge(s_deg, 48)
            link(dve.tensor_tensor(deg0, deg0.bitcast(I32), deg1.bitcast(I32), ALU.is_equal))
            link(dve.tensor_reduce(flag_col[:, :], deg0, AX_X, ALU.max))
            dve.sem_inc(s_degT, 1)
            dve.wait_ge(s_flagT, 1)
            link(dve.tensor_reduce(flag_f[:, 0:1], bank[6][0:1, 0:100], AX_X, ALU.max))
            link(dve.tensor_copy(flag_i[:, 0:1], flag_f[:, 0:1]))
            dve.sem_inc(s_flag, 1)
            for k, g in enumerate(range(0, NB, 8)):
                m = min(8, NB - g)
                dve.wait_ge(s_qn, k + 1)
                dve.tensor_copy(qn[:, g * DK:(g + m) * DK], bank[4][0:P, 0:m * DK]).then_inc(s_qnc, 1)
            dve.wait_ge(s_rows, 16 * 3 * SK)
            for k in range(SK):
                link(dve.tensor_scalar(dlA[:, k, :], dstR[:, k, :].bitcast(I32), wn_f[0][:, k:k + 1], None, ALU.subtract))
                link(dve.tensor_scalar(dstRB[:, k, :], dstRB[:, k, :].bitcast(I32), wn_f[1][:, k:k + 1], None, ALU.subtract))
            window(hiA, srcR.bitcast(I32), P, 0)
            link(dve.scalar_tensor_tensor(out=srcR, in0=hiA, scalar=-float(P), in1=srcR.bitcast(I32), op0=ALU.mult, op1=ALU.add))
            link(dve.tensor_scalar(okA, dlA, 0.0, None, ALU.is_ge))
            link(dve.scalar_tensor_tensor(out=okA, in0=dlA, scalar=float(WA), in1=okA, op0=ALU.is_lt, op1=ALU.mult))
            link(dve.scalar_tensor_tensor(out=dlA, in0=hiA, scalar=float(WA), in1=dlA, op0=ALU.mult, op1=ALU.add))
            link(dve.scalar_tensor_tensor(out=dlA, in0=dlA, scalar=1.0, in1=okA, op0=ALU.add, op1=ALU.mult))
            link(dve.tensor_scalar(dlA, dlA, 1.0, None, ALU.subtract))
            dve.sem_inc(s_rowsF, 2)
            n = 0
            for tab, q in ((pairA, QA), (loA, QA), (dstB, QB)):
                for k in range(SK):
                    dve.wait_ge(s_tabT, n + 1)
                    dve.tensor_copy(tab[:, k * q:(k + 1) * q, :].rearrange("p s j -> p j s"),
                                    bank[6 + n % 2][0:P, 0:G * q].rearrange("p (j s) -> p j s", j=G)).then_inc(s_tab, 1)
                    n += 1
            dve.wait_ge(s_walk, 48)
            link(dve.tensor_tensor(keep_row[:, 1:SA], walkA[:, 1:SA], walkA[:, 0:SA - 1], ALU.is_equal))
            dve.sem_inc(s_keepr, 1)
            link(dve.tensor_copy(goal[:, :], dummy_i[:, :]))
            late, ends_here = start_row[:, :, :].rearrange("o w c -> o (w c)")[:, 0:RA], junk_row[:, 0:RA]
            link(dve.tensor_tensor(late, walkA[:, 0:RA], walkA[:, 1:RA + 1], ALU.not_equal))
            link(dve.tensor_tensor(ends_here, walkA[:, 0:RA], dummy_i[:, 0:RA], ALU.subtract))
            link(dve.tensor_tensor(ends_here, ends_here, late, ALU.mult))
            link(dve.tensor_tensor(goal[:, 0:RA], ends_here, dummy_i[:, 0:RA], ALU.add))
            dve.wait_ge(s_keepT, 1)
            link(dve.tensor_copy(keep[:, :], bank[6][0:P, 0:SA]))
            dve.sem_inc(s_goal, 1)
            def gated(q, g):
                dve.wait_ge(s_xTc, done(g))
                dve.wait_ge(s_hid, done(g))
                dve.wait_ge(s_E, two_ago(g))
                dve.tensor_tensor(yk[:, q, :], xT[:, q, :], bank[2][:, 0:GE], ALU.mult)
                dve.tensor_tensor(yv[:, q, :], xT[:, q, :], bank[3][:, 0:GE], ALU.mult).then_inc(s_y, 1)

            def finish(i, q, g):
                dve.wait_ge(s_radc, done(g))
                for b in range(2):
                    r = dve.tensor_tensor(kt[:, q, 2 * b:2 * b + 2, :], rad[:, q, 2 * b:2 * b + 2, 0:DK],
                                          pair_bank(b)[:, :, DK + D:], ALU.mult)
                r.then_inc(s_t1, 1)
                dve.wait_ge(s_vfree, g + 1)
                dve.tensor_tensor(vo[:, q, :, :], rad[:, q, :, DK:],
                                  bank[6][0:P, :].rearrange("p (j k) -> p j k", j=G), ALU.mult).then_inc(s_v, 1)
                dve.wait_ge(s_gq[q], 16 * G * i + 16 * G)
                dve.wait_ge(s_t1, g + 1)
                dve.tensor_tensor(kt[:, q, :, :], kt[:, q, :, :], qg[:, q * G:(q + 1) * G, :], ALU.mult).then_inc(s_t2, 1)
                dve.wait_ge(s_t2, g + 1)
                dve.reduce_sum(alpha_em[:, bass.ds(g * (G * H), G * H)],
                               kt[:, q, :, :].rearrange("p j (h k) -> p (j h) k", h=H), axis=AX_X).then_inc(s_al, 1)

            def mark(n, k):
                dve.wait_ge(s_bm, n + 1)
                for j in range(G):
                    dve.tensor_scalar(ohl[:, k, j, :], iota_p[0:P, :], loA[:, bass.ds(n, 1), j], None, ALU.is_equal)
                    m = dve.tensor_scalar(ohp[:, k, j, :], iota_pair[0:P, :], pairA[:, bass.ds(n, 1), j], None, ALU.is_equal)
                m.then_inc(s_ohA, 1)

            def take(n, k, m):
                dve.wait_ge(s_bm, n + 3)
                dve.wait_ge(s_cbf, n)
                dve.wait_ge(s_cnt, n + 1)
                dve.scalar_tensor_tensor(out=cnt[:, k, :], in0=cnt[:, 1 - k, :], scalar=keep[:, bass.ds(n, 1)],
                                         in1=bank[4][0:P, 0:PW], op0=ALU.mult, op1=ALU.add).then_inc(s_cnt, 1)
                with dve.If(over):
                    dve.wait_ge(s_cbf, n + 2)
                    dve.wait_ge(s_cnt, n + 2)
                    dve.wait_ge(s_arst[k], 16 * m + 16)
                    dve.tensor_tensor(cnt_res[:, k, :], cnt[:, k, :], cnt_bf[:, k, :], ALU.subtract).then_inc(s_cres, 1)
                dve.sem_inc(s_pad, 1)

            over = dve.value_load(flag_i[0:1, 0:1], min_val=0, max_val=1)
            link(dve.memset(cnt, 0.0))
            dve.memset(cnt_bf, 0.0)
            link(dve.memset(cnt_res, 0.0))
            dve.sem_inc(s_cnt0, 1)
            mark(0, 0)
            with dve.Fori(0, IT) as i:
                for q in range(2):
                    g = 2 * i + q
                    gated(q, g)
                    take(2 * g, 0, g)
                    mark(2 * g + 1, 1)
                    mark(2 * g + 2, 0)
                    finish(i, q, g)
                    take(2 * g + 1, 1, g)

            dve.wait_ge(s_al, 2 * IT + 2)
            dve.wait_ge(s_afree, 1)
            dve.wait_ge(s_vfree, 2 * IT + 2)
            dve.wait_ge(s_bm, SA + 2)
            dve.tensor_copy(relaid.rearrange("p (t c h) -> p t c h", c=CH, h=H),
                            alpha_em[:, :].rearrange("p (c t h) -> p t c h", c=CH, h=H)).then_inc(s_relaid, 1)
            for k in range(0, CG, 2):
                dve.wait_ge(s_alT, k + 1)
                dve.tensor_copy(al[:, k * GE:(k + 1) * GE].rearrange("c (p j) -> c j p", j=G),
                                bank[0][0:CHH, 0:GE].rearrange("c (j p) -> c j p", j=G)).then_inc(s_eTc, 1)
            dve.wait_ge(s_alT, CG)
            dve.memset(dst_s[:, :], -1).then_inc(s_halo, 1)
            dview = bufR[0:CHH, :].bitcast(I32)
            dve.wait_ge(s_dsts, 16 * (2 * CH - 1))
            link(dve.tensor_tensor(pen[:, 1:CE], dview[:, 1:CE], dview[:, 0:CE - 1], ALU.not_equal))
            link(dve.tensor_tensor(pen[:, CE:CE + 1], dst_s[:, :], dview[:, CE - 1:CE], ALU.not_equal))
            link(dve.tensor_scalar(pen[:, 1:CE + 1], pen[:, 1:CE + 1], BIG, None, ALU.mult))
            link(dve.memset(pen[:, 0:1], 0.0))
            dve.wait_ge(s_alc, CG // 2)
            link(dve.tensor_tensor_scan(run, pen[:, 0:CE], al, BIG, ALU.add, ALU.max))
            link(dve.tensor_tensor_scan(run[:, ::-1], pen[:, CE:0:-1], run[:, ::-1], BIG, ALU.add, ALU.max))
            FIRST, LAST, INNER, LINK = range(4)
            dve.tensor_copy(ends[:, FIRST:FIRST + 1], run[:, 0:1])
            dve.tensor_copy(ends[:, LAST:LAST + 1], run[:, CE - 1:CE])
            dve.tensor_copy(ends[:, LINK:LINK + 1], pen[:, CE:CE + 1])
            dve.tensor_reduce(ends[:, INNER:INNER + 1], pen[:, 1:CE], AX_X, ALU.min).then_inc(s_endsd, 1)
            dve.wait_ge(s_endT, 1)
            link(dve.tensor_copy(row_end[:, :, :], bank[2][0:1, 0:4 * CHH].rearrange("o (w c) -> o w c", w=4)))
            link(dve.memset(row_c[:, :, :], BIG))

            def part(row, c):
                return row[:, c * H:(c + 1) * H]

            for c in range(1, CH):
                link(dve.tensor_tensor(part(row_E[:, 0, :], c), part(row_c[:, 0, :], c - 1), part(row_end[:, INNER, :], c - 1), ALU.add))
                link(dve.tensor_tensor(part(row_E[:, 0, :], c), part(row_E[:, 0, :], c), part(row_end[:, LAST, :], c - 1), ALU.max))
                link(dve.tensor_tensor(part(row_c[:, 0, :], c), part(row_E[:, 0, :], c), part(row_end[:, LINK, :], c - 1), ALU.add))
            for c in range(CH - 2, -1, -1):
                link(dve.tensor_tensor(part(row_E[:, 1, :], c), part(row_c[:, 1, :], c + 1), part(row_end[:, INNER, :], c + 1), ALU.add))
                link(dve.tensor_tensor(part(row_E[:, 1, :], c), part(row_E[:, 1, :], c), part(row_end[:, FIRST, :], c + 1), ALU.max))
                link(dve.tensor_tensor(part(row_c[:, 1, :], c), part(row_E[:, 1, :], c), part(row_end[:, LINK, :], c), ALU.add))
            dve.sem_inc(s_rowE, 1)
            dve.wait_ge(s_carT, 1)
            link(dve.tensor_copy(carry[:, :], bank[3][0:CHH, 0:2]))
            link(dve.tensor_tensor_scan(run, pen[:, 0:CE], run, carry[:, 0:1], ALU.add, ALU.max))
            link(dve.memset(pen[:, CE:CE + 1], 0.0))
            link(dve.tensor_tensor_scan(run[:, ::-1], pen[:, CE:0:-1], run[:, ::-1], carry[:, 1:2], ALU.add, ALU.max))
            dve.tensor_tensor(al, al, run, ALU.subtract).then_inc(s_sub, 1)
            for k in range(CG):
                dve.wait_ge(s_eT, k + 1)
                dve.tensor_copy(alpha_em[:, :].rearrange("p (c g j h) -> p g j c h", c=CH, h=H, j=G)[:, k],
                                bank[4 + k % 2][0:P, 0:G * CHH].rearrange("p (j c h) -> p j c h", j=G, c=CH)).then_inc(s_eTc, 1)
            dve.wait_ge(s_eTc, CG // 2 + CG)

            def prepare(i, u):
                st = 4 * i + u
                dve.wait_ge(s_mm, st + 1)
                dve.tensor_tensor(oh[:, u, :, :], iota_row[0:P, :].unsqueeze(1).to_broadcast([P, G, P]),
                                  dstB[:, bass.ds(st, 1), :].rearrange("p o j -> p (o j)").unsqueeze(2).to_broadcast([P, G, P]),
                                  ALU.is_equal).then_inc(s_oh, 1)

            def add(i, u, b):
                st = 4 * i + u
                dve.wait_ge(s_acc, st + 4)
                dve.wait_ge(s_mm, st + 5)
                o = acc[:, bass.ds(b, 1), :]
                dve.tensor_tensor(o, bank[u][0:P, 0:W].unsqueeze(1), o, ALU.add).then_inc(s_acc, 1)

            def block_of(i, u):
                return dve.value_load(walkB[0:1, 1, bass.ds(4 * i + u, 1)], min_val=0, max_val=NB - 1)

            link(dve.memset(acc, 0.0))
            for u in range(2):
                prepare(0, u)
            with dve.Fori(0, SB // 4 - 1) as i:
                for u in range(4):
                    b = block_of(i, u)
                    prepare(i + (u + 2) // 4, (u + 2) % 4)
                    add(i, u, b)
            end = SB // 4 - 1
            for u in range(4):
                if u < 2:
                    prepare(end, u + 2)
                add(end, u, block_of(end, u))

            def blocks(a):
                return a.rearrange("p (b f) -> p b f", b=NB)

            def spread(a):
                return a.unsqueeze(2).to_broadcast([P, NB, D])

            def layernorm(n, y, o):
                sq = bufR[0:P, 2 * N:2 * N + NB * D]
                link(dve.reduce_sum(st25[:, 0, :], blocks(y), axis=AX_X))
                link(dve.tensor_scalar(st25[:, 0, :], st25[:, 0, :], -1.0 / D, None, ALU.mult))
                link(dve.tensor_tensor(blocks(y), blocks(y), spread(st25[:, 0, :]), ALU.add))
                link(dve.tensor_tensor(sq, y, y, ALU.mult))
                dve.reduce_sum(st25[:, 1, :], blocks(sq), axis=AX_X).then_inc(s_var, 1)
                dve.wait_ge(s_sd, n)
                link(dve.reciprocal(st25[:, 3, :], st25[:, 2, :]))
                dve.tensor_tensor(o, blocks(y), spread(st25[:, 3, :]), ALU.mult).then_inc(s_ready, 1)

            dve.wait_ge(s_acc, SB + 4)
            link(dve.tensor_scalar(rden[:, :].rearrange("p (b h) -> p b h", b=NB), acc[:, :, D:W], 0.5, None, ALU.max))
            link(dve.reciprocal(rden[:, :], rden[:, :]))
            for b in range(NB):
                mul = dve.tensor_tensor(tmp[:, b * D:(b + 1) * D].rearrange("p (h v) -> p h v", h=H),
                                        acc[:, b, 0:D].rearrange("p (h v) -> p h v", h=H),
                                        rden[:, b * H:(b + 1) * H].unsqueeze(2).to_broadcast([P, H, D // H]), ALU.mult)
            mul.then_inc(s_nm, 1)
            for k, (g, m) in enumerate(NG):
                dve.wait_ge(s_qn, len(range(0, NB, 8)) + k + 1)
                dve.tensor_tensor(tmp2[:, g * D:(g + m) * D], bank[2 + k % 2][0:P, 0:m * D],
                                  x_nm[:, g:g + m, :].rearrange("p b f -> p (b f)"), ALU.add).then_inc(s_bn, 1)
            dve.wait_ge(s_bn, len(NG))
            layernorm(1, tmp2, x_nm[:, :, :])
            dve.wait_ge(s_ready, 1)

            def split(n, g, m, of):
                r = rest[:, n % 2, 0:m * D].rearrange("p (b f) -> p b f", b=m)
                dve.wait_ge(s_hi, n + 1)
                dve.tensor_tensor(r, of, parts[:, g:g + m, 0, :], ALU.subtract).then_inc(s_r1, 1)
                dve.wait_ge(s_mid, n + 1)
                return dve.tensor_tensor(parts[:, g:g + m, 2, :], r, parts[:, g:g + m, 1, :], ALU.subtract)

            for k, (g, m) in enumerate(NG):
                split(k, g, m, x_nm[:, g:g + m, :]).then_inc(s_parts, 1)
            for l in range(L):
                for k, (g, m) in enumerate(NG):
                    n = l * NGRP + k
                    dve.wait_ge(s_agg, n + 1)
                    if l == 0:
                        dve.wait_ge(s_nfc, NGRP + k + 1)
                    dve.tensor_tensor(fT[:, g * P:(g + m) * P], bank[n % 2][:, 0:m * P], fT[:, g * P:(g + m) * P], ALU.add).then_inc(s_hT, 1)
                    if k >= 3:
                        dve.wait_ge(s_m2c, n - 2)
                        g3, m3 = NG[k - 3]
                        dve.bn_stats(bn6[:, k - 3, :], h2T[:, g3 * P:(g3 + m3) * P]).then_inc(s_st, 1)
                for k in range(NGRP - 3, NGRP):
                    dve.wait_ge(s_m2c, l * NGRP + k + 1)
                    g3, m3 = NG[k]
                    dve.bn_stats(bn6[:, k, :], h2T[:, g3 * P:(g3 + m3) * P]).then_inc(s_st, 1)
                dve.wait_ge(s_st, (l + 1) * NGRP)
                dve.bn_aggr(bn2[:, :], bn6[:, :, :].rearrange("p k s -> p (k s)")).then_inc(s_var, 1)
                dve.wait_ge(s_sd, l + 2)
                link(dve.reciprocal(st1[:, 4:5], st1[:, 3:4]))
                link(dve.tensor_tensor(st1[:, 5:6], st1[:, 4:5], Lvec[:, 2, l:l + 1], ALU.mult))
                dve.wait_ge(s_m1, (l + 1) * NGRP)
                link(dve.tensor_scalar(h2T, h2T, bn2[:, 0:1], None, ALU.subtract))
                for k, (g, m) in enumerate(NG):
                    e = slice(g * P, (g + m) * P)
                    dve.tensor_scalar(fT[:, e], h2T[:, e], st1[:, 5:6], Lvec[:, 3, l:l + 1], ALU.mult, ALU.add).then_inc(s_bn, 1)
                for k, (g, m) in enumerate(NG):
                    dve.wait_ge(s_bkT, l * NGRP + k + 1)
                    rows_ = bank[6 + k % 2][0:P, 0:m * D].rearrange("p (b f) -> p b f", b=m)
                    if l < L - 1:
                        last = split((l + 1) * NGRP + k, g, m, rows_)
                        last.then_inc(s_parts, 1)
                        dve.wait_ge(s_parts, (l + 1) * NGRP + k + 1)
                        dve.sem_inc(s_bk, 1)
                    else:
                        link(dve.tensor_tensor(blocks(tmp2)[:, g:g + m, :], rows_, x_nm[:, g:g + m, :], ALU.add))
                        dve.sem_inc(s_bk, 1)
            layernorm(L + 2, tmp2, blocks(tmp2))


_INS = ['x', 'src', 'dst', 'edge_attr_16', 'edge_attr_16_n2', 'L0_gnn_Wq', 'L0_gnn_Wang_k', 'L0_gnn_Wlin_k', 'L0_gnn_W1k',
        'L0_gnn_b1k', 'L0_gnn_W2k', 'L0_gnn_Wang_v', 'L0_gnn_Wlin_v', 'L0_gnn_W1v', 'L0_gnn_b1v', 'L0_gnn_W2v', 'L0_gnn_Wdot',
        'L0_gnn_Wout', 'L1_gnn_W1', 'L1_gnn_b1', 'L1_gnn_W2', 'L1_gnn_b2', 'L1_gnn_gamma', 'L1_gnn_beta']
_OUTS = [((3125, 128), 'float32')]


def kernel(**inputs):
    import numpy as _np
    import concourse.bacc as _bacc
    from concourse import mybir as _mybir
    from concourse.bass_utils import run_bass_kernel_spmd as _run

    nc = _bacc.Bacc("TRN2", target_bir_lowering=False, num_devices=1)
    arrays, args = {}, []
    for name in _INS:
        a = _np.ascontiguousarray(inputs[name])
        arrays[f"in_{name}_dram"] = a
        args.append(nc.dram_tensor(f"in_{name}_dram", a.shape, _mybir.dt.from_np(a.dtype), kind="ExternalInput").ap())
    for i, (shape, dtype) in enumerate(_OUTS):
        dt = _mybir.dt.from_np(_np.dtype(dtype))
        args.append(nc.dram_tensor(f"out_{i}_dram", shape, dt, kind="ExternalOutput").ap())
    gnn(nc, *args)
    r = _run(nc, [arrays], core_ids=[0])
    return r.results[0]["out_0_dram"]
```

```python
from contextlib import ExitStack

import concourse.bass as bass
from concourse import mybir

F32 = mybir.dt.float32
F16 = mybir.dt.float16
I32 = mybir.dt.int32
BF16 = mybir.dt.bfloat16
ALU = mybir.AluOpType
ACT = mybir.ActivationFunctionType
AX_X = mybir.AxisListType.X


def gnn(nc, x, src, dst, edge_attr, edge_sh, Wq, Wang_k, Wlin_k, W1k, b1k, W2k, Wang_v, Wlin_v, W1v, b1v, W2v,
        Wdot, Wout, L_W1, L_b1, L_W2, L_b2, L_gamma, L_beta, out):
    N, D = x.shape
    E = src.shape[0]
    A = edge_attr.shape[1]
    HID = W1k.shape[1]
    DK = W2k.shape[1]
    HD = Wdot.shape[0]
    H = DK // HD
    L = L_W1.shape[0]
    P = 125
    NB = N // P
    T = E // P
    G = 4
    GE = G * P
    IT = E // (2 * GE)
    CH = 10
    CE = E // CH
    CG = (E // GE) // CH
    CHH = CH * H
    NC = E // GE
    SK = 4
    WA = 20
    NWA = -(-N // WA)
    RA = NC + NWA - 1
    SA = 2 * NC
    QA = SA // SK
    RB = NC + NB - 1
    SB = -(-RB // 16) * 16
    QB = SB // SK
    PW = NB * WA
    GW = 500 // WA
    TERMS = 6
    W_PART = (0, 1, 2, 0, 1, 0)
    PW_T = P + 1
    NV = 8
    BIG = -1.0e30
    V1 = D // H + 1
    W = H * V1
    NG = [(g, min(4, NB - g)) for g in range(0, NB, 4)]
    assert N == NB * P and E == IT * 2 * GE and RA <= SA and QA <= 128 and E == CH * CE and GW * WA == 4 * P

    ctx = ExitStack()
    with ctx:
        def sb(name, shape, dt=F32):
            return ctx.enter_context(nc.sbuf_tensor(name, shape, dt))

        def sem(name):
            return ctx.enter_context(nc.semaphore(name))

        def dram(name, shape, dt=F32):
            return nc.dram_tensor(name, shape, dt, kind="Internal").ap()

        q_table = dram("q_table", (N, DK))
        v_table = dram("v_table", (E, W))
        walk_dram = dram("walk_dram", (2, 2, SA), I32)
        DUMMY = 4
        adj = dram("adj", (NWA + DUMMY, P, PW), BF16)
        adj_res = dram("adj_res", (NWA + DUMMY, P, PW), BF16)

        ident = sb("ident", [128, 128])
        iota_i = sb("iota_i", [128, P], I32)
        iota_row = sb("iota_row", [128, P])
        zero_bf = sb("zero_bf", [128, 128], BF16)
        iota_p = sb("iota_p", [128, P], BF16)
        iota_pair_i = sb("iota_pair_i", [128, PW], I32)
        iota_pair = sb("iota_pair", [128, PW], F16)
        step_i = [sb("stepA_i", [QA, SK], I32), sb("stepB_i", [QB, SK], I32)]
        chunk_i = sb("chunk_i", [1, NC], I32)
        dummy_i = sb("dummy_i", [1, SA], I32)
        ones = sb("ones", [1, 128])
        Wq_sb = sb("Wq_sb", [D, DK])
        Wlk = sb("Wlk", [D, DK])
        Wlv = sb("Wlv", [D, D])
        ident_bf = sb("ident_bf", [128, 128], BF16)
        W_st = sb("W_st", [TERMS * A, 3, D], BF16)
        W2c = sb("W2c", [2 * HID, DK + D])
        b1c = sb("b1c", [2 * HID, 1])
        Wang_sb = sb("Wang_sb", [D, 2, A])
        Wdot_bd = sb("Wdot_bd", [DK, DK])
        Wout_sb = sb("Wout_sb", [D, D])
        LW1 = sb("LW1", [D, L, D])
        LW2 = sb("LW2", [D, L, D])
        Lvec = sb("Lvec", [D, 4, L])
        eps = sb("eps", [128, 1])
        first_dst = sb("first_dst", [1, NC], I32)
        start_row = sb("start_row", [1, 2, NC])
        step_f, c_f, w_f, wn_f, w_min, c_i, w_i = ([sb(f"{name}{k}", [q, SK], dt) for k, q in enumerate((QA, QB))]
                                                   for name, dt in (("step_f", F32), ("c_f", F32), ("w_f", F32), ("wn_f", F32),
                                                                    ("w_min", F32), ("c_i", I32), ("w_i", I32)))
        walkA = sb("walkA", [1, SA], I32)
        keep_row = sb("keep_row", [1, SA])
        junk_row = sb("junk_row", [1, SA])
        goal = sb("goal", [1, SA], I32)
        walkB = sb("walkB", [1, 2, SB], I32)
        keep = sb("keep", [P, SA])
        loA = sb("loA", [P, SA + 1, G])
        pairA = sb("pairA", [P, SA + 1, G])
        dstB = sb("dstB", [P, SB, G])
        flag_f = sb("flag_f", [1, 2])
        flag_i = sb("flag_i", [1, 2], I32)
        flag_col = sb("flag_col", [100, 1])
        x_nm = sb("x_nm", [P, NB, D])
        idx_src = sb("idx_src", [P, NC * G], I32)
        idx_dst = sb("idx_dst", [P, NC * G], I32)
        idx_slot = sb("idx_slot", [P, 2, 2 * G], I32)
        es = sb("es", [P, 2, G, 2, A])
        xg = sb("xg", [P, 2 * G, D])
        qg = sb("qg", [P, 2 * G, DK])
        rad = sb("rad", [P, 2, G, DK + D])
        kt = sb("kt", [P, 2, G, DK])
        alpha_em = sb("alpha_em", [P, T * H])
        W_src, W_rest = (alpha_em[0:A, c:c + 3 * D].rearrange("a (m f) -> a m f", m=3) for c in (5000, 5000 + 3 * D))
        W_parts = alpha_em[0:A, 5000 + 6 * D:5000 + 6 * D + 9 * D // 2].bitcast(BF16).rearrange("a (t m f) -> a t m f", t=3, m=3)
        bufA = sb("bufA", [128, CE])
        bufR = sb("bufR", [128, CE])
        bufP = sb("bufP", [128, CE + 2], BF16)
        adj_sb = [alpha_em[:, 0:GW * PW // 2].bitcast(BF16).rearrange("p (w c) -> p w c", w=GW),
                  bufA[0:P, 0:GW * PW // 2].bitcast(BF16).rearrange("p (w c) -> p w c", w=GW)]
        rest = bufA[0:P, GW * PW // 2:GW * PW // 2 + 8 * D].rearrange("p (s e) -> p s e", s=2)
        parts = bufP[0:P, 0:NB * 3 * D].rearrange("p (b w f) -> p b w f", b=NB, w=3)
        yk, yv, hidT = (bufA[:, k * 2 * GE:(k + 1) * 2 * GE].rearrange("p (q e) -> p q e", q=2) for k in range(3))
        vo = bufA[0:P, 3000:3000 + 2 * G * W].rearrange("p (q j f) -> p q j f", q=2, j=G)
        al = bufA[0:CHH, :]
        run = bufR[0:CHH, :]
        pen = bufP[0:CHH, 0:CE + 1]
        dst_s = sb("dst_s", [CHH, 1], I32)
        tmp = bufA[0:P, 0:NB * D]
        tmp2 = bufA[0:P, 2 * NB * D:3 * NB * D]
        fT = bufR[:, 0:N]
        h1T = bufR[:, N:2 * N]
        h2T = bufR[:, 2 * N:3 * N]
        ohl = bufR[0:P, 0:500].bitcast(BF16).rearrange("p (s j c) -> p s j c", s=2, j=G)
        ohp = bufR[0:P, 500:2500].bitcast(BF16).rearrange("p (s j c) -> p s j c", s=2, j=G)
        cnt = bufR[0:P, 2500:3500].rearrange("p (s c) -> p s c", s=2)
        cnt_bf = bufR[0:P, 3500:4000].bitcast(BF16).rearrange("p (s c) -> p s c", s=2)
        cnt_res = bufR[0:P, 4000:4500].bitcast(BF16).rearrange("p (s c) -> p s c", s=2)
        sT = bufR[0:TERMS * A, 4500:5500].bitcast(BF16).rearrange("p (q w e) -> p q w e", q=2, w=2)
        es_parts = bufP[0:P, 0:4 * G * TERMS * A].rearrange("p (q r t a) -> p q r t a", q=2, r=2 * G, t=TERMS)
        es_rest = bufP[0:P, 4 * G * TERMS * A:4 * G * TERMS * A + 8 * G * A].bitcast(F32).rearrange("p (q r a) -> p q r a", q=2, r=2 * G)
        xT = bufR[:, 5500:6500].rearrange("p (q e) -> p q e", q=2)
        relaid = bufR[0:P, 0:T * H]
        gs = bufA[0:P, 0:4 * G * W].rearrange("p (s j w) -> p s j w", s=4, j=G)
        oh = bufA[0:P, 4 * G * W:4 * G * (W + P)].rearrange("p (s j w) -> p s j w", s=4, j=G)
        v_ring = bufR[0:P, 0:NV * G * W].rearrange("p (u e) -> p u e", u=NV)
        qn = bufR[0:P, 2 * N:2 * N + NB * DK]
        acc = bufP[0:P, 0:2 * NB * W].bitcast(F32).rearrange("p (b w) -> p b w", b=NB)
        ends = sb("ends", [CHH, 4])
        carry = sb("carry", [CHH, 2])
        row_end = sb("row_end", [1, 4, CHH])
        row_c = sb("row_c", [1, 2, CHH])
        row_E = sb("row_E", [1, 2, CHH])
        st25 = sb("st25", [P, 4, NB])
        rden = sb("rden", [P, NB * H])
        st1 = sb("st1", [128, 8])
        bn6 = sb("bn6", [128, len(NG), 6])
        bn2 = sb("bn2", [128, 2])

        bank = [ctx.enter_context(nc.psum_tensor(f"bank{i}", [128, 512], F32)) for i in range(8)]

        turned = bank[1][0:TERMS * A, :].bitcast(BF16)[:, 0:2 * G * PW_T].rearrange("p (r e) -> p r e", r=2 * G)

        def rows(buf, n, k):
            return buf[0:n, k * SK * GE:(k + 1) * SK * GE].rearrange("s (k e) -> s k e", k=SK)

        srcR, dstR, hiA, dlA, okA = (rows(bufA, QA, k) for k in range(5))
        dstRB = rows(alpha_em, QB, 0)
        startB = alpha_em[0:QA, 2000:2000 + 2 * NC].rearrange("p (w c) -> p w c", w=2)
        junk = alpha_em[0:QA, 2400:2400 + NC]
        deg0, deg1 = (alpha_em[0:100, 3000 + k * 1000:4000 + k * 1000] for k in range(2))

        s_ident0, s_ident, s_iota, s_identb = (sem(n) for n in ("s_ident0", "s_ident", "s_iota", "s_identb"))
        s_zero, s_weights, s_node_weights, s_x_loaded, s_first_dst = (sem(n) for n in ("s_zero", "s_weights", "s_node_weights", "s_x_loaded", "s_first_dst"))
        s_chain, s_pad = sem("s_chain"), sem("s_pad")
        s_start, s_startB, s_steps, s_rows = (sem(n) for n in ("s_start", "s_startB", "s_steps", "s_rows"))
        s_rowsF, s_tabT, s_tab, s_walk_st, s_walk = (sem(n) for n in ("s_rowsF", "s_tabT", "s_tab", "s_walk_st", "s_walk"))
        s_keepr, s_keepT, s_goal = (sem(n) for n in ("s_keepr", "s_keepT", "s_goal"))
        s_deg0, s_degrees, s_degT, s_flagT, s_flag = (sem(n) for n in ("s_deg0", "s_degrees", "s_degT", "s_flagT", "s_flag"))
        s_wangT, s_wang, s_wparts, s_wst = (sem(n) for n in ("s_wangT", "s_wang", "s_wparts", "s_wst"))
        s_xnT, s_xn, s_qT, s_qTc, s_qn, s_qnc, s_qst = (sem(n) for n in ("s_xnT", "s_xn", "s_qT", "s_qTc", "s_qn", "s_qnc", "s_qst"))
        s_idx, s_attributes, s_x_rows, s_q_rows, s_values_st = ([sem(f"{n}{q}") for q in range(2)] for n in ("s_idx", "s_attributes", "s_x_rows", "s_q_rows", "s_values_st"))
        s_idx_x, s_idx_q = sem("s_idx_x"), sem("s_idx_q")
        s_part1, s_rest1, s_part2, s_part3 = (sem(n) for n in ("s_part1", "s_rest1", "s_part2", "s_part3"))
        s_turned, s_hidden, s_edges = (sem(n) for n in ("s_turned", "s_hidden", "s_edges"))
        s_sTc, s_xTc, s_hidc, s_radc = (sem(n) for n in ("s_sTc", "s_xTc", "s_hidc", "s_radc"))
        s_gated, s_values, s_k, s_qk, s_alpha, s_vfree = (sem(n) for n in ("s_gated", "s_values", "s_k", "s_qk", "s_alpha", "s_vfree"))
        s_cnt0, s_marked, s_counted, s_taken, s_narrowed, s_dropped = (sem(n) for n in ("s_cnt0", "s_marked", "s_counted", "s_taken", "s_narrowed", "s_dropped"))
        s_adj_st, s_adj_res_st = ([sem(f"{n}{k}") for k in range(2)] for n in ("s_adj_st", "s_adj_res_st"))
        s_afree = sem("s_afree")
        s_relaid, s_halo, s_dsts, s_alT, s_alc = (sem(n) for n in ("s_relaid", "s_halo", "s_dsts", "s_alT", "s_alc"))
        s_endsd, s_endT, s_carT, s_rowE = (sem(n) for n in ("s_endsd", "s_endT", "s_carT", "s_rowE"))
        s_sub, s_exp, s_eT, s_eTc = (sem(n) for n in ("s_sub", "s_exp", "s_eT", "s_eTc"))
        s_values_ld = [sem(f"s_values_ld{u}") for u in range(NV)]
        s_onehot, s_weighted, s_product, s_summed = (sem(n) for n in ("s_onehot", "s_weighted", "s_product", "s_summed"))
        s_divided, s_nfT, s_nfc, s_ready = (sem(n) for n in ("s_divided", "s_nfT", "s_nfc", "s_ready"))
        s_adj_ld = [sem(f"s_adj_ld{k}") for k in range(2)]
        s_main, s_adj_res_ld, s_aggregated, s_h = (sem(n) for n in ("s_main", "s_adj_res_ld", "s_aggregated", "s_h"))
        s_high, s_rest, s_mid, s_parts = (sem(n) for n in ("s_high", "s_rest", "s_mid", "s_parts"))
        s_mlp1, s_mlp1c, s_mlp2, s_mlp2c = (sem(n) for n in ("s_mlp1", "s_mlp1c", "s_mlp2", "s_mlp2c"))
        s_stats, s_var, s_root, s_normed, s_backT, s_back = (sem(n) for n in ("s_stats", "s_var", "s_root", "s_normed", "s_backT", "s_back"))
        s_out = sem("s_out")

        def done(g):
            return g + 3

        def one_ago(g):
            return g + 2

        def two_ago(g):
            return g + 1

        def within(g):
            return not isinstance(g, int) or g < NC

        def pair_bank(b):
            return bank[5 + 2 * b][0:P, :].rearrange("p (j c) -> p j c", j=2)

        NA = [(d * GW, min(GW, NWA - d * GW)) for d in range(-(-NWA // GW))]
        NGRP = len(NG)
        v_c = v_table.rearrange("(c p j) f -> c p (j f)", p=P, j=G)
        assert len(NA) == NGRP
        LG = [(l, d) for l in range(L) for d in range(NGRP)]

        def back_rows(k, g, m):
            return bank[6 + k % 2][0:P, 0:m * D].rearrange("p (b f) -> p b f", b=m)

        block = ctx.enter_context(nc.Block())

        @block.sync
        def _(sp):
            with nc.allow_non_contiguous_dma(reason="one value for each chunk"):
                sp.dma_start(first_dst[:, :], dst.rearrange("(o c e) -> o c e", o=1, e=GE)[:, :, 0]).then_inc(s_first_dst, 16)
            sp.wait_ge(s_deg0, 1)
            sp.dma_start(deg0.bitcast(I32), dst.rearrange("(p e) -> p e", p=100)).then_inc(s_degrees, 16)
            sp.dma_start(deg1.bitcast(I32)[0:99, :], dst[256:256 + 99000].rearrange("(p e) -> p e", p=99)).then_inc(s_degrees, 16)
            sp.dma_start(deg1.bitcast(I32)[99:100, 0:E - 99256], dst[99256:E].rearrange("(p e) -> p e", p=1)).then_inc(s_degrees, 16)
            sp.dma_start(x_nm[:, :, :], x.rearrange("(b p) f -> p b f", p=P)).then_inc(s_x_loaded, 16)
            sp.wait_ge(s_zero, 1)
            loads = [(Wq_sb[:, :], Wq), (Wlk[:, :], Wlin_k), (Wlv[:, :], Wlin_v),
                     (W_src[:, 0, 0:HID], W1k), (W_src[:, 0, HID:], W1v), (W2c[0:HID, 0:DK], W2k), (W2c[HID:, DK:], W2v),
                     (b1c[0:HID, :], b1k.rearrange("(a b) -> a b", b=1)),
                     (b1c[HID:, :], b1v.rearrange("(a b) -> a b", b=1)),
                     (Wang_sb[:, 0, :], Wang_k), (Wang_sb[:, 1, :], Wang_v)]
            loads += [(Wdot_bd[h * HD:(h + 1) * HD, h * HD:(h + 1) * HD], Wdot) for h in range(H)]
            for a, b in loads:
                sp.dma_start(a, b).then_inc(s_weights, 16)
            sp.wait_ge(s_steps, 1)
            with nc.allow_non_contiguous_dma(reason="two numbers for each step"):
                for k, q in enumerate((QA, QB)):
                    for w, tab in enumerate((c_i[k], w_i[k])):
                        sp.dma_start(walk_dram[k, w, 0:SK * q].rearrange("(k q) -> q k", k=SK), tab[:, :]).then_inc(s_walk_st, 16)
                sp.wait_ge(s_walk_st, 64)
                sp.dma_start(walkA[:, :], walk_dram[0, 1:2, :]).then_inc(s_walk, 16)
                sp.dma_start(walkB[:, 0, :], walk_dram[1, 0:1, 0:SB]).then_inc(s_walk, 16)
                sp.dma_start(walkB[:, 1, :], walk_dram[1, 1:2, 0:SB]).then_inc(s_walk, 16)
                sp.dma_start(Wout_sb[:, :], Wout).then_inc(s_node_weights, 16)
                sp.dma_start(LW1[:, :, :], L_W1.rearrange("l a b -> a l b")).then_inc(s_node_weights, 16)
                sp.dma_start(LW2[:, :, :], L_W2.rearrange("l a b -> a l b")).then_inc(s_node_weights, 16)
                for k, vec in enumerate((L_b1, L_b2, L_gamma, L_beta)):
                    sp.dma_start(Lvec[:, k, :], vec.rearrange("l a -> a l")).then_inc(s_node_weights, 16)
            sp.wait_ge(s_wparts, 1)
            for t in range(TERMS):
                sp.dma_start(W_st[t * A:(t + 1) * A, :, :], W_parts[:, W_PART[t], :, :]).then_inc(s_wst, 16)
            sp.wait_ge(s_qnc, len(range(0, NB, 8)))
            sp.dma_start(q_table.rearrange("(b p) k -> p b k", p=P),
                         qn[:, :].rearrange("p (b k) -> p b k", b=NB)).then_inc(s_qst, 16)

            src_v = src.rearrange("(i q p j) -> i q p j", p=P, q=2, j=G)
            dst_v = dst.rearrange("(i q p j) -> i q p j", p=P, q=2, j=G)
            ea_v = edge_attr.rearrange("(i q p j) a -> i q p j a", p=P, q=2, j=G)
            sh_v = edge_sh.rearrange("(i q p j) a -> i q p j a", p=P, q=2, j=G)
            v_v = v_table.rearrange("(i q p j) f -> i q p (j f)", p=P, q=2, j=G)

            def one(view, i):
                return view[bass.ds(i, 1)] if not isinstance(i, int) else view[i:i + 1]

            def load_idx(i, q):
                at = bass.ds((2 * i + q) * G, G)
                sp.dma_start(idx_src[:, at], one(src_v, i)[0, q]).then_inc(s_idx[q], 16)
                sp.dma_start(idx_dst[:, at], one(dst_v, i)[0, q]).then_inc(s_idx[q], 16)

            def load_es(i, q):
                sp.dma_start(es[:, q, :, 0, :], one(ea_v, i)[0, q]).then_inc(s_attributes[q], 16)
                sp.dma_start(es[:, q, :, 1, :], one(sh_v, i)[0, q]).then_inc(s_attributes[q], 16)

            def store(i, q):
                sp.wait_ge(s_values, 2 * i + q + 1)
                sp.sem_inc(s_pad, 1)
                sp.dma_start(one(v_v, i)[0, q], vo[:, q, :, :].rearrange("p j f -> p (j f)")).then_inc(s_values_st[q], 16)

            def stored(i):
                for q in range(2):
                    sp.wait_ge(s_values_st[q], 16 * i + 16)
                    sp.sem_inc(s_vfree, 1)

            sp.sem_inc(s_vfree, 2)
            for q in range(2):
                load_idx(0, q)
                load_es(0, q)
            for q in range(2):
                sp.wait_ge(s_idx[q], 32)
                load_idx(1, q)
                sp.wait_ge(s_rest1, q + 1)
                load_es(1, q)

            def refill(i):
                for q in range(2):
                    if within(2 * i + q + 4):
                        sp.wait_ge(s_idx[q], 32 * i + 64)
                        sp.sem_inc(s_pad, 1)
                        load_idx(i + 2, q)
                        sp.wait_ge(s_rest1, 2 * i + q + 3)
                        sp.sem_inc(s_pad, 1)
                        load_es(i + 2, q)
                    store(i, q)
                stored(i)

            with sp.Fori(0, IT - 2) as i:
                refill(i)
            refill(IT - 2)
            refill(IT - 1)

            sp.wait_ge(s_halo, 1)
            sp.wait_ge(s_alpha, 2 * IT + 2)
            dview = bufR[0:CHH, :].bitcast(I32)
            for c in range(CH):
                sp.dma_start(dview[c * H:(c + 1) * H, :], dst[c * CE:(c + 1) * CE].partition_broadcast(H)).then_inc(s_dsts, 16)
                if c < CH - 1:
                    sp.dma_start(dst_s[c * H:(c + 1) * H, :], dst[(c + 1) * CE:(c + 1) * CE + 1].partition_broadcast(H)).then_inc(s_dsts, 16)

            sp.wait_ge(s_flag, 1)
            over = sp.value_load(flag_i[0:1, 0:1], min_val=0, max_val=1)
            sp.wait_ge(s_sub, 1)
            with sp.Fori(0, SB // NV) as i:
                for u in range(0, NV, 2):
                    c = sp.value_load(walkB[0:1, 0, bass.ds(NV * i + u, 1)], min_val=0, max_val=NC - 1)
                    sp.wait_ge(s_weighted, NV * i + u + 1)
                    sp.sem_inc(s_pad, 1)
                    sp.dma_start(v_ring[:, u, :], v_c[bass.ds(c, 1)][0]).then_inc(s_values_ld[u], 16)

            def residue(n):
                w0, nw = NA[n % NGRP]
                with sp.If(over):
                    sp.wait_ge(s_main, n + 1)
                    sp.dma_start(adj_sb[n % 2][:, 0:nw, :], adj_res[w0:w0 + nw].rearrange("w p c -> p w c")).then_inc(s_adj_res_ld, 16)
                sp.sem_inc(s_pad, 1)

            for n, (l, d) in enumerate(LG):
                w0, nw = NA[d]
                if n >= 2:
                    sp.wait_ge(s_aggregated, n - 1)
                elif n == 0:
                    sp.wait_ge(s_summed, SB + 4)
                else:
                    sp.wait_ge(s_ready, 1)
                sp.dma_start(adj_sb[n % 2][:, 0:nw, :], adj[w0:w0 + nw].rearrange("w p c -> p w c")).then_inc(s_adj_ld[n % 2], 16)
                if n >= 1:
                    residue(n - 1)
            residue(len(LG) - 1)
            sp.wait_ge(s_ready, 2)
            sp.dma_start(out.rearrange("(b p) f -> p b f", p=P),
                         tmp2.rearrange("p (b f) -> p b f", b=NB)).then_inc(s_out, 16)
            sp.wait_ge(s_out, 16)

        @block.gpsimd
        def _(pool):
            pool.memset(ident[:, :], 0.0).then_inc(s_ident0, 1)
            pool.wait_ge(s_ident0, 1)
            pool.affine_select(out=ident[:, :], in_=ident[:, :], compare_op=ALU.not_equal, fill=1.0, base=0,
                               pattern=[[-1, 128]], channel_multiplier=1).then_inc(s_ident, 1)
            pool.iota(iota_i[:, :], pattern=[[1, P]], base=0, channel_multiplier=0).then_inc(s_iota, 1)
            pool.iota(iota_pair_i[:, :], pattern=[[1, PW]], base=0, channel_multiplier=0).then_inc(s_iota, 1)
            for k, q in enumerate((QA, QB)):
                pool.iota(step_i[k][:, :], pattern=[[q, SK]], base=0, channel_multiplier=1).then_inc(s_iota, 1)
            pool.iota(chunk_i[:, :], pattern=[[1, NC]], base=0, channel_multiplier=0).then_inc(s_iota, 1)
            pool.iota(dummy_i[:, :], pattern=[[0, SA // DUMMY], [1, DUMMY]], base=NWA, channel_multiplier=0).then_inc(s_iota, 1)
            pool.wait_ge(s_steps, 1)
            for rws, table, ci in ((srcR, src, c_i[0]), (dstR, dst, c_i[0]), (dstRB, dst, c_i[1])):
                for k in range(SK):
                    pool.indirect_dma_start(rws[:, k, :].bitcast(I32), None, table.rearrange("(c e) -> c e", e=GE),
                                            bass.IndirectOffsetOnAxis(ap=ci[:, k:k + 1], axis=0)).then_inc(s_rows, 16)
            pool.wait_ge(s_qst, 16)
            def gather_x(q, g):
                pool.wait_ge(s_idx_x, g + 1)
                pool.sem_inc(s_pad, 1)
                for j in range(G):
                    pool.indirect_dma_start(xg[:, q * G + j, :], None, x,
                                            bass.IndirectOffsetOnAxis(ap=idx_slot[:, q, j:j + 1], axis=0)).then_inc(s_x_rows[q], 16)

            def gather_q(q, g):
                pool.wait_ge(s_idx_q, g + 1)
                pool.sem_inc(s_pad, 1)
                for j in range(G):
                    pool.indirect_dma_start(qg[:, q * G + j, :], None, q_table,
                                            bass.IndirectOffsetOnAxis(ap=idx_slot[:, q, G + j:G + j + 1], axis=0)).then_inc(s_q_rows[q], 16)

            gather_x(0, 0)
            gather_x(1, 1)
            with pool.Fori(0, IT - 1) as i:
                for q in range(2):
                    gather_x(q, 2 * i + q + 2)
                    gather_q(q, 2 * i + q)
            for q in range(2):
                gather_q(q, NC - 2 + q)
            pool.sem_inc(s_weighted, NV)
            pool.wait_ge(s_eTc, CG // 2 + CG)
            with pool.Fori(0, SB // NV) as i:
                cs = [pool.value_load(walkB[0:1, 0, bass.ds(NV * i + u, 1)], min_val=0, max_val=NC - 1) for u in range(NV)]
                for u in range(NV):
                    pool.wait_ge(s_product, NV * i + u + 1)
                    pool.wait_ge(s_values_ld[u], 16 * i + 16)
                    e = alpha_em[:, bass.ds(cs[u] * (G * H), G * H)].rearrange("p (j h) -> p j h", j=G)
                    pool.tensor_tensor(gs[:, u % 4, :, :].rearrange("p j (h v) -> p j h v", h=H),
                                       v_ring[:, u, :].rearrange("p (j h v) -> p j h v", j=G, h=H),
                                       e.unsqueeze(3).to_broadcast([P, G, H, V1]), ALU.mult).then_inc(s_weighted, 1)

        @block.scalar
        def _(act):
            for s in (s_sTc, s_xTc, s_hidc, s_radc):
                act.sem_inc(s, 2)
            act.wait_ge(s_wangT, 1)
            act.copy(W_src[:, 1:3, :], bank[7][0:A, 0:2 * D].rearrange("p (w f) -> p w f", w=2)).then_inc(s_wang, 1)
            for k, (g, m) in enumerate(NG):
                act.wait_ge(s_xnT, k + 1)
                act.copy(fT[:, g * P:(g + m) * P], bank[k % 2][:, 0:m * P]).then_inc(s_xn, 1)
            for k, (g, m) in enumerate(NG):
                act.wait_ge(s_qT, k + 1)
                act.copy(h1T[0:DK, g * P:(g + m) * P], bank[2 + k % 2][0:DK, 0:m * P]).then_inc(s_qTc, 1)
            def index_x(i, q, g):
                act.wait_ge(s_idx[q], 32 * i + 32)
                act.wait_ge(s_turned, two_ago(g))
                act.copy(idx_slot[:, q, 0:G], idx_src[:, bass.ds(g * G, G)]).then_inc(s_idx_x, 1)

            def index_q(i, q, g):
                act.wait_ge(s_idx[q], 32 * i + 32)
                act.wait_ge(s_alpha, two_ago(g))
                act.copy(idx_slot[:, q, G:2 * G], idx_dst[:, bass.ds(g * G, G)]).then_inc(s_idx_q, 1)

            index_x(0, 0, 0)
            index_x(0, 1, 1)
            index_q(0, 0, 0)

            def copies(g, q):
                act.wait_ge(s_turned, done(g))
                act.wait_ge(s_hidden, two_ago(g))
                act.copy(sT[:, q, :, :].rearrange("p w (j e) -> p (w j) e", j=G), turned[:, :, 0:P]).then_inc(s_sTc, 1)
                act.wait_ge(s_gated, two_ago(g))
                act.copy(xT[:, q, :], bank[0][:, 0:GE]).then_inc(s_xTc, 1)

            def part1(i, q, g):
                act.wait_ge(s_attributes[q], 32 * i + 32)
                act.wait_ge(s_turned, two_ago(g))
                act.copy(es_parts[:, q, :, 0:3, :],
                         es[:, q, :, :, :].rearrange("p j w a -> p (j w) a").unsqueeze(2).to_broadcast([P, 2 * G, 3, A])).then_inc(s_part1, 1)

            def part2(q, g):
                act.wait_ge(s_rest1, g + 1)
                act.copy(es_parts[:, q, :, 3:5, :],
                         es_rest[:, q, :, :].unsqueeze(2).to_broadcast([P, 2 * G, 2, A])).then_inc(s_part2, 1)

            def relu(g, q):
                act.wait_ge(s_hidden, done(g))
                act.wait_ge(s_edges, two_ago(g))
                act.activation(hidT[:, q, :], bank[1][:, 0:GE], ACT.Relu, bias=b1c[:, 0:1]).then_inc(s_hidc, 1)

            def rads(g, q):
                act.wait_ge(s_edges, done(g))
                act.wait_ge(s_alpha, two_ago(g))
                for b in range(2):
                    r = act.copy(rad[:, q, 2 * b:2 * b + 2, :], pair_bank(b)[:, :, 0:DK + D])
                r.then_inc(s_radc, 1)

            over = {}

            def put(n, k):
                w = act.value_load(goal[0:1, bass.ds(n, 1)], min_val=0, max_val=NWA + DUMMY - 1)
                act.wait_ge(s_narrowed, n + 3)
                act.sem_inc(s_pad, 1)
                act.dma_start(adj[bass.ds(w, 1)][0], cnt_bf[:, k, :]).then_inc(s_adj_st[k], 16)
                with act.If(over["reg"]):
                    act.wait_ge(s_dropped, n + 1)
                    act.sem_inc(s_pad, 1)
                    act.dma_start(adj_res[bass.ds(w, 1)][0], cnt_res[:, k, :]).then_inc(s_adj_res_st[k], 16)
                act.sem_inc(s_pad, 1)

            act.wait_ge(s_goal, 1)
            act.wait_ge(s_flag, 1)
            over["reg"] = act.value_load(flag_i[0:1, 0:1], min_val=0, max_val=1)
            act.sem_inc(s_narrowed, 2)
            act.wait_ge(s_cnt0, 1)
            for k in range(2):
                act.dma_start(adj[NWA + 2 + k], cnt_bf[:, k, :]).then_inc(s_adj_st[k], 16)
                act.dma_start(adj_res[NWA + 2 + k], cnt_res[:, k, :]).then_inc(s_adj_res_st[k], 16)

            def slot(i, q):
                g = 2 * i + q
                first = isinstance(g, int) and g == 0
                if within(g + 3):
                    index_x(i + 1 + q, 1 - q, g + 3)
                if within(g + 1):
                    index_q(i + q, 1 - q, g + 1)
                if within(g + 3):
                    part1(i + 1 + q, 1 - q, g + 3)
                if within(g + 1):
                    relu(g + 1, 1 - q)
                if not first:
                    narrow_put(2 * g - 2, 0, g - 1)
                if within(g + 3):
                    part2(1 - q, g + 3)
                rads(g, q)
                if within(g + 2):
                    copies(g + 2, q)
                if not first:
                    narrow_put(2 * g - 1, 1, g - 1)

            def narrow_put(n, k, m):
                act.wait_ge(s_taken, n + 3)
                act.wait_ge(s_adj_st[k], 16 * m + 16)
                act.copy(cnt_bf[:, k, :], cnt[:, k, :]).then_inc(s_narrowed, 1)
                put(n, k)

            for q in range(2):
                part1(0, q, q)
                part2(q, q)
            copies(0, 0)
            relu(0, 0)
            index_x(1, 0, 2)
            part1(1, 0, 2)
            copies(1, 1)
            part2(0, 2)
            for q in range(2):
                slot(0, q)
            with act.Fori(1, IT - 2) as i:
                for q in range(2):
                    slot(i, q)
            for i in (IT - 2, IT - 1):
                for q in range(2):
                    slot(i, q)
            for k in range(2):
                narrow_put(SA - 2 + k, k, NC - 1)
            for k in range(2):
                act.wait_ge(s_adj_st[k], 16 * NC + 16)
                act.wait_ge(s_adj_res_st[k], 16)
            with act.If(over["reg"]):
                for k in range(2):
                    act.wait_ge(s_adj_res_st[k], 16 * NC + 16)
                act.sem_inc(s_pad, 1)
            act.sem_inc(s_afree, 1)

            for k in range(0, CG):
                if k % 2 == 1:
                    act.wait_ge(s_alT, k + 1)
                    act.copy(al[:, k * GE:(k + 1) * GE].rearrange("c (p j) -> c j p", j=G),
                             bank[k % 2][0:CHH, 0:GE].rearrange("c (j p) -> c j p", j=G)).then_inc(s_alc, 1)
            act.wait_ge(s_sub, 1)
            act.activation(al, al, ACT.Exp).then_inc(s_exp, 1)
            with act.Fori(0, SB // NV) as i:
                for u in range(1, NV, 2):
                    c = act.value_load(walkB[0:1, 0, bass.ds(NV * i + u, 1)], min_val=0, max_val=NC - 1)
                    act.wait_ge(s_weighted, NV * i + u + 1)
                    act.sem_inc(s_pad, 1)
                    act.dma_start(v_ring[:, u, :], v_c[bass.ds(c, 1)][0]).then_inc(s_values_ld[u], 16)
            def root(n, sd, var, scale):
                act.wait_ge(s_var, n)
                act.activation(sd, var, ACT.Sqrt, bias=eps[0:sd.shape[0], 0:1], scale=scale).then_inc(s_root, 1)

            for k, (g, m) in enumerate(NG):
                act.wait_ge(s_nfT, k + 1)
                act.copy(fT[:, g * P:(g + m) * P], bank[k % 2][:, 0:m * P]).then_inc(s_nfc, 1)
            root(1, st25[:, 2, :], st25[:, 1, :], 1.0 / D)
            for k, (g, m) in enumerate(NG):
                act.wait_ge(s_nfT, NGRP + k + 1)
                act.copy(fT[:, g * P:(g + m) * P], bank[k % 2][:, 0:m * P]).then_inc(s_nfc, 1)

            def split(n0, of, wait):
                for k in range(NGRP + 1):
                    if k < NGRP:
                        g, m = NG[k]
                        wait(k)
                        act.copy(parts[:, g:g + m, 0, :], of(k, g, m)).then_inc(s_high, 1)
                    if k >= 1:
                        g, m = NG[k - 1]
                        act.wait_ge(s_rest, n0 + k)
                        act.copy(parts[:, g:g + m, 1, :],
                                 rest[:, (n0 + k - 1) % 2, 0:m * D].rearrange("p (b f) -> p b f", b=m)).then_inc(s_mid, 1)

            split(0, lambda k, g, m: x_nm[:, g:g + m, :], lambda k: act.wait_ge(s_ready, 1))
            for l in range(L):
                for k, (g, m) in enumerate(NG):
                    act.wait_ge(s_mlp1, l * NGRP + k + 1)
                    act.activation(h1T[:, g * P:(g + m) * P], bank[2 + k % 2][:, 0:m * P], ACT.Relu,
                                   bias=Lvec[:, 0, l:l + 1]).then_inc(s_mlp1c, 1)
                    act.wait_ge(s_mlp2, l * NGRP + k + 1)
                    act.activation(h2T[:, g * P:(g + m) * P], bank[4 + k % 2][:, 0:m * P], ACT.Relu,
                                   bias=Lvec[:, 1, l:l + 1]).then_inc(s_mlp2c, 1)
                root(l + 2, st1[:, 3:4], bn2[:, 1:2], 1.0)
                if l < L - 1:
                    split((l + 1) * NGRP, back_rows, lambda k: act.wait_ge(s_backT, l * NGRP + k + 1))
            root(L + 2, st25[:, 2, :], st25[:, 1, :], 1.0 / D)

        @block.tensor
        def _(pe):
            for s in (s_turned, s_hidden, s_edges):
                pe.sem_inc(s, 2)
            pe.sem_inc(s_product, 4)
            pe.sem_inc(s_counted, 2)
            pe.wait_ge(s_ident, 1)
            pe.wait_ge(s_start, 1)
            pe.matmul(bank[5][0:QA, 0:2 * NC], lhsT=ones[:, 0:QA], rhs=start_row[:, :, :].rearrange("o w c -> o (w c)"),
                      start=True, stop=True).then_inc(s_startB, 1)
            pe.wait_ge(s_degT, 1)
            pe.transpose(bank[6][0:1, 0:100], flag_col[:, :], ident[0:100, 0:100]).then_inc(s_flagT, 1)
            pe.wait_ge(s_weights, 16 * (11 + H))
            for w in range(2):
                mm = pe.transpose(bank[7][0:A, w * D:(w + 1) * D], Wang_sb[:, w, :], ident[:, :])
            mm.then_inc(s_wangT, 1)
            pe.wait_ge(s_x_loaded, 16)
            for k, (g, m) in enumerate(NG):
                if k >= 2:
                    pe.wait_ge(s_xn, k - 1)
                for b in range(m):
                    mm = pe.transpose(bank[k % 2][:, b * P:(b + 1) * P], x_nm[:, g + b, :], ident[0:P, 0:P])
                mm.then_inc(s_xnT, 1)
            for k, (g, m) in enumerate(NG):
                pe.wait_ge(s_xn, k + 1)
                if k >= 2:
                    pe.wait_ge(s_qTc, k - 1)
                pe.matmul(bank[2 + k % 2][0:DK, 0:m * P], lhsT=Wq_sb[:, :], rhs=fT[:, g * P:(g + m) * P],
                          start=True, stop=True).then_inc(s_qT, 1)
            pe.wait_ge(s_qTc, len(NG))
            for k, g in enumerate(range(0, NB, 8)):
                if k >= 1:
                    pe.wait_ge(s_qnc, k)
                for b in range(g, min(g + 8, NB)):
                    mm = pe.matmul(bank[4][0:P, (b - g) * DK:(b - g + 1) * DK], lhsT=h1T[0:DK, b * P:(b + 1) * P],
                                   rhs=Wdot_bd[:, :], start=True, stop=True)
                mm.then_inc(s_qn, 1)
            pe.wait_ge(s_wst, 16 * TERMS)
            pe.wait_ge(s_identb, 1)
            n = 0
            for tab, q in ((dlA, QA), (srcR, QA), (dstRB, QB)):
                pe.wait_ge(s_rowsF, 1 if q == QA else 2)
                for k in range(SK):
                    if n >= 2:
                        pe.wait_ge(s_tab, n - 1)
                    for j in range(G):
                        mm = pe.transpose(bank[6 + n % 2][0:P, j * q:(j + 1) * q], tab[:, k, j:GE:G], ident[0:q, 0:q])
                    mm.then_inc(s_tabT, 1)
                    n += 1
            pe.wait_ge(s_tab, 3 * SK)
            pe.wait_ge(s_keepr, 1)
            pe.matmul(bank[6][0:P, 0:SA], lhsT=ones[:, 0:P], rhs=keep_row[:, :], start=True, stop=True).then_inc(s_keepT, 1)
            pe.wait_ge(s_goal, 1)
            def turn(i, q, g, first=False):
                pe.wait_ge(s_x_rows[q], 16 * G * i + 16 * G)
                pe.wait_ge(s_part3, g + 1)
                pe.wait_ge(s_xTc, one_ago(g))
                if not first:
                    pe.wait_ge(s_taken, 2 * g - 2)
                pe.wait_ge(s_hidc, one_ago(g))
                for w in range(2):
                    for j in range(G):
                        pe.transpose(turned[:, w * G + j, 0:P], es_parts[:, q, 2 * j + w, :, :].rearrange("p t a -> p (t a)"),
                                     ident_bf[0:P, 0:P])
                for j in range(G):
                    mm = pe.transpose(bank[0][:, j * P:(j + 1) * P], xg[:, q * G + j, :], ident[0:P, 0:P])
                mm.then_inc(s_turned, 1)

            def features(q, g):
                pe.wait_ge(s_sTc, done(g))
                pe.wait_ge(s_gated, one_ago(g))
                for w in range(2):
                    pe.matmul(bank[2 + w][:, 0:GE], lhsT=W_st[:, 1 + w, :], rhs=sT[:, q, 1, :], start=True, stop=True)
                pe.wait_ge(s_hidc, one_ago(g))
                pe.matmul(bank[1][:, 0:GE], lhsT=W_st[:, 0, :], rhs=sT[:, q, 0, :], start=True, stop=True).then_inc(s_hidden, 1)

            def edges(q, g):
                pe.wait_ge(s_gated, done(g))
                pe.wait_ge(s_hidc, done(g))
                pe.wait_ge(s_alpha, one_ago(g))
                pe.wait_ge(s_radc, one_ago(g))
                for j in range(G):
                    e = slice(j * P, (j + 1) * P)
                    pe.matmul(pair_bank(j // 2)[:, j % 2, 0:DK + D], lhsT=hidT[:, q, e], rhs=W2c[:, :], start=True, stop=True)
                    pe.matmul(pair_bank(j // 2)[:, j % 2, DK + D:], lhsT=yk[:, q, e], rhs=Wlk[:, :], start=True, stop=True)
                    mm = pe.matmul(bank[6][0:P, j * D:(j + 1) * D], lhsT=yv[:, q, e], rhs=Wlv[:, :], start=True, stop=True)
                mm.then_inc(s_edges, 1)

            def count(n, k, x_copied=0):
                pe.wait_ge(s_marked, n + 1)
                pe.wait_ge(s_taken, n + 1)
                if k == 1:
                    pe.wait_ge(s_xTc, x_copied)
                for j in range(G):
                    mm = pe.matmul(bank[4 - 4 * k][0:P, 0:PW], lhsT=ohl[:, k, j, :], rhs=ohp[:, k, j, :], start=(j == 0), stop=(j == G - 1))
                mm.then_inc(s_counted, 1)

            def slot(i, q):
                g = 2 * i + q
                if within(g + 1):
                    features(1 - q, g + 1)
                edges(q, g)
                if within(g + 2):
                    turn(i + 1, q, g + 2)
                count(2 * g, 0)
                count(2 * g + 1, 1, done(g + 2) if within(g + 2) else done(NC - 1))

            turn(0, 0, 0, True)
            features(0, 0)
            turn(0, 1, 1, True)
            with pe.Fori(0, IT - 2) as i:
                for q in range(2):
                    slot(i, q)
            for i in (IT - 2, IT - 1):
                for q in range(2):
                    slot(i, q)

            pe.wait_ge(s_relaid, 1)
            for k in range(CG):
                if k >= 2:
                    pe.wait_ge(s_alc if k % 2 else s_eTc, k // 2)
                for j in range(G):
                    mm = pe.transpose(bank[k % 2][0:CHH, j * P:(j + 1) * P], relaid[:, (k * G + j) * CHH:(k * G + j + 1) * CHH], ident[0:P, 0:P])
                mm.then_inc(s_alT, 1)
            pe.wait_ge(s_endsd, 1)
            for w in range(4):
                mm = pe.transpose(bank[2][0:1, w * CHH:(w + 1) * CHH], ends[:, w:w + 1], ident[0:CHH, 0:CHH])
            mm.then_inc(s_endT, 1)
            pe.wait_ge(s_rowE, 1)
            for w in range(2):
                mm = pe.matmul(bank[3][0:CHH, w:w + 1], lhsT=row_c[:, w, :], rhs=ones[:, 0:1], start=True, stop=True)
            mm.then_inc(s_carT, 1)
            pe.wait_ge(s_exp, 1)
            for k in range(CG):
                if k >= 2:
                    pe.wait_ge(s_eTc, CG // 2 + k - 1)
                for j in range(G):
                    mm = pe.transpose(bank[4 + k % 2][0:P, j * CHH:(j + 1) * CHH], al[:, k * GE + j:(k + 1) * GE:G], ident[0:CHH, 0:CHH])
                mm.then_inc(s_eT, 1)
            with pe.Fori(0, SB // 4) as i:
                for u in range(4):
                    st = 4 * i + u
                    pe.wait_ge(s_onehot, st + 1)
                    pe.wait_ge(s_weighted, st + NV + 1)
                    pe.wait_ge(s_summed, st + 1)
                    for j in range(G):
                        mm = pe.matmul(bank[u][0:P, 0:W], lhsT=oh[:, u, j, :], rhs=gs[:, u, j, :], start=(j == 0), stop=(j == G - 1))
                    mm.then_inc(s_product, 1)

            pe.wait_ge(s_divided, 1)
            for k, (g, m) in enumerate(NG):
                if k >= 2:
                    pe.wait_ge(s_nfc, k - 1)
                for b in range(m):
                    mm = pe.transpose(bank[k % 2][:, b * P:(b + 1) * P], tmp[:, (g + b) * D:(g + b + 1) * D], ident[0:P, 0:P])
                mm.then_inc(s_nfT, 1)
            pe.wait_ge(s_nfc, NGRP)
            pe.wait_ge(s_node_weights, 16 * 7)
            for k, (g, m) in enumerate(NG):
                if k >= 2:
                    pe.wait_ge(s_normed, k - 1)
                for b in range(m):
                    mm = pe.matmul(bank[2 + k % 2][0:P, b * D:(b + 1) * D], lhsT=fT[:, (g + b) * P:(g + b + 1) * P], rhs=Wout_sb[:, :],
                                   start=True, stop=True)
                mm.then_inc(s_qn, 1)
            pe.wait_ge(s_ready, 1)
            for k, (g, m) in enumerate(NG):
                if k >= 2:
                    pe.wait_ge(s_nfc, NGRP + k - 1)
                for b in range(m):
                    mm = pe.transpose(bank[k % 2][:, b * P:(b + 1) * P], x_nm[:, g + b, :], ident[0:P, 0:P])
                mm.then_inc(s_nfT, 1)
            pe.wait_ge(s_nfc, 2 * NGRP)
            pe.wait_ge(s_flag, 1)
            over = pe.value_load(flag_i[0:1, 0:1], min_val=0, max_val=1)

            def products(n, first):
                d = n % NGRP
                o = bank[n % 2][:, 0:NA[d][1] * WA]
                cols = adj_sb[n % 2][:, 0:NA[d][1], :].rearrange("p w (b n) -> p b w n", b=NB)
                for b in range(NB):
                    for w in range(3):
                        mm = pe.matmul(o, lhsT=parts[:, b, w, :], rhs=cols[:, b], start=first and b == 0 and w == 0,
                                       stop=False)
                return mm

            def close(n):
                d = n % NGRP
                return pe.matmul(bank[n % 2][:, 0:NA[d][1] * WA], lhsT=zero_bf[0:P, :],
                                 rhs=adj_sb[n % 2][:, 0:NA[d][1], 0:WA], start=False, stop=True)

            def mlp1(l, k):
                g, m = NG[k]
                pe.wait_ge(s_h, l * NGRP + k + 1)
                if k >= 2:
                    pe.wait_ge(s_mlp1c, l * NGRP + k - 1)
                pe.matmul(bank[2 + k % 2][:, 0:m * P], lhsT=LW1[:, l, :], rhs=fT[:, g * P:(g + m) * P], start=True, stop=True).then_inc(s_mlp1, 1)

            def mlp2(l, k):
                g, m = NG[k]
                pe.wait_ge(s_mlp1c, l * NGRP + k + 1)
                if k >= 2:
                    pe.wait_ge(s_mlp2c, l * NGRP + k - 1)
                pe.matmul(bank[4 + k % 2][:, 0:m * P], lhsT=LW2[:, l, :], rhs=h1T[:, g * P:(g + m) * P], start=True, stop=True).then_inc(s_mlp2, 1)

            for l in range(L):
                pe.wait_ge(s_parts, (l + 1) * NGRP)
                for d in range(NGRP):
                    n = l * NGRP + d
                    pe.wait_ge(s_adj_ld[n % 2], 16 * (n // 2) + 16)
                    if n >= 2:
                        pe.wait_ge(s_h, n - 1)
                    products(n, True).then_inc(s_main, 1)
                    with pe.If(over):
                        pe.wait_ge(s_adj_res_ld, 16 * n + 16)
                        products(n, False)
                    close(n).then_inc(s_aggregated, 1)
                    if d >= 1:
                        mlp1(l, d - 1)
                    if d >= 2:
                        mlp2(l, d - 2)
                mlp1(l, NGRP - 1)
                mlp2(l, NGRP - 2)
                mlp2(l, NGRP - 1)
                for k, (g, m) in enumerate(NG):
                    pe.wait_ge(s_normed, NGRP + l * NGRP + k + 1)
                    if k >= 2 and l < L - 1:
                        pe.wait_ge(s_rest, (l + 1) * NGRP + k - 1)
                    elif k >= 2:
                        pe.wait_ge(s_back, k - 1)
                    for b in range(m):
                        mm = pe.transpose(bank[6 + k % 2][0:P, b * D:(b + 1) * D], fT[:, (g + b) * P:(g + b + 1) * P], ident[:, :])
                    mm.then_inc(s_backT, 1)

        @block.vector
        def _(dve):
            chain = [0]

            def link(ins):
                chain[0] += 1
                ins.then_inc(s_chain, 1)
                dve.wait_ge(s_chain, chain[0])

            for s in (s_gated, s_alpha):
                dve.sem_inc(s, 2)
            dve.sem_inc(s_summed, 4)
            dve.sem_inc(s_taken, 2)
            dve.memset(zero_bf[:, :], 0.0)
            dve.memset(loA[:, SA:SA + 1, :], 0.0)
            dve.memset(pairA[:, SA:SA + 1, :], 0.0)
            dve.memset(keep_row[:, :], 0.0)
            dve.memset(deg1, 0.0).then_inc(s_deg0, 1)
            dve.memset(W2c[:, :], 0.0)
            dve.memset(eps[:, :], 1e-5)
            dve.memset(ones[:, :], 1.0)
            dve.memset(Wdot_bd[:, :], 0.0).then_inc(s_zero, 1)
            dve.wait_ge(s_iota, 6)
            dve.tensor_copy(iota_row[:, :], iota_i[:, :])
            dve.tensor_copy(iota_p[:, :], iota_i[:, :])
            dve.tensor_copy(iota_pair[:, :], iota_pair_i[:, :])
            dve.wait_ge(s_first_dst, 16)
            C = 12582912.0

            def window(o, of, size, k):
                link(dve.tensor_scalar(o, of, (size - 1) / 2.0, 1.0 / size, ALU.subtract, ALU.mult))
                link(dve.tensor_scalar(o, o, C, None, ALU.add))
                link(dve.tensor_scalar(o, o, C, None, ALU.subtract))

            for k, size in enumerate((WA, P)):
                window(start_row[:, k, :], first_dst[:, :], size, k)
                link(dve.tensor_tensor(start_row[:, k, :], start_row[:, k, :], chunk_i[:, :], ALU.add))
            dve.sem_inc(s_start, 1)
            dve.wait_ge(s_startB, 1)
            link(dve.tensor_copy(startB, bank[5][0:QA, 0:2 * NC].rearrange("p (w c) -> p w c", w=2)))
            for w, (q, size, last) in enumerate(((QA, WA, NWA + SA), (QB, P, NB - 1))):
                link(dve.tensor_copy(step_f[w][:, :], step_i[w][:, :]))
                for k in range(SK):
                    link(dve.tensor_scalar(junk[0:q, 1:NC], startB[0:q, w, 1:NC], step_f[w][:, k:k + 1], None, ALU.is_le))
                    link(dve.reduce_sum(c_f[w][:, k:k + 1], junk[0:q, 1:NC], axis=AX_X))
                link(dve.tensor_tensor(w_f[w][:, :], step_f[w][:, :], c_f[w][:, :], ALU.subtract))
                link(dve.tensor_scalar(w_min[w][:, :], w_f[w][:, :], float(last), None, ALU.min))
                link(dve.tensor_scalar(wn_f[w][:, :], w_f[w][:, :], float(size), None, ALU.mult))
                link(dve.tensor_copy(c_i[w][:, :], c_f[w][:, :]))
                link(dve.tensor_copy(w_i[w][:, :], w_min[w][:, :]))
            dve.sem_inc(s_steps, 1)
            dve.wait_ge(s_degrees, 48)
            link(dve.tensor_tensor(deg0, deg0.bitcast(I32), deg1.bitcast(I32), ALU.is_equal))
            link(dve.tensor_reduce(flag_col[:, :], deg0, AX_X, ALU.max))
            dve.sem_inc(s_degT, 1)
            dve.wait_ge(s_flagT, 1)
            link(dve.tensor_reduce(flag_f[:, 0:1], bank[6][0:1, 0:100], AX_X, ALU.max))
            link(dve.tensor_copy(flag_i[:, 0:1], flag_f[:, 0:1]))
            dve.sem_inc(s_flag, 1)
            dve.wait_ge(s_wang, 1)
            dve.wait_ge(s_weights, 16 * (11 + H))
            link(dve.tensor_copy(W_parts[:, 0, :, :], W_src[:, :, :]))
            link(dve.tensor_tensor(W_rest[:, :, :], W_src[:, :, :], W_parts[:, 0, :, :], ALU.subtract))
            link(dve.tensor_copy(W_parts[:, 1, :, :], W_rest[:, :, :]))
            link(dve.tensor_tensor(W_parts[:, 2, :, :], W_rest[:, :, :], W_parts[:, 1, :, :], ALU.subtract))
            dve.sem_inc(s_wparts, 1)
            dve.wait_ge(s_ident, 1)
            dve.tensor_copy(ident_bf[:, :], ident[:, :]).then_inc(s_identb, 1)
            for k, g in enumerate(range(0, NB, 8)):
                m = min(8, NB - g)
                dve.wait_ge(s_qn, k + 1)
                dve.tensor_copy(qn[:, g * DK:(g + m) * DK], bank[4][0:P, 0:m * DK]).then_inc(s_qnc, 1)
            dve.wait_ge(s_rows, 16 * 3 * SK)
            for k in range(SK):
                link(dve.tensor_scalar(dlA[:, k, :], dstR[:, k, :].bitcast(I32), wn_f[0][:, k:k + 1], None, ALU.subtract))
                link(dve.tensor_scalar(dstRB[:, k, :], dstRB[:, k, :].bitcast(I32), wn_f[1][:, k:k + 1], None, ALU.subtract))
            window(hiA, srcR.bitcast(I32), P, 0)
            link(dve.scalar_tensor_tensor(out=srcR, in0=hiA, scalar=-float(P), in1=srcR.bitcast(I32), op0=ALU.mult, op1=ALU.add))
            link(dve.tensor_scalar(okA, dlA, 0.0, None, ALU.is_ge))
            link(dve.scalar_tensor_tensor(out=okA, in0=dlA, scalar=float(WA), in1=okA, op0=ALU.is_lt, op1=ALU.mult))
            link(dve.scalar_tensor_tensor(out=dlA, in0=hiA, scalar=float(WA), in1=dlA, op0=ALU.mult, op1=ALU.add))
            link(dve.scalar_tensor_tensor(out=dlA, in0=dlA, scalar=1.0, in1=okA, op0=ALU.add, op1=ALU.mult))
            link(dve.tensor_scalar(dlA, dlA, 1.0, None, ALU.subtract))
            dve.sem_inc(s_rowsF, 2)
            n = 0
            for tab, q in ((pairA, QA), (loA, QA), (dstB, QB)):
                for k in range(SK):
                    dve.wait_ge(s_tabT, n + 1)
                    dve.tensor_copy(tab[:, k * q:(k + 1) * q, :].rearrange("p s j -> p j s"),
                                    bank[6 + n % 2][0:P, 0:G * q].rearrange("p (j s) -> p j s", j=G)).then_inc(s_tab, 1)
                    n += 1
            dve.wait_ge(s_walk, 48)
            link(dve.tensor_tensor(keep_row[:, 1:SA], walkA[:, 1:SA], walkA[:, 0:SA - 1], ALU.is_equal))
            dve.sem_inc(s_keepr, 1)
            link(dve.tensor_copy(goal[:, :], dummy_i[:, :]))
            late, ends_here = start_row[:, :, :].rearrange("o w c -> o (w c)")[:, 0:RA], junk_row[:, 0:RA]
            link(dve.tensor_tensor(late, walkA[:, 0:RA], walkA[:, 1:RA + 1], ALU.not_equal))
            link(dve.tensor_tensor(ends_here, walkA[:, 0:RA], dummy_i[:, 0:RA], ALU.subtract))
            link(dve.tensor_tensor(ends_here, ends_here, late, ALU.mult))
            link(dve.tensor_tensor(goal[:, 0:RA], ends_here, dummy_i[:, 0:RA], ALU.add))
            dve.wait_ge(s_keepT, 1)
            link(dve.tensor_copy(keep[:, :], bank[6][0:P, 0:SA]))
            dve.sem_inc(s_goal, 1)
            def gated(q, g):
                dve.wait_ge(s_xTc, done(g))
                dve.wait_ge(s_hidden, done(g))
                dve.wait_ge(s_edges, two_ago(g))
                dve.tensor_tensor(yk[:, q, :], xT[:, q, :], bank[2][:, 0:GE], ALU.mult)
                dve.tensor_tensor(yv[:, q, :], xT[:, q, :], bank[3][:, 0:GE], ALU.mult).then_inc(s_gated, 1)

            def finish(i, q, g):
                dve.wait_ge(s_radc, done(g))
                for b in range(2):
                    r = dve.tensor_tensor(kt[:, q, 2 * b:2 * b + 2, :], rad[:, q, 2 * b:2 * b + 2, 0:DK],
                                          pair_bank(b)[:, :, DK + D:], ALU.mult)
                r.then_inc(s_k, 1)
                dve.wait_ge(s_vfree, g + 1)
                dve.tensor_tensor(vo[:, q, :, :].rearrange("p j (h v) -> p j h v", h=H)[:, :, :, 0:D // H],
                                  rad[:, q, :, DK:].rearrange("p j (h v) -> p j h v", h=H),
                                  bank[6][0:P, :].rearrange("p (j h v) -> p j h v", j=G, h=H), ALU.mult).then_inc(s_values, 1)
                dve.wait_ge(s_q_rows[q], 16 * G * i + 16 * G)
                dve.wait_ge(s_k, g + 1)
                dve.tensor_tensor(kt[:, q, :, :], kt[:, q, :, :], qg[:, q * G:(q + 1) * G, :], ALU.mult).then_inc(s_qk, 1)
                dve.wait_ge(s_qk, g + 1)
                dve.reduce_sum(alpha_em[:, bass.ds(g * (G * H), G * H)],
                               kt[:, q, :, :].rearrange("p j (h k) -> p (j h) k", h=H), axis=AX_X).then_inc(s_alpha, 1)

            def mark(n, k):
                dve.wait_ge(s_counted, n + 1)
                for j in range(G):
                    dve.tensor_scalar(ohl[:, k, j, :], iota_p[0:P, :], loA[:, bass.ds(n, 1), j], None, ALU.is_equal)
                    m = dve.tensor_scalar(ohp[:, k, j, :], iota_pair[0:P, :], pairA[:, bass.ds(n, 1), j], None, ALU.is_equal)
                m.then_inc(s_marked, 1)

            def take(n, k):
                dve.wait_ge(s_counted, n + 3)
                dve.wait_ge(s_narrowed, n + 1)
                dve.wait_ge(s_taken, n + 2)
                dve.scalar_tensor_tensor(out=cnt[:, k, :], in0=cnt[:, 1 - k, :], scalar=keep[:, bass.ds(n, 1)],
                                         in1=bank[4 - 4 * k][0:P, 0:PW], op0=ALU.mult, op1=ALU.add).then_inc(s_taken, 1)

            def drop(*steps):
                with dve.If(over):
                    for n, k, m in steps:
                        dve.wait_ge(s_narrowed, n + 3)
                        dve.wait_ge(s_taken, n + 3)
                        dve.wait_ge(s_adj_res_st[k], 16 * m + 16)
                        dve.tensor_tensor(cnt_res[:, k, :], cnt[:, k, :], cnt_bf[:, k, :], ALU.subtract).then_inc(s_dropped, 1)
                dve.sem_inc(s_pad, 1)

            over = dve.value_load(flag_i[0:1, 0:1], min_val=0, max_val=1)
            link(dve.memset(vo, 1.0))
            link(dve.memset(cnt, 0.0))
            dve.memset(cnt_bf, 0.0)
            link(dve.memset(cnt_res, 0.0))
            dve.sem_inc(s_cnt0, 1)
            def rest1(q, g):
                dve.wait_ge(s_part1, g + 1)
                dve.tensor_tensor(es_rest[:, q, :, :], es[:, q, :, :, :].rearrange("p j w a -> p (j w) a"),
                                  es_parts[:, q, :, 0, :], ALU.subtract).then_inc(s_rest1, 1)

            def part3(q, g):
                dve.wait_ge(s_part2, g + 1)
                dve.tensor_tensor(es_parts[:, q, :, 5, :], es_rest[:, q, :, :], es_parts[:, q, :, 3, :],
                                  ALU.subtract).then_inc(s_part3, 1)

            def slot(i, q):
                g = 2 * i + q
                first = isinstance(g, int) and g == 0
                if not first:
                    take(2 * g - 2, 0)
                    if isinstance(g, int) and g == 1:
                        drop((0, 0, 0))
                    else:
                        drop((2 * g - 3, 1, g - 2), (2 * g - 2, 0, g - 1))
                    take(2 * g - 1, 1)
                if within(g + 1):
                    gated(1 - q, g + 1)
                if within(g + 3):
                    rest1(1 - q, g + 3)
                mark(2 * g, 0)
                mark(2 * g + 1, 1)
                if within(g + 3):
                    part3(1 - q, g + 3)
                finish(i, q, g)

            for q in range(2):
                rest1(q, q)
                part3(q, q)
            gated(0, 0)
            rest1(0, 2)
            part3(0, 2)
            for q in range(2):
                slot(0, q)
            with dve.Fori(1, IT - 2) as i:
                for q in range(2):
                    slot(i, q)
            for i in (IT - 2, IT - 1):
                for q in range(2):
                    slot(i, q)
            take(SA - 2, 0)
            drop((SA - 3, 1, NC - 2), (SA - 2, 0, NC - 1))
            take(SA - 1, 1)
            drop((SA - 1, 1, NC - 1))

            dve.wait_ge(s_alpha, 2 * IT + 2)
            dve.wait_ge(s_afree, 1)
            dve.wait_ge(s_vfree, 2 * IT + 2)
            dve.wait_ge(s_counted, SA + 2)
            dve.tensor_copy(relaid.rearrange("p (t c h) -> p t c h", c=CH, h=H),
                            alpha_em[:, :].rearrange("p (c t h) -> p t c h", c=CH, h=H)).then_inc(s_relaid, 1)
            for k in range(0, CG, 2):
                dve.wait_ge(s_alT, k + 1)
                dve.tensor_copy(al[:, k * GE:(k + 1) * GE].rearrange("c (p j) -> c j p", j=G),
                                bank[0][0:CHH, 0:GE].rearrange("c (j p) -> c j p", j=G)).then_inc(s_eTc, 1)
            FIRST, LAST, INNER, LINK = range(4)
            dve.wait_ge(s_alT, CG)
            dve.memset(dst_s[:, :], -1).then_inc(s_halo, 1)
            dview = bufR[0:CHH, :].bitcast(I32)
            dve.wait_ge(s_dsts, 16 * (2 * CH - 1))
            link(dve.tensor_tensor(pen[:, 1:CE], dview[:, 1:CE], dview[:, 0:CE - 1], ALU.not_equal))
            link(dve.tensor_tensor(pen[:, CE:CE + 1], dst_s[:, :], dview[:, CE - 1:CE], ALU.not_equal))
            link(dve.tensor_scalar(pen[:, 1:CE + 1], pen[:, 1:CE + 1], BIG, None, ALU.mult))
            link(dve.tensor_tensor(ends[:, INNER:INNER + 1], dview[:, 0:1], dview[:, CE - 1:CE], ALU.not_equal))
            link(dve.tensor_scalar(ends[:, INNER:INNER + 1], ends[:, INNER:INNER + 1], BIG, None, ALU.mult))
            link(dve.memset(pen[:, 0:1], 0.0))
            dve.wait_ge(s_alc, CG // 2)
            link(dve.tensor_tensor_scan(run, pen[:, 0:CE], al, BIG, ALU.add, ALU.max))
            link(dve.tensor_tensor_scan(run[:, ::-1], pen[:, CE:0:-1], run[:, ::-1], BIG, ALU.add, ALU.max))
            dve.tensor_copy(ends[:, FIRST:FIRST + 1], run[:, 0:1])
            dve.tensor_copy(ends[:, LAST:LAST + 1], run[:, CE - 1:CE])
            dve.tensor_copy(ends[:, LINK:LINK + 1], pen[:, CE:CE + 1]).then_inc(s_endsd, 1)
            dve.wait_ge(s_endT, 1)
            link(dve.tensor_copy(row_end[:, :, :], bank[2][0:1, 0:4 * CHH].rearrange("o (w c) -> o w c", w=4)))
            link(dve.memset(row_c[:, :, :], BIG))

            def part(row, c):
                return row[:, c * H:(c + 1) * H]

            for f, b in zip(range(1, CH), range(CH - 2, -1, -1)):
                dve.tensor_tensor(part(row_E[:, 0, :], f), part(row_c[:, 0, :], f - 1), part(row_end[:, INNER, :], f - 1), ALU.add)
                link(dve.tensor_tensor(part(row_E[:, 1, :], b), part(row_c[:, 1, :], b + 1), part(row_end[:, INNER, :], b + 1), ALU.add))
                dve.tensor_tensor(part(row_E[:, 0, :], f), part(row_E[:, 0, :], f), part(row_end[:, LAST, :], f - 1), ALU.max)
                link(dve.tensor_tensor(part(row_E[:, 1, :], b), part(row_E[:, 1, :], b), part(row_end[:, FIRST, :], b + 1), ALU.max))
                dve.tensor_tensor(part(row_c[:, 0, :], f), part(row_E[:, 0, :], f), part(row_end[:, LINK, :], f - 1), ALU.add)
                link(dve.tensor_tensor(part(row_c[:, 1, :], b), part(row_E[:, 1, :], b), part(row_end[:, LINK, :], b), ALU.add))
            dve.sem_inc(s_rowE, 1)
            dve.wait_ge(s_carT, 1)
            link(dve.tensor_copy(carry[:, :], bank[3][0:CHH, 0:2]))
            link(dve.tensor_tensor_scan(run, pen[:, 0:CE], run, carry[:, 0:1], ALU.add, ALU.max))
            link(dve.memset(pen[:, CE:CE + 1], 0.0))
            link(dve.tensor_tensor_scan(run[:, ::-1], pen[:, CE:0:-1], run[:, ::-1], carry[:, 1:2], ALU.add, ALU.max))
            dve.tensor_tensor(al, al, run, ALU.subtract).then_inc(s_sub, 1)
            for k in range(CG):
                dve.wait_ge(s_eT, k + 1)
                dve.tensor_copy(alpha_em[:, :].rearrange("p (c g j h) -> p g j c h", c=CH, h=H, j=G)[:, k],
                                bank[4 + k % 2][0:P, 0:G * CHH].rearrange("p (j c h) -> p j c h", j=G, c=CH)).then_inc(s_eTc, 1)
            dve.wait_ge(s_eTc, CG // 2 + CG)

            def prepare(i, u):
                st = 4 * i + u
                dve.wait_ge(s_product, st + 1)
                dve.tensor_tensor(oh[:, u, :, :], iota_row[0:P, :].unsqueeze(1).to_broadcast([P, G, P]),
                                  dstB[:, bass.ds(st, 1), :].rearrange("p o j -> p (o j)").unsqueeze(2).to_broadcast([P, G, P]),
                                  ALU.is_equal).then_inc(s_onehot, 1)

            def add(i, u, b):
                st = 4 * i + u
                dve.wait_ge(s_summed, st + 4)
                dve.wait_ge(s_product, st + 5)
                o = acc[:, bass.ds(b, 1), :]
                dve.tensor_tensor(o, bank[u][0:P, 0:W].unsqueeze(1), o, ALU.add).then_inc(s_summed, 1)

            def block_of(i, u):
                return dve.value_load(walkB[0:1, 1, bass.ds(4 * i + u, 1)], min_val=0, max_val=NB - 1)

            link(dve.memset(acc, 0.0))
            for u in range(2):
                prepare(0, u)
            with dve.Fori(0, SB // 4 - 1) as i:
                for u in range(4):
                    b = block_of(i, u)
                    prepare(i + (u + 2) // 4, (u + 2) % 4)
                    add(i, u, b)
            end = SB // 4 - 1
            for u in range(4):
                if u < 2:
                    prepare(end, u + 2)
                add(end, u, block_of(end, u))

            def blocks(a):
                return a.rearrange("p (b f) -> p b f", b=NB)

            def spread(a):
                return a.unsqueeze(2).to_broadcast([P, NB, D])

            def layernorm(n, y, o):
                sq = bufR[0:P, 2 * N:2 * N + NB * D]
                link(dve.reduce_sum(st25[:, 0, :], blocks(y), axis=AX_X))
                link(dve.tensor_scalar(st25[:, 0, :], st25[:, 0, :], -1.0 / D, None, ALU.mult))
                link(dve.tensor_tensor(blocks(y), blocks(y), spread(st25[:, 0, :]), ALU.add))
                link(dve.tensor_tensor(sq, y, y, ALU.mult))
                dve.reduce_sum(st25[:, 1, :], blocks(sq), axis=AX_X).then_inc(s_var, 1)
                dve.wait_ge(s_root, n)
                link(dve.reciprocal(st25[:, 3, :], st25[:, 2, :]))
                dve.tensor_tensor(o, blocks(y), spread(st25[:, 3, :]), ALU.mult).then_inc(s_ready, 1)

            dve.wait_ge(s_summed, SB + 4)
            heads = acc.rearrange("p b (h v) -> p b h v", h=H)
            link(dve.tensor_scalar(rden[:, :].rearrange("p (b h) -> p b h", b=NB), heads[:, :, :, D // H], 0.5, None, ALU.max))
            link(dve.reciprocal(rden[:, :], rden[:, :]))
            for b in range(NB):
                mul = dve.tensor_tensor(tmp[:, b * D:(b + 1) * D].rearrange("p (h v) -> p h v", h=H),
                                        heads[:, b, :, 0:D // H],
                                        rden[:, b * H:(b + 1) * H].unsqueeze(2).to_broadcast([P, H, D // H]), ALU.mult)
            mul.then_inc(s_divided, 1)
            for k, (g, m) in enumerate(NG):
                dve.wait_ge(s_qn, len(range(0, NB, 8)) + k + 1)
                dve.tensor_tensor(tmp2[:, g * D:(g + m) * D], bank[2 + k % 2][0:P, 0:m * D],
                                  x_nm[:, g:g + m, :].rearrange("p b f -> p (b f)"), ALU.add).then_inc(s_normed, 1)
            dve.wait_ge(s_normed, len(NG))
            layernorm(1, tmp2, x_nm[:, :, :])
            dve.wait_ge(s_ready, 1)

            def split(n0, of):
                for k in range(NGRP + 1):
                    if k < NGRP:
                        g, m = NG[k]
                        r = rest[:, (n0 + k) % 2, 0:m * D].rearrange("p (b f) -> p b f", b=m)
                        dve.wait_ge(s_high, n0 + k + 1)
                        if n0 + k >= 2:
                            dve.wait_ge(s_parts, n0 + k - 1)
                        dve.tensor_tensor(r, of(k, g, m), parts[:, g:g + m, 0, :], ALU.subtract).then_inc(s_rest, 1)
                    if k >= 1:
                        g, m = NG[k - 1]
                        r = rest[:, (n0 + k - 1) % 2, 0:m * D].rearrange("p (b f) -> p b f", b=m)
                        dve.wait_ge(s_mid, n0 + k)
                        dve.tensor_tensor(parts[:, g:g + m, 2, :], r, parts[:, g:g + m, 1, :], ALU.subtract).then_inc(s_parts, 1)

            split(0, lambda k, g, m: x_nm[:, g:g + m, :])
            for l in range(L):
                for k, (g, m) in enumerate(NG):
                    n = l * NGRP + k
                    dve.wait_ge(s_aggregated, n + 1)
                    if l == 0:
                        dve.wait_ge(s_nfc, NGRP + k + 1)
                    dve.tensor_tensor(fT[:, g * P:(g + m) * P], bank[n % 2][:, 0:m * P], fT[:, g * P:(g + m) * P], ALU.add).then_inc(s_h, 1)
                    if k >= 3:
                        dve.wait_ge(s_mlp2c, n - 2)
                        g3, m3 = NG[k - 3]
                        dve.bn_stats(bn6[:, k - 3, :], h2T[:, g3 * P:(g3 + m3) * P]).then_inc(s_stats, 1)
                for k in range(NGRP - 3, NGRP):
                    dve.wait_ge(s_mlp2c, l * NGRP + k + 1)
                    g3, m3 = NG[k]
                    dve.bn_stats(bn6[:, k, :], h2T[:, g3 * P:(g3 + m3) * P]).then_inc(s_stats, 1)
                dve.wait_ge(s_stats, (l + 1) * NGRP)
                dve.bn_aggr(bn2[:, :], bn6[:, :, :].rearrange("p k s -> p (k s)")).then_inc(s_var, 1)
                dve.wait_ge(s_root, l + 2)
                link(dve.reciprocal(st1[:, 4:5], st1[:, 3:4]))
                link(dve.tensor_tensor(st1[:, 5:6], st1[:, 4:5], Lvec[:, 2, l:l + 1], ALU.mult))
                dve.wait_ge(s_mlp1, (l + 1) * NGRP)
                link(dve.tensor_scalar(h2T, h2T, bn2[:, 0:1], None, ALU.subtract))
                for k, (g, m) in enumerate(NG):
                    e = slice(g * P, (g + m) * P)
                    dve.tensor_scalar(fT[:, e], h2T[:, e], st1[:, 5:6], Lvec[:, 3, l:l + 1], ALU.mult, ALU.add).then_inc(s_normed, 1)
                if l < L - 1:
                    split((l + 1) * NGRP, back_rows)
                    continue
                for k, (g, m) in enumerate(NG):
                    dve.wait_ge(s_backT, l * NGRP + k + 1)
                    dve.tensor_tensor(blocks(tmp2)[:, g:g + m, :], back_rows(k, g, m), x_nm[:, g:g + m, :], ALU.add).then_inc(s_back, 1)
                dve.wait_ge(s_back, NGRP)
            layernorm(L + 2, tmp2, blocks(tmp2))


_INS = ['x', 'src', 'dst', 'edge_attr_16', 'edge_attr_16_n2', 'L0_gnn_Wq', 'L0_gnn_Wang_k', 'L0_gnn_Wlin_k', 'L0_gnn_W1k',
        'L0_gnn_b1k', 'L0_gnn_W2k', 'L0_gnn_Wang_v', 'L0_gnn_Wlin_v', 'L0_gnn_W1v', 'L0_gnn_b1v', 'L0_gnn_W2v', 'L0_gnn_Wdot',
        'L0_gnn_Wout', 'L1_gnn_W1', 'L1_gnn_b1', 'L1_gnn_W2', 'L1_gnn_b2', 'L1_gnn_gamma', 'L1_gnn_beta']
_OUTS = [((3125, 128), 'float32')]


def kernel(**inputs):
    import numpy as _np
    import concourse.bacc as _bacc
    from concourse import mybir as _mybir
    from concourse.bass_utils import run_bass_kernel_spmd as _run

    nc = _bacc.Bacc("TRN2", target_bir_lowering=False, num_devices=1)
    arrays, args = {}, []
    for name in _INS:
        a = _np.ascontiguousarray(inputs[name])
        arrays[f"in_{name}_dram"] = a
        args.append(nc.dram_tensor(f"in_{name}_dram", a.shape, _mybir.dt.from_np(a.dtype), kind="ExternalInput").ap())
    for i, (shape, dtype) in enumerate(_OUTS):
        dt = _mybir.dt.from_np(_np.dtype(dtype))
        args.append(nc.dram_tensor(f"out_{i}_dram", shape, dt, kind="ExternalOutput").ap())
    gnn(nc, *args)
    r = _run(nc, [arrays], core_ids=[0])
    return r.results[0]["out_0_dram"]
```
